# Optimizing a Trainium2 kernel written in Bass

```python
import numpy as np
import jax
import jax.numpy as jnp

def _softmax(x, axis=-1):
    return jax.nn.softmax(x, axis=axis)

def _gelu(x):
    return jax.nn.gelu(x, approximate=True)

def _silu(x):
    return jax.nn.silu(x)

def _sigmoid(x):
    return jax.nn.sigmoid(x)

def _layernorm(x, axis=-1, eps=1e-05):
    m = jnp.mean(x, axis=axis, keepdims=True)
    v = jnp.var(x, axis=axis, keepdims=True)
    return (x - m) / jnp.sqrt(v + eps)

def _scatter_add(tgt, idx, src, axis=0):
    return tgt.at[idx].add(src)

def _segment_sum(src, seg, n):
    return jax.ops.segment_sum(src, seg, n)
kernel_name = 'mk_seq_postln_d2_jaxref_r8_6d39f1'

def setup_inputs(seed: int=0):
    np.random.seed(seed)
    _w = jnp.asarray

    def _L0_attn_setup():
        import jax, jax.numpy as jnp
        import numpy as np
        EPS = 1e-08
        C_RGLRU = 8.0

        def rmsnorm(x, w):
            rms = jnp.sqrt(jnp.mean(x * x, axis=-1, keepdims=True) + EPS)
            return w * (x / rms)

        def causal_depthwise_conv(x, conv_w, conv_b):
            K = conv_w.shape[0]
            S = x.shape[1]
            xp = jnp.pad(x, ((0, 0), (K - 1, 0), (0, 0)))
            y = sum((conv_w[k] * xp[:, k:k + S, :] for k in range(K)))
            return y + conv_b

        def rg_lru(x, ga_W, ga_b, gx_W, gx_b, a_param):
            r = jax.nn.sigmoid(x @ ga_W + ga_b)
            i = jax.nn.sigmoid(x @ gx_W + gx_b)
            log_a = -C_RGLRU * jax.nn.softplus(a_param) * r
            a = jnp.exp(log_a)
            mult = jnp.sqrt(-jnp.expm1(2.0 * log_a))
            b = mult * (i * x)

            def combine(c1, c2):
                a1, b1 = c1
                a2, b2 = c2
                return (a1 * a2, a2 * b1 + b2)
            _, h = jax.lax.associative_scan(combine, (a, b), axis=1)
            return h
        D, H, F, K, B, S = (256, 256, 768, 4, 2, 256)
        key = jax.random.key(seed)
        ks = jax.random.split(key, 16)

        def lin(k, fan_in, shape):
            return jax.random.normal(k, shape, jnp.float32) * fan_in ** (-0.5)
        return {'x': jax.random.normal(ks[0], (B, S, D), jnp.float32), 'norm1_w': jnp.ones((D,), jnp.float32), 'left_W': lin(ks[1], D, (D, H)), 'left_b': jnp.zeros((H,), jnp.float32), 'right_W': lin(ks[2], D, (D, H)), 'right_b': jnp.zeros((H,), jnp.float32), 'conv_w': lin(ks[3], K, (K, H)), 'conv_b': jnp.zeros((H,), jnp.float32), 'ga_W': lin(ks[4], H, (H, H)), 'ga_b': jnp.zeros((H,), jnp.float32), 'gx_W': lin(ks[5], H, (H, H)), 'gx_b': jnp.zeros((H,), jnp.float32), 'a_param': jax.random.uniform(ks[6], (H,), jnp.float32, 0.5, 3.0), 'out_W': lin(ks[7], H, (H, D)), 'out_b': jnp.zeros((D,), jnp.float32), 'norm2_w': jnp.ones((D,), jnp.float32), 'up1_W': lin(ks[8], D, (D, F)), 'up1_b': jnp.zeros((F,), jnp.float32), 'up2_W': lin(ks[9], D, (D, F)), 'up2_b': jnp.zeros((F,), jnp.float32), 'down_W': lin(ks[10], F, (F, D)), 'down_b': jnp.zeros((D,), jnp.float32)}
    _L0_attn_in = _L0_attn_setup()

    def _L0_ffn_setup():
        import jax, jax.numpy as jnp
        import numpy as np
        D_MODEL = 256
        D_EXPERT = 1024
        EPS = 1e-08

        def ternary_quant(w):
            scale = jnp.mean(jnp.abs(w)) + EPS
            q = jnp.clip(jnp.round(w / scale), -1.0, 1.0) * scale
            return w + jax.lax.stop_gradient(q - w)
        key = jax.random.key(seed)
        k_x, k_up, k_gate, k_down = jax.random.split(key, 4)
        std_in = 1.0 / np.sqrt(D_MODEL)
        std_exp = 1.0 / np.sqrt(D_EXPERT)
        return {'x': jax.random.normal(k_x, (4, 256, D_MODEL), dtype=jnp.float32), 'W_up': jax.random.normal(k_up, (D_EXPERT, D_MODEL), dtype=jnp.float32) * std_in, 'W_gate': jax.random.normal(k_gate, (D_EXPERT, D_MODEL), dtype=jnp.float32) * std_in, 'W_down': jax.random.normal(k_down, (D_MODEL, D_EXPERT), dtype=jnp.float32) * std_exp}
    _L0_ffn_in = _L0_ffn_setup()

    def _L1_attn_setup():
        import jax, jax.numpy as jnp
        import numpy as np
        SCALE_BASE = 64
        EPS = 1e-05

        def _xpos_terms(seq_len, d):
            half = d // 2
            xscale = (jnp.arange(0, d, 2, dtype=jnp.float32) + 0.4 * d) / (1.4 * d)
            pos = jnp.arange(seq_len, dtype=jnp.float32)
            scale = xscale[None, :] ** (pos[:, None] / SCALE_BASE)
            inv_freq = 1.0 / 10000.0 ** (jnp.arange(half, dtype=jnp.float32) / half)
            sinu = pos[:, None] * inv_freq[None, :]
            return (jnp.sin(sinu), jnp.cos(sinu), scale)

        def _dup(t):
            return jnp.repeat(t, 2, axis=-1)

        def _rot(x):
            x1 = x[..., ::2]
            x2 = x[..., 1::2]
            return jnp.stack((-x2, x1), axis=-1).reshape(x.shape)

        def _apply_xpos(x, sin, cos, scale):
            c = _dup(cos * scale)
            s = _dup(sin * scale)
            return x * c + _rot(x) * s
        key = jax.random.key(seed)
        ks = jax.random.split(key, 6)
        B, S, H, nheads = (2, 128, 256, 16)
        d = H // nheads
        X = jax.random.normal(ks[0], (B, S, H), dtype=jnp.float32)
        W_Q = jax.random.normal(ks[1], (nheads, H, d), dtype=jnp.float32) / H
        W_K = jax.random.normal(ks[2], (nheads, H, d), dtype=jnp.float32) / H
        W_V = jax.random.normal(ks[3], (nheads, H, d), dtype=jnp.float32) / H
        W_G = jax.random.normal(ks[4], (H, H), dtype=jnp.float32) / H
        W_O = jax.random.normal(ks[5], (H, H), dtype=jnp.float32) / H
        gn_weight = jnp.ones((H,), dtype=jnp.float32)
        gn_bias = jnp.zeros((H,), dtype=jnp.float32)
        return {'X': X, 'W_Q': W_Q, 'W_K': W_K, 'W_V': W_V, 'W_G': W_G, 'W_O': W_O, 'gn_weight': gn_weight, 'gn_bias': gn_bias}
    _L1_attn_in = _L1_attn_setup()

    def _L1_ffn_setup():
        import math
        import jax, jax.numpy as jnp
        import numpy as np
        DIM = 256
        RANK = 8
        B, T = (4, 512)

        def _orthogonal(key, n):
            a = jax.random.normal(key, (n, n), dtype=jnp.float32)
            q, r = jnp.linalg.qr(a)
            q = q * jnp.sign(jnp.diagonal(r))[None, :]
            return q
        key = jax.random.key(seed)
        kx, kf = jax.random.split(key)
        x = jax.random.normal(kx, (B, T, DIM), dtype=jnp.float32)
        fkeys = jax.random.split(kf, RANK)
        factors = jnp.stack([_orthogonal(fkeys[r], DIM) * (r + 1) ** (-0.5) for r in range(RANK)])
        bias = jnp.zeros((DIM,), dtype=jnp.float32)
        return {'x': x, 'factors': factors, 'bias': bias}
    _L1_ffn_in = _L1_ffn_setup()
    _d = {'L0_attn_x': _L0_attn_in['x'], 'L0_attn_norm1_w': _L0_attn_in['norm1_w'], 'L0_attn_left_W': _L0_attn_in['left_W'], 'L0_attn_left_b': _L0_attn_in['left_b'], 'L0_attn_right_W': _L0_attn_in['right_W'], 'L0_attn_right_b': _L0_attn_in['right_b'], 'L0_attn_conv_w': _L0_attn_in['conv_w'], 'L0_attn_conv_b': _L0_attn_in['conv_b'], 'L0_attn_ga_W': _L0_attn_in['ga_W'], 'L0_attn_ga_b': _L0_attn_in['ga_b'], 'L0_attn_gx_W': _L0_attn_in['gx_W'], 'L0_attn_gx_b': _L0_attn_in['gx_b'], 'L0_attn_a_param': _L0_attn_in['a_param'], 'L0_attn_out_W': _L0_attn_in['out_W'], 'L0_attn_out_b': _L0_attn_in['out_b'], 'L0_attn_norm2_w': _L0_attn_in['norm2_w'], 'L0_attn_up1_W': _L0_attn_in['up1_W'], 'L0_attn_up1_b': _L0_attn_in['up1_b'], 'L0_attn_up2_W': _L0_attn_in['up2_W'], 'L0_attn_up2_b': _L0_attn_in['up2_b'], 'L0_attn_down_W': _L0_attn_in['down_W'], 'L0_attn_down_b': _L0_attn_in['down_b'], 'L0_ffn_W_up': _L0_ffn_in['W_up'], 'L0_ffn_W_gate': _L0_ffn_in['W_gate'], 'L0_ffn_W_down': _L0_ffn_in['W_down'], 'L1_attn_W_Q': _L1_attn_in['W_Q'], 'L1_attn_W_K': _L1_attn_in['W_K'], 'L1_attn_W_V': _L1_attn_in['W_V'], 'L1_attn_W_G': _L1_attn_in['W_G'], 'L1_attn_W_O': _L1_attn_in['W_O'], 'L1_attn_gn_weight': _L1_attn_in['gn_weight'], 'L1_attn_gn_bias': _L1_attn_in['gn_bias'], 'L1_ffn_factors': _L1_ffn_in['factors'], 'L1_ffn_bias': _L1_ffn_in['bias']}
    _x0 = _d['L0_attn_x']
    _d['L0_attn_x'] = jax.random.normal(jax.random.fold_in(jax.random.key(seed), 1), (4, 256, 256), dtype=_x0.dtype)
    del _x0
    return _d

def reference(L0_attn_x, L0_attn_norm1_w, L0_attn_left_W, L0_attn_left_b, L0_attn_right_W, L0_attn_right_b, L0_attn_conv_w, L0_attn_conv_b, L0_attn_ga_W, L0_attn_ga_b, L0_attn_gx_W, L0_attn_gx_b, L0_attn_a_param, L0_attn_out_W, L0_attn_out_b, L0_attn_norm2_w, L0_attn_up1_W, L0_attn_up1_b, L0_attn_up2_W, L0_attn_up2_b, L0_attn_down_W, L0_attn_down_b, L0_ffn_W_up, L0_ffn_W_gate, L0_ffn_W_down, L1_attn_W_Q, L1_attn_W_K, L1_attn_W_V, L1_attn_W_G, L1_attn_W_O, L1_attn_gn_weight, L1_attn_gn_bias, L1_ffn_factors, L1_ffn_bias):

    def _L0_attn_ref(x, norm1_w, left_W, left_b, right_W, right_b, conv_w, conv_b, ga_W, ga_b, gx_W, gx_b, a_param, out_W, out_b, norm2_w, up1_W, up1_b, up2_W, up2_b, down_W, down_b):
        import jax, jax.numpy as jnp
        import numpy as np
        EPS = 1e-08
        C_RGLRU = 8.0

        def rmsnorm(x, w):
            rms = jnp.sqrt(jnp.mean(x * x, axis=-1, keepdims=True) + EPS)
            return w * (x / rms)

        def causal_depthwise_conv(x, conv_w, conv_b):
            K = conv_w.shape[0]
            S = x.shape[1]
            xp = jnp.pad(x, ((0, 0), (K - 1, 0), (0, 0)))
            y = sum((conv_w[k] * xp[:, k:k + S, :] for k in range(K)))
            return y + conv_b

        def rg_lru(x, ga_W, ga_b, gx_W, gx_b, a_param):
            r = jax.nn.sigmoid(x @ ga_W + ga_b)
            i = jax.nn.sigmoid(x @ gx_W + gx_b)
            log_a = -C_RGLRU * jax.nn.softplus(a_param) * r
            a = jnp.exp(log_a)
            mult = jnp.sqrt(-jnp.expm1(2.0 * log_a))
            b = mult * (i * x)

            def combine(c1, c2):
                a1, b1 = c1
                a2, b2 = c2
                return (a1 * a2, a2 * b1 + b2)
            _, h = jax.lax.associative_scan(combine, (a, b), axis=1)
            return h
        gelu = lambda t: jax.nn.gelu(t, approximate=False)
        xn = rmsnorm(x, norm1_w)
        left = gelu(xn @ left_W + left_b)
        right = rg_lru(causal_depthwise_conv(xn @ right_W + right_b, conv_w, conv_b), ga_W, ga_b, gx_W, gx_b, a_param)
        x1 = left * right @ out_W + out_b + x
        x1n = rmsnorm(x1, norm2_w)
        mlp = gelu(x1n @ up1_W + up1_b) * (x1n @ up2_W + up2_b) @ down_W + down_b
        return mlp + x1

    def _L0_ffn_ref(x, W_up, W_gate, W_down):
        import jax, jax.numpy as jnp
        import numpy as np
        D_MODEL = 256
        D_EXPERT = 1024
        EPS = 1e-08

        def ternary_quant(w):
            scale = jnp.mean(jnp.abs(w)) + EPS
            q = jnp.clip(jnp.round(w / scale), -1.0, 1.0) * scale
            return w + jax.lax.stop_gradient(q - w)
        wu = ternary_quant(W_up)
        wg = ternary_quant(W_gate)
        wd = ternary_quant(W_down)
        up = jnp.einsum('bsd,ed->bse', x, wu)
        gate = jnp.einsum('bsd,ed->bse', x, wg)
        hidden = jax.nn.silu(up) * gate
        return jnp.einsum('bse,de->bsd', hidden, wd)

    def _L1_attn_ref(X, W_Q, W_K, W_V, W_G, W_O, gn_weight, gn_bias):
        import jax, jax.numpy as jnp
        import numpy as np
        SCALE_BASE = 64
        EPS = 1e-05

        def _xpos_terms(seq_len, d):
            half = d // 2
            xscale = (jnp.arange(0, d, 2, dtype=jnp.float32) + 0.4 * d) / (1.4 * d)
            pos = jnp.arange(seq_len, dtype=jnp.float32)
            scale = xscale[None, :] ** (pos[:, None] / SCALE_BASE)
            inv_freq = 1.0 / 10000.0 ** (jnp.arange(half, dtype=jnp.float32) / half)
            sinu = pos[:, None] * inv_freq[None, :]
            return (jnp.sin(sinu), jnp.cos(sinu), scale)

        def _dup(t):
            return jnp.repeat(t, 2, axis=-1)

        def _rot(x):
            x1 = x[..., ::2]
            x2 = x[..., 1::2]
            return jnp.stack((-x2, x1), axis=-1).reshape(x.shape)

        def _apply_xpos(x, sin, cos, scale):
            c = _dup(cos * scale)
            s = _dup(sin * scale)
            return x * c + _rot(x) * s
        B, S, H = X.shape
        nheads, _, d = W_Q.shape
        gammas = 1.0 - jnp.exp(jnp.linspace(np.log(1.0 / 32), np.log(1.0 / 64), nheads)).astype(jnp.float32)
        sin, cos, scale = _xpos_terms(S, d)
        Q = jnp.einsum('bsh,nhd->bnsd', X, W_Q)
        K = jnp.einsum('bsh,nhd->bnsd', X, W_K)
        V = jnp.einsum('bsh,nhd->bnsd', X, W_V)
        Q = _apply_xpos(Q, sin, cos, scale)
        K = _apply_xpos(K, sin, cos, 1.0 / scale)
        n = jnp.arange(S)[:, None]
        m = jnp.arange(S)[None, :]
        D = jnp.where(n >= m, gammas[:, None, None] ** (n - m).astype(jnp.float32), 0.0)
        ret = jnp.einsum('bnsd,bntd->bnst', Q, K) * D[None]
        Y = jnp.einsum('bnst,bntv->bnsv', ret, V)
        Y = jnp.transpose(Y, (0, 2, 1, 3)).reshape(B, S, nheads * d)
        Yg = Y.reshape(B, S, nheads, d)
        mu = Yg.mean(-1, keepdims=True)
        var = Yg.var(-1, keepdims=True)
        Yn = ((Yg - mu) / jnp.sqrt(var + EPS)).reshape(B, S, nheads * d)
        Yn = Yn * gn_weight + gn_bias
        G = X @ W_G
        gate = G * jax.nn.sigmoid(G)
        return gate * Yn @ W_O

    def _L1_ffn_ref(x, factors, bias):
        import math
        import jax, jax.numpy as jnp
        import numpy as np
        DIM = 256
        RANK = 8
        B, T = (4, 512)

        def _orthogonal(key, n):
            a = jax.random.normal(key, (n, n), dtype=jnp.float32)
            q, r = jnp.linalg.qr(a)
            q = q * jnp.sign(jnp.diagonal(r))[None, :]
            return q
        rank = factors.shape[0]
        mixed = jnp.einsum('btd,rde->bte', x, factors)
        mixed = mixed / math.sqrt(rank) + bias
        return mixed
    x = L0_attn_x
    x = _layernorm(x + _L0_attn_ref(x, L0_attn_norm1_w, L0_attn_left_W, L0_attn_left_b, L0_attn_right_W, L0_attn_right_b, L0_attn_conv_w, L0_attn_conv_b, L0_attn_ga_W, L0_attn_ga_b, L0_attn_gx_W, L0_attn_gx_b, L0_attn_a_param, L0_attn_out_W, L0_attn_out_b, L0_attn_norm2_w, L0_attn_up1_W, L0_attn_up1_b, L0_attn_up2_W, L0_attn_up2_b, L0_attn_down_W, L0_attn_down_b), axis=-1)
    x = _layernorm(x + _L0_ffn_ref(x, L0_ffn_W_up, L0_ffn_W_gate, L0_ffn_W_down), axis=-1)
    x = _layernorm(x + _L1_attn_ref(x, L1_attn_W_Q, L1_attn_W_K, L1_attn_W_V, L1_attn_W_G, L1_attn_W_O, L1_attn_gn_weight, L1_attn_gn_bias), axis=-1)
    x = _layernorm(x + _L1_ffn_ref(x, L1_ffn_factors, L1_ffn_bias), axis=-1)
    return x

_drawn_inputs = setup_inputs


def setup_inputs(seed=0):
    import zlib

    import numpy as np

    out = dict(_drawn_inputs(seed))
    spreads = {'L0_attn_norm1_w': (1.0, 0.2),
     'L0_attn_left_b': (0.0, 0.328),
     'L0_attn_right_b': (0.0, 0.279),
     'L0_attn_conv_b': (0.0, 0.296),
     'L0_attn_ga_b': (0.0, 0.8),
     'L0_attn_gx_b': (0.0, 0.8),
     'L0_attn_out_b': (0.0, 0.1),
     'L0_attn_norm2_w': (1.0, 0.2),
     'L0_attn_up1_b': (0.0, 0.1),
     'L0_attn_up2_b': (0.0, 0.1),
     'L0_attn_down_b': (0.0, 0.1),
     'L1_attn_gn_weight': (1.0, 0.6),
     'L1_attn_gn_bias': (0.0, 0.8),
     'L1_ffn_bias': (0.0, 0.1)}
    factors = {'L0_attn_ga_W': 3.632,
     'L0_attn_a_param': 7.569,
     'L1_attn_W_Q': 8.0,
     'L1_attn_W_K': 8.0,
     'L1_attn_W_V': 8.0,
     'L1_attn_W_G': 8.0,
     'L1_attn_W_O': 8.0}
    for name, (base, spread) in spreads.items():
        noise = np.random.default_rng([zlib.crc32(name.encode()), seed]).standard_normal(out[name].shape)
        drawn = base * np.exp(spread * noise) if base else spread * noise
        out[name] = jnp.asarray(drawn.astype(out[name].dtype))
    for name, factor in factors.items():
        out[name] = (out[name] * factor).astype(out[name].dtype)
    return out
```

```python
import numpy as np
import concourse.bass as bass
from concourse import mybir
from contextlib import ExitStack

B, S, D = 4, 256, 256
P = 128
NT, NC = S // P, D // P
F, E = 768, 1024
H, DH = 16, 16
SLOT = 32
QUADS = H // 4
RANK = 8
BANKS = 8
EPS_RMS, EPS_Q, EPS_LN = 1e-8, 1e-8, 1e-5
C_RGLRU = 8.0

VECTORS, _at = {}, 0
for _name, _n in (("norm1_w", 2), ("left_b", 2), ("right_b", 2), ("conv_w", 8), ("conv_b", 2),
                  ("ga_b", 2), ("gx_b", 2), ("a_param", 2), ("norm2_w", 2), ("up1_b", 6),
                  ("up2_b", 6), ("gn_w", 2), ("gn_b", 2)):
    VECTORS[_name] = _at
    _at += _n
N_VECTORS = _at

LOADS, _at = [], 0
for _name, _n in (("rg", 4 * 512), ("out_down", 512 + 6 * 256), ("up_k0", 2 * F), ("up_k1", 2 * F),
                  ("ffn_up", 2 * E), ("ffn_gate", 2 * E), ("ffn_down", 2 * E),
                  ("qkvg", 4 * 512), ("factors0", 2048), ("factors1", 2048), ("o", 512)):
    LOADS.append((_name, _at, _n))
    _at += _n
N_WEIGHTS = _at
LOAD = {name: n for n, (name, _, _) in enumerate(LOADS)}

STAGES = [
    ("final", 44), ("f", 43), ("x4_T", 42), ("norm_x4", 41), ("o", 40), ("yn_T", 39), ("yn", 38),
    ("y_T", 37), ("scores", 36), ("qz", 35), ("qk_T", 35), ("qkv", 34),
    ("x3_T", 32), ("norm_x3", 31), ("ffn_down", 30), ("ffn", 29),
    ("x2_T", 27), ("norm_x2", 26), ("down", 25), ("mlp", 24),
    ("x1_T", 22), ("norm_x1", 21), ("out", 20), ("lr_split", 19), ("scan", 18), ("decay", 14), ("gates", 10),
    ("conv", 8), ("left_right", 6), ("xn_T", 2), ("norm_x0", 1), ("square_x0", 0),
]
STAGES += [("prep_up", 12), ("prep_down", 12), ("quant", 15), ("ternary", 16), ("prep_qkvg", 26),
           ("prep_f", 28), ("prep_o", 30)]
COUNT = {"prep_up": 2, "prep_down": 1, "quant": 3, "ternary": 3, "prep_qkvg": 1, "prep_f": 2, "prep_o": 1}
STEPS = max(s for _, s in STAGES) + B


def walk(work):
    for step in range(STEPS):
        for stage, start in STAGES:
            if stage in work and 0 <= step - start < COUNT.get(stage, B):
                yield work[stage], step - start


GROUPS = {
    "xn_T": [("xn_T",)], "left_right": [("left",), ("right",)], "gates": [("ga",), ("gx",)],
    "out": [("out",)], "x1_T": [("x1_T",)],
    "mlp": [(k, j) for j in range(F // 256) for k in ("up1", "up2")],
    "down": [("down",)], "x2_T": [("x2_T",)],
    "ffn": [(k, j) for j in range(E // 256) for k in ("fup", "fgate")],
    "ffn_down": [("ffn_down",)], "x3_T": [("x3_T",)],
    "qkv": [("qk", 0), ("qk", 1), ("v",), ("gate",)],
    "qk_T": [("qk_T", 0), ("qk_T", 1), ("kv",)],
    "scores": [(k, t, *q) for t in range(NT) for k, q in
               [("sc", (q,)) for q in range(QUADS)] + [("y", ())]],
    "y_T": [("y_T", 0), ("y_T", 1)], "yn_T": [("yn_T",)], "o": [("o",)], "x4_T": [("x4_T",)],
    "f": [("f",)], "quant": [("absum",)],
}


def number_groups():
    order = []
    for (stage, b) in walk({s: s for s in GROUPS}):
        order += [(key[0], b, *key[1:]) for key in GROUPS[stage]]
    return {key: n for n, key in enumerate(order)}


def build(nc, x_dram, vec_dram, row_dram, early_dram, table_dram, w_dram, out_dram):
    fp32, fp32r = mybir.dt.float32, mybir.dt.float32r
    ALU, ACT, AX = mybir.AluOpType, mybir.ActivationFunctionType, mybir.AxisListType
    number = number_groups()

    ctx = ExitStack()
    with ctx:
        def sb(name, shape, dt=fp32, scope=None):
            return (scope or ctx).enter_context(nc.sbuf_tensor(name, shape, dt))

        def sem(name):
            return ctx.enter_context(nc.semaphore(name))

        x0 = sb("x0", [P, B, NT, D])
        x0o = sb("x0o", [P, B, NT, D])
        x1 = sb("x1", [P, B, NT, D])
        xh = sb("xh", [P, B, NC, S], fp32r)
        xl = sb("xl", [P, B, NC, S], fp32r)
        staging = [sb(f"staging{i}", [P, 2048]) for i in range(2)]
        q_up = sb("q_up", [P, NC, E], fp32r)
        q_gate = sb("q_gate", [P, NC, E], fp32r)
        q_down = sb("q_down", [P, E // P, D], fp32r)
        rope = sb("rope", [P, 2, NT, 2 * D])
        early = sb("consts", [P, 2 * P])
        ident, ones = early[:, 0:P], early[:, P:2 * P]
        masks = sb("masks", [P, P + 256 + 8])
        causal, own_head, head_rows = masks[:, 0:P], masks[:, P:P + 256], masks[:, P + 256:P + 264]
        rows = sb("row_vectors", [P, 3, D])
        vec = sb("vec", [P, N_VECTORS])
        stats = sb("stats", [P, B, NT, 6])
        mv = sb("mv", [P, B, NT, 2])
        ssq = sb("ssq", [P, B, NT])
        rs = sb("rs", [P, B, NT])
        rse = sb("rse", [P, B, NT])
        neg_half = sb("neg_half", [P, H])
        sp = sb("sp", [P, 9, 2])
        decay_c = sb("decay_c", [P, 2, 2])
        absums = sb("absums", [P, 12])
        qs = sb("qs", [P, 3])
        qt = sb("qt", [P, 2, 3])
        qc = sb("qc", [P, 2])
        vmean = sb("vmean", [P, NC, H])
        ysum = sb("ysum", [P, B, NT, H])
        yrs = sb("yrs", [P, B, NT, H])
        square_out = sb("square_out", [P, 2, 256], mybir.dt.bfloat16)
        abs_out = sb("abs_out", [P, 512], mybir.dt.bfloat16)
        yse = sb("yse", [P, 2, H])

        with ExitStack() as r1:
            w_ups = [sb(f"w_ups_{k}", [P, NC, 2 * F], fp32r, r1) for k in ("hi", "lo")]
            w_dn = [sb(f"w_down_{k}", [P, F // P, D], fp32r, r1) for k in ("hi", "lo")]
        r1 = ctx.enter_context(ExitStack())
        qz = [sb(f"qz{i}", [P, H, P], fp32, r1) for i in range(2)]
        vpad = sb("vpad", [P, 2, NT, H * SLOT], fp32, r1)
        probs = sb("probs", [P, 4, 4 * P], fp32, r1)
        state = sb("state", [P, 2, NC, 8 * SLOT], fp32, r1)

        with ExitStack() as r2:
            left = sb("left", [P, B, NC, S], fp32, r2)
            r_gate = sb("r_gate", [P, B, NC, S], fp32, r2)
            i_gate = sb("i_gate", [P, B, NC, S], fp32, r2)
            decay = sb("decay", [P, B, NC, S], fp32, r2)
            right = sb("right", [P, 2, NC, S + 3], fp32, r2)
            conv = sb("conv", [P, 2, NC, S], fp32, r2)
            squared = sb("squared", [P, NC, S], fp32, r2)
            ch = sb("ch", [P, 2, NC, S], fp32r, r2)
            cl = sb("cl", [P, 2, NC, S], fp32r, r2)
        with ExitStack() as r2:
            act = sb("act", [P, 3, 2, S], fp32, r2)
            hid = sb("hid", [P, 2, 2, S], fp32, r2)
            hh = sb("hh", [P, 2, E // P, S], fp32r, r2)
            hl = sb("hl", [P, 2, E // P, S], fp32r, r2)
            fsum = sb("fsum", [P, NC * D], fp32, r2)
        r2 = ctx.enter_context(ExitStack())
        qk = sb("qk", [P, 4, 2 * D], fp32, r2)
        qk_sin = sb("qk_sin", [P, 2, 2 * D], fp32, r2)
        qkT = sb("qkT", [P, 4, 4, P], fp32, r2)
        ys = sb("ys", [P, 2, 4, P], fp32, r2)
        ysq = sb("ysq", [P, 2, D], fp32, r2)
        yn = sb("yn", [P, 4, D], fp32, r2)
        gate = sb("gate", [P, B, NC, S], fp32, r2)
        y3 = sb("y3", [P, 2, NC, S], fp32, r2)
        y3h = sb("y3h", [P, 2, NC, S], fp32r, r2)
        y3l = sb("y3l", [P, 2, NC, S], fp32r, r2)
        sb("pad", [P, 12], fp32, r2)

        with ExitStack() as r3:
            w_rg = [sb(f"w_rg_{k}", [P, 4, NC, D], fp32r, r3) for k in ("hi", "lo")]
            w_out = [sb(f"w_out_{k}", [P, NC, D], fp32r, r3) for k in ("hi", "lo")]
        r3 = ctx.enter_context(ExitStack())
        w_qkvg = [sb(f"w_qkvg_{k}", [P, NC, 4 * D], fp32r, r3) for k in ("hi", "lo")]
        w_o = [sb(f"w_o_{k}", [P, NC, D], fp32r, r3) for k in ("hi", "lo")]
        w_f = [sb(f"w_f_{k}", [P, NC, D], fp32r, r3) for k in ("hi", "lo")]

        banks = [ctx.enter_context(nc.psum_tensor(f"bank{i}", [P, 512], fp32)) for i in range(BANKS)]

        x_loaded = [sem(f"x_loaded{b}") for b in range(B)]
        vec_loaded, rows_loaded = sem("vec_loaded"), sem("rows_loaded")
        early_loaded, tables_loaded, masks_loaded = sem("early_loaded"), sem("tables_loaded"), sem("masks_loaded")
        raw_loaded = [sem(f"raw_loaded{i}") for i in range(2)]
        filled = sem("filled")
        drained = [sem(f"drained{k}") for k in range(BANKS)]
        half_ready = sem("half_ready")
        pads_ready = sem("pads_ready")
        squares_ready = sem("squares_ready")
        var_ready, rs_ready = sem("var_ready"), sem("rs_ready")
        act_chain = sem("act_chain")
        for_names = ("stats_ready", "quant_step", "vmean_ready", "centred", "softplus_step", "rse_ready",
                     "yse_ready", "pool_hi", "fsum_step")
        (stats_ready, quant_step, vmean_ready, centred, softplus_step, rse_ready, yse_ready, pool_hi,
         fsum_step) = (sem(x) for x in for_names)
        normed = sem("normed")
        hi_ready = sem("hi_ready")
        w_hi, w_lo = sem("w_hi"), sem("w_lo")
        w_hi_p, w_ready_p = sem("w_hi_p"), sem("w_ready_p")
        softplus_a, softplus_d = sem("softplus_a"), sem("softplus_d")
        absums_ready = sem("absums_ready")
        scales_ready, above_ready, ternary_ready = sem("scales_ready"), sem("above_ready"), sem("ternary_ready")
        xo_ready, xs_part, xs_ready, x4b_ready = sem("xo_ready"), sem("xs_part"), sem("xs_ready"), sem("x4b_ready")
        conv_step, conv_ready, conv_hi, conv_lo = sem("conv_step"), sem("conv_ready"), sem("conv_hi"), sem("conv_lo")
        gated_x, decay_ready, tanh_ready, a2_ready, mult2_ready = (
            sem("gated_x"), sem("decay_ready"), sem("tanh_ready"), sem("a2_ready"), sem("mult2_ready"))
        mult_ready, scan_step, lr_ready, lr_hi, lr_lo = (
            sem("mult_ready"), sem("scan_step"), sem("lr_ready"), sem("lr_hi"), sem("lr_lo"))
        hid_hi, hid_lo = sem("hid_hi"), sem("hid_lo")
        cos_done, sin_done, qk_ready = sem("cos_done"), sem("sin_done"), sem("qk_ready")
        vzero, qz_ready, probs_ready = sem("vzero"), sem("qz_ready"), sem("probs_ready")
        ysq_ready, ysum_ready, yrs_ready, yn_ready = sem("ysq_ready"), sem("ysum_ready"), sem("yrs_ready"), sem("yn_ready")
        y3_ready, y3_gated, y3_hi, y3_lo = sem("y3_ready"), sem("y3_gated"), sem("y3_hi"), sem("y3_lo")
        out_ready = sem("out_ready")
        out_stored = [sem(f"out_stored{b}") for b in range(B)]

        def bank(*key):
            return banks[number[key] % BANKS]

        def wait_filled(eng, *key):
            eng.wait_ge(filled, number[key] + 1)

        def wait_drained(eng, *key):
            eng.wait_ge(drained[number[key] % BANKS], number[key] // BANKS + 1)

        def drains(instruction, *key):
            instruction.then_inc(drained[number[key] % BANKS], 1)

        def v(name, c=0, n=1):
            return vec[:, VECTORS[name] + c:VECTORS[name] + c + n]

        def raw_wait(eng, name):
            n = LOAD[name]
            eng.wait_ge(raw_loaded[n % 2], 16 * (n // 2 + 1))
            return staging[n % 2]

        hi_count = {}
        for stage, b in walk({s: s for s in ("xn_T", "x1_T", "x2_T", "x3_T", "x4_T")}):
            hi_count[stage, b] = len(hi_count) + 1
        def hidden_key(n):
            return ("up2", n // 3, n % 3) if n < 3 * B else ("fgate", (n - 3 * B) // 4, (n - 3 * B) % 4)

        rs_count = {}
        for stage, b in walk({s: s for s in ("square_x0", "out", "down", "ffn_down", "o", "f")}):
            rs_count[stage, b] = len(rs_count) + 1
        ln_count = {}
        for stage, b in walk({s: s for s in ("down", "ffn_down", "o", "f")}):
            ln_count[stage, b] = len(ln_count) + 1
        normed_count = {}
        for stage, b in walk({s: s for s in ("norm_x0", "norm_x1", "norm_x2", "norm_x3", "norm_x4")}):
            normed_count[stage, b] = len(normed_count) + 1

        block = ctx.enter_context(nc.Block())

        @block.sync
        def _(sp_eng):
            e = sp_eng
            last_use = [(w_lo, 4), (w_ready_p, 1), (w_lo, 6), (w_lo, 7), (ternary_ready, 1), (ternary_ready, 2),
                        (ternary_ready, 3), (w_ready_p, 2), (fsum_step, 4)]
            e.dma_start(early[:, :], early_dram).then_inc(early_loaded, 16)
            e.dma_start(vec[:, :], vec_dram).then_inc(vec_loaded, 16)
            for b in range(B):
                e.dma_start(x0[:, b], x_dram[:, b]).then_inc(x_loaded[b], 16)
                if b == 0:
                    for n in range(2):
                        _, at, cols = LOADS[n]
                        e.dma_start(staging[n][:, 0:cols], w_dram[:, at:at + cols]).then_inc(raw_loaded[n], 16)
            e.dma_start(rows[:, :, :], row_dram).then_inc(rows_loaded, 16)
            for n in range(2, len(LOADS)):
                _, at, cols = LOADS[n]
                e.wait_ge(*last_use[n - 2])
                e.dma_start(staging[n % 2][:, 0:cols], w_dram[:, at:at + cols]).then_inc(raw_loaded[n % 2], 16)
                if n == 4:
                    e.dma_start(rope[:, :, :, :], table_dram[:, 0:4 * 2 * D]).then_inc(tables_loaded, 16)
                    e.dma_start(masks[:, :], table_dram[:, 4 * 2 * D:]).then_inc(masks_loaded, 16)
            for b in range(B):
                e.wait_ge(out_ready, b + 1)
                e.dma_start(out_dram[:, b], x0o[:, b]).then_inc(out_stored[b], 16)
            for b in range(B):
                e.wait_ge(out_stored[b], 16)

        @block.tensor
        def _(pe):
            def open_bank(*key):
                n = number[key]
                if n >= BANKS:
                    pe.wait_ge(drained[n % BANKS], n // BANKS)
                return banks[n % BANKS]

            def split_product(out, stationary, moving, first=True):
                terms = []
                for (sh, sl), (mh, ml) in zip(stationary, moving):
                    if sl is not None:
                        terms.append((sl, mh))
                    if ml is not None:
                        terms.append((sh, ml))
                terms += [(sh, mh) for (sh, _), (mh, _) in zip(stationary, moving)]
                for n, (a, m) in enumerate(terms):
                    last = nc.tensor.matmul(out, a, m, start=(first and n == 0), stop=(n == len(terms) - 1),
                                            skip_group_check=True)
                return last

            def fm_product(key, weights, k_chunks, acts, m_at=0):
                out = open_bank(*key)
                for m in range(2):
                    last = split_product(
                        out[:, m * S:(m + 1) * S],
                        [weights(k, m_at + m) for k in range(k_chunks)],
                        [acts(k) for k in range(k_chunks)], first=(m == 0))
                last.then_inc(filled, 1)

            def tm_product(key, acts, k_chunks, weights):
                out = open_bank(*key)
                for t in range(NT):
                    last = split_product(
                        out[:, t * D:(t + 1) * D],
                        [tuple(None if a is None else a[:, t * P:(t + 1) * P] for a in acts(k))
                         for k in range(k_chunks)],
                        [weights(k) for k in range(k_chunks)], first=(t == 0))
                last.then_inc(filled, 1)

            def x_acts(b):
                return lambda k: (xh[:, b, k, :], xl[:, b, k, :])

            def turn(stage, source):
                def work(b):
                    pe.wait_ge(normed, normed_count[source[0], b])
                    out = open_bank(stage, b)
                    for c in range(NC):
                        for t in range(NT):
                            last = nc.tensor.transpose(out[:, c * S + t * P:c * S + (t + 1) * P],
                                                       source[1][:, b, t, c * P:(c + 1) * P], ident)
                    last.then_inc(filled, 1)
                return work

            def left_right(b):
                wait_drained(pe, "xn_T", b)
                for j, name in enumerate(("left", "right")):
                    if b == 0:
                        pe.wait_ge(w_lo, j + 1)
                    fm_product((name, b), lambda k, m: tuple(w[:, j, k, m * P:(m + 1) * P] for w in w_rg), NC, x_acts(b))

            def quant(n):
                pe.wait_ge(absums_ready, 4 * (n + 1))
                nc.tensor.matmul(open_bank("absum", n)[:, 0:4], ones, absums[:, 4 * n:4 * n + 4],
                                 start=True, stop=True).then_inc(filled, 1)

            def gates(b):
                pe.wait_ge(conv_lo, b + 1)
                for j, name in enumerate(("ga", "gx")):
                    if b == 0:
                        pe.wait_ge(w_lo, j + 3)
                    fm_product((name, b), lambda k, m: tuple(w[:, 2 + j, k, m * P:(m + 1) * P] for w in w_rg), NC,
                               lambda k: (ch[:, b % 2, k, :], cl[:, b % 2, k, :]))

            def out(b):
                pe.wait_ge(lr_lo, b + 1)
                if b == 0:
                    pe.wait_ge(w_lo, 5)
                tm_product(("out", b), lambda k: (ch[:, b % 2, k, :], cl[:, b % 2, k, :]), NC,
                           lambda k: tuple(w[:, k, :] for w in w_out))

            def mlp(b):
                wait_drained(pe, "x1_T", b)
                if b == 0:
                    pe.wait_ge(w_lo, 7)
                for j in range(F // 256):
                    for n, name in enumerate(("up1", "up2")):
                        fm_product((name, b, j), lambda k, m: tuple(w[:, k, n * F + m * P:n * F + (m + 1) * P] for w in w_ups),
                                   NC, x_acts(b), m_at=2 * j)

            def down(b):
                if b == 0:
                    pe.wait_ge(w_ready_p, 1)
                pe.wait_ge(hid_lo, 3 * (b + 1))
                tm_product(("down", b), lambda k: (hh[:, b % 2, k, :], hl[:, b % 2, k, :]), F // P,
                           lambda k: tuple(w[:, k, :] for w in w_dn))

            def ffn(b):
                wait_drained(pe, "x2_T", b)
                if b == 0:
                    pe.wait_ge(ternary_ready, 2)
                for j in range(E // 256):
                    for name, w in (("fup", q_up), ("fgate", q_gate)):
                        fm_product((name, b, j), lambda k, m: (w[:, k, m * P:(m + 1) * P], None), NC, x_acts(b), m_at=2 * j)

            def ffn_down(b):
                if b == 0:
                    pe.wait_ge(ternary_ready, 3)
                pe.wait_ge(hid_lo, 3 * B + 4 * (b + 1))
                tm_product(("ffn_down", b), lambda k: (hh[:, b % 2, k, :], hl[:, b % 2, k, :]), E // P,
                           lambda k: (q_down[:, k, :], None))

            def qkv(b):
                wait_drained(pe, "x3_T", b)
                if b == 0:
                    pe.wait_ge(w_ready_p, 3)
                def tile(k, t):
                    return xh[:, b, k, t * P:(t + 1) * P], xl[:, b, k, t * P:(t + 1) * P]
                for t in range(NT):
                    dst = open_bank("qk", b, t)
                    split_product(dst[:, :], [tile(k, t) for k in range(NC)],
                                  [tuple(w[:, k, 0:2 * D] for w in w_qkvg) for k in range(NC)]).then_inc(filled, 1)
                tm_product(("v", b), x_acts(b), NC, lambda k: tuple(w[:, k, 2 * D:3 * D] for w in w_qkvg))
                fm_product(("gate", b), lambda k, m: tuple(w[:, k, 3 * D + m * P:3 * D + (m + 1) * P] for w in w_qkvg),
                           NC, x_acts(b))

            def qk_T(b):
                for t in range(NT):
                    i = NT * b + t
                    pe.wait_ge(qk_ready, i + 1)
                    dst = open_bank("qk_T", b, t)
                    for c in range(4):
                        last = nc.tensor.transpose(dst[:, c * P:(c + 1) * P], qk[:, i % 4, c * P:(c + 1) * P], ident)
                    last.then_inc(filled, 1)
                wait_drained(pe, "v", b)
                dst = open_bank("kv", b)
                for c in range(NC):
                    last = nc.tensor.matmul(dst[:, c * 256:(c + 1) * 256], qk[:, (NT * b) % 4, D + c * P:D + (c + 1) * P],
                                            vpad[:, b % 2, 0, c * 256:(c + 1) * 256], start=(c == 0), stop=True,
                                            skip_group_check=True)
                last.then_inc(filled, 1)

            def scores(b):
                for t in range(NT):
                    i = NT * b + t
                    pe.wait_ge(qz_ready, i + 1)
                    for q in range(QUADS):
                        dst = open_bank("sc", b, t, q)
                        nc.tensor.matmul(dst[:, :], qkT[:, i % 4, 2 + q // 2, :], qz[i % 2][:, 4 * q:4 * q + 4, :],
                                         start=True, stop=True).then_inc(filled, 1)
                    dst = open_bank("y", b, t)
                    if t > 0:
                        wait_drained(pe, "kv", b)
                        for q in range(QUADS):
                            nc.tensor.matmul(dst[:, q * P:(q + 1) * P], state[:, b % 2, q // 2, (q % 2) * P:(q % 2 + 1) * P],
                                             qkT[:, i % 4, q // 2, :], start=(q == 0), stop=False, skip_group_check=True)
                    for q in range(QUADS):
                        wait_drained(pe, "sc", b, t, q)
                        for j in range(4):
                            h = 4 * q + j
                            last = nc.tensor.matmul(dst[SLOT * j:SLOT * (j + 1), q * P:(q + 1) * P],
                                                    vpad[:, b % 2, t, h * SLOT:(h + 1) * SLOT],
                                                    probs[:, q, j * P:(j + 1) * P],
                                                    start=(t == 0 and q == 0), stop=True, skip_group_check=True)
                    last.then_inc(filled, 1)

            def y_T(b):
                for t in range(NT):
                    i = NT * b + t
                    wait_drained(pe, "y", b, t)
                    dst = open_bank("y_T", b, t)
                    for q in range(QUADS):
                        last = nc.tensor.transpose(dst[:, q * P:(q + 1) * P], ys[:, i % 2, q, :], ident)
                    last.then_inc(filled, 1)

            def yn_T(b):
                pe.wait_ge(yn_ready, NT * (b + 1))
                dst = open_bank("yn_T", b)
                for c in range(NC):
                    for t in range(NT):
                        last = nc.tensor.transpose(dst[:, c * S + t * P:c * S + (t + 1) * P],
                                                   yn[:, (NT * b + t) % 4, c * P:(c + 1) * P], ident)
                last.then_inc(filled, 1)

            def o(b):
                pe.wait_ge(y3_lo, b + 1)
                if b == 0:
                    pe.wait_ge(w_ready_p, 4)
                tm_product(("o", b), lambda k: (y3h[:, b % 2, k, :], y3l[:, b % 2, k, :]), NC,
                           lambda k: tuple(w[:, k, :] for w in w_o))

            def f(b):
                wait_drained(pe, "x4_T", b)
                tm_product(("f", b), x_acts(b), NC, lambda k: tuple(w[:, k, :] for w in w_f))

            pe.wait_ge(early_loaded, 16)
            for work, b in walk({
                    "xn_T": turn("xn_T", ("norm_x0", x1)), "left_right": left_right, "gates": gates, "out": out, "quant": quant,
                    "x1_T": turn("x1_T", ("norm_x1", x0o)), "mlp": mlp, "down": down,
                    "x2_T": turn("x2_T", ("norm_x2", x0o)), "ffn": ffn, "ffn_down": ffn_down,
                    "x3_T": turn("x3_T", ("norm_x3", x0)), "qkv": qkv, "qk_T": qk_T, "scores": scores,
                    "y_T": y_T, "yn_T": yn_T, "o": o, "x4_T": turn("x4_T", ("norm_x4", x1)), "f": f}):
                work(b)

        @block.scalar
        def _(act_eng):
            e = act_eng
            A = nc.scalar.activation

            def square_x0(b):
                e.wait_ge(x_loaded[b], 16)
                for t in range(NT):
                    if NT * b + t >= 2:
                        e.wait_ge(squares_ready, NT * b + t - 1)
                    A(square_out[:, t, :], x0[:, b, t, :], ACT.Square, accum_out=ssq[:, b, t:t + 1]).then_inc(squares_ready, 1)

            def turned(stage):
                def work(b):
                    wait_filled(e, stage, b)
                    A(xh[:, b], bank(stage, b)[:, :], ACT.Copy).then_inc(hi_ready, 1)
                return work

            def left_right(b):
                e.wait_ge(vec_loaded, 16)
                wait_filled(e, "left", b)
                for m in range(NC):
                    last = A(left[:, b, m, :], bank("left", b)[:, m * S:(m + 1) * S], ACT.Gelu, bias=v("left_b", m))
                drains(last, "left", b)
                wait_filled(e, "right", b)
                if b >= 2:
                    e.wait_ge(conv_ready, b - 1)
                for m in range(NC):
                    last = A(right[:, b % 2, m, 3:], bank("right", b)[:, m * S:(m + 1) * S], ACT.Identity, bias=v("right_b", m))
                drains(last, "right", b)

            def conv_split(b):
                e.wait_ge(conv_ready, b + 1)
                if b >= 2:
                    wait_filled(e, "gx", b - 2)
                A(ch[:, b % 2], conv[:, b % 2], ACT.Copy).then_inc(conv_hi, 1)

            def gates(b):
                for name, dst in (("ga", r_gate), ("gx", i_gate)):
                    wait_filled(e, name, b)
                    for m in range(NC):
                        last = A(dst[:, b, m, :], bank(name, b)[:, m * S:(m + 1) * S], ACT.Sigmoid, bias=v(f"{name}_b", m))
                    drains(last, name, b)

            def decays(b):
                if b == 0:
                    e.wait_ge(softplus_d, 1)
                wait_drained(e, "ga", b)
                for m in range(NC):
                    last = A(decay[:, b, m, :], r_gate[:, b, m, :], ACT.Exp, scale=decay_c[:, 0, m:m + 1])
                last.then_inc(decay_ready, 1)
                e.wait_ge(decay_ready, b + 1)
                for m in range(NC):
                    last = A(r_gate[:, b, m, :], r_gate[:, b, m, :], ACT.Tanh, scale=decay_c[:, 1, m:m + 1])
                last.then_inc(tanh_ready, 1)

            def scan(b):
                e.wait_ge(mult2_ready, b + 1)
                A(r_gate[:, b], r_gate[:, b], ACT.Sqrt).then_inc(mult_ready, 1)

            def out_split(b):
                e.wait_ge(lr_ready, b + 1)
                if b < 2:
                    wait_filled(e, "gx", b + 2)
                else:
                    wait_filled(e, "out", b - 2)
                A(ch[:, b % 2], left[:, b], ACT.Copy).then_inc(lr_hi, 1)

            def square_x1(b):
                wait_drained(e, "out", b)
                for t in range(NT):
                    e.wait_ge(squares_ready, NT * (B + b) + t - 1)
                    A(square_out[:, t, :], x1[:, b, t, :], ACT.Square, accum_out=ssq[:, b, t:t + 1]).then_inc(squares_ready, 1)

            def gated(b, j, name, n, func, biased, count):
                wait_filled(e, name, b, j)
                if n >= 3:
                    wait_drained(e, *hidden_key(n - 3))
                if biased:
                    for m in range(2):
                        last = A(act[:, n % 3, m, :], bank(name, b, j)[:, m * S:(m + 1) * S], func, bias=v("up1_b", 2 * j + m))
                else:
                    last = A(act[:, n % 3], bank(name, b, j)[:, :], func, scale=qc[:, 0:1])
                drains(last, name, b, j)
                wait_drained(e, *hidden_key(n))
                A(hh[:, b % 2, 2 * j:2 * j + 2, :], hid[:, n % 2], ACT.Copy).then_inc(hid_hi, 1)

            def mlp(b):
                if b >= 2:
                    wait_filled(e, "down", b - 2)
                if b == 0:
                    wait_filled(e, "out", B - 1)
                for j in range(F // 256):
                    gated(b, j, "up1", 3 * b + j, ACT.Gelu, True, None)

            def ffn(b):
                if b == 0:
                    e.wait_ge(scales_ready, 4)
                if b >= 2:
                    wait_filled(e, "ffn_down", b - 2)
                else:
                    wait_filled(e, "down", b + 2)
                for j in range(E // 256):
                    gated(b, j, "fup", 3 * B + 4 * b + j, ACT.Silu, False, None)

            def qkv(b):
                wait_filled(e, "v", b)
                e.wait_ge(vzero, 1)
                if b >= 2:
                    wait_filled(e, "y", b - 2, 1)
                drains(A(vpad[:, b % 2].rearrange("p t (h s) -> p t h s", s=SLOT)[:, :, :, 0:DH],
                         bank("v", b)[:, :].rearrange("p (t h s) -> p t h s", t=NT, s=DH), ACT.Copy), "v", b)
                wait_filled(e, "gate", b)
                drains(A(gate[:, b], bank("gate", b)[:, :], ACT.Silu), "gate", b)

            def qk_T(b):
                for t in range(NT):
                    wait_filled(e, "qk_T", b, t)
                    if b >= 2:
                        wait_filled(e, "y", b - 2, t)
                    drains(A(qkT[:, (NT * b + t) % 4], bank("qk_T", b, t)[:, :], ACT.Copy), "qk_T", b, t)

            def scores(b):
                for t in range(NT):
                    wait_filled(e, "y", b, t)
                    if b >= 1:
                        wait_filled(e, "y_T", b - 1, t)
                    drains(A(ys[:, (NT * b + t) % 2], bank("y", b, t)[:, :], ACT.Copy), "y", b, t)

            def y_T(b):
                for t in range(NT):
                    i = NT * b + t
                    wait_filled(e, "y_T", b, t)
                    src = bank("y_T", b, t)[:, :].rearrange("p (h s) -> p h s", s=SLOT)[:, :, 0:DH]
                    if i >= 2:
                        e.wait_ge(ysum_ready, i - 1)
                    A(ysq[:, i % 2].rearrange("p (h s) -> p h s", s=DH), src, ACT.Square).then_inc(ysq_ready, 1)
                    if i >= 4:
                        wait_filled(e, "yn_T", b - 2)
                    drains(A(yn[:, i % 4].rearrange("p (h s) -> p h s", s=DH), src, ACT.Copy), "y_T", b, t)

            def yn_T(b):
                wait_filled(e, "yn_T", b)
                if b >= 2:
                    e.wait_ge(y3_lo, b - 1)
                for c in range(NC):
                    last = A(y3[:, b % 2, c, :], bank("yn_T", b)[:, c * S:(c + 1) * S], ACT.Identity,
                             scale=v("gn_w", c), bias=v("gn_b", c))
                drains(last, "yn_T", b)
                e.wait_ge(y3_gated, b + 1)
                if b >= 2:
                    wait_filled(e, "o", b - 2)
                A(y3h[:, b % 2], y3[:, b % 2], ACT.Copy).then_inc(y3_hi, 1)

            e.wait_ge(vec_loaded, 16)
            A(sp[:, 0, :], v("a_param", 0, 2), ACT.Abs).then_inc(act_chain, 1)
            e.wait_ge(act_chain, 1)
            A(sp[:, 1, :], sp[:, 0, :], ACT.Exp, scale=-1.0).then_inc(act_chain, 1)
            e.wait_ge(act_chain, 2)
            A(sp[:, 2, :], sp[:, 1, :], ACT.Ln, bias=1.0).then_inc(softplus_a, 1)
            raw = raw_wait(e, "rg")
            for j in range(4):
                for k in range(NC):
                    src = raw[:, (2 * j + k) * D:(2 * j + k + 1) * D]
                    last = A(w_rg[0][:, j, k, :], src, ACT.Copy, scale=v("norm1_w", k)) if j < 2 else \
                        A(w_rg[0][:, j, k, :], src, ACT.Copy)
                last.then_inc(w_hi, 1)
            raw = raw_wait(e, "out_down")
            A(w_out[0][:, :, :], raw[:, 0:2 * D], ACT.Copy).then_inc(w_hi, 1)

            def quant(n):
                raw = raw_wait(e, ("ffn_up", "ffn_gate", "ffn_down")[n])
                for part in range(4 * n, 4 * n + 4):
                    if part >= 1:
                        e.wait_ge(absums_ready, part)
                    at = (part - 4 * n) * 512
                    A(abs_out[:, :], raw[:, at:at + 512], ACT.Abs,
                      accum_out=absums[:, part:part + 1]).then_inc(absums_ready, 1)

            for work, b in walk({
                    "square_x0": square_x0, "xn_T": turned("xn_T"), "left_right": left_right, "conv": conv_split,
                    "gates": gates, "decay": decays, "scan": scan, "lr_split": out_split,
                    "out": square_x1, "quant": quant,
                    "x1_T": turned("x1_T"), "mlp": mlp, "x2_T": turned("x2_T"), "ffn": ffn,
                    "x3_T": turned("x3_T"), "qkv": qkv, "qk_T": qk_T, "scores": scores, "y_T": y_T,
                    "yn_T": yn_T, "x4_T": turned("x4_T")}):
                work(b)

        @block.vector
        def _(dve):
            e, V = dve, nc.vector
            TT, TS, STT = V.tensor_tensor, V.tensor_scalar, V.scalar_tensor_tensor

            def norm(stage, stat_stage, src, dst, mean):
                def work(b):
                    e.wait_ge(rs_ready, rs_count[stat_stage, b])
                    for t in range(NT):
                        if mean:
                            last = TS(dst[:, b, t, :], src[:, b, t, :], mv[:, b, t, 0:1], rs[:, b, t:t + 1],
                                      ALU.subtract, ALU.mult)
                        else:
                            last = TS(dst[:, b, t, :], src[:, b, t, :], rs[:, b, t:t + 1], None, ALU.mult)
                    last.then_inc(out_ready if stage == "final" else normed, 1)
                return work

            def turned(stage):
                def work(b):
                    e.wait_ge(hi_ready, hi_count[stage, b])
                    drains(TT(xl[:, b], bank(stage, b)[:, :].rearrange("p (c s) -> p c s", c=NC),
                              xh[:, b].bitcast(fp32), ALU.subtract), stage, b)
                return work

            def conv_work(b):
                wait_drained(e, "right", b)
                if b == 0:
                    e.wait_ge(pads_ready, 1)
                if b >= 2:
                    e.wait_ge(gated_x, b - 1)
                for k in range(4):
                    for m in range(NC):
                        tap = right[:, b % 2, m, k:k + S]
                        w = v("conv_w", 2 * k + m)
                        dst = conv[:, b % 2, m, :]
                        if k == 0:
                            last = TS(dst, tap, w, v("conv_b", m), ALU.mult, ALU.add)
                        else:
                            e.wait_ge(conv_step, 6 * b + 2 * (k - 1) + m + 1)
                            last = STT(out=dst, in0=tap, scalar=w, in1=dst, op0=ALU.mult, op1=ALU.add)
                        if k < 3:
                            last.then_inc(conv_step, 1)
                last.then_inc(conv_ready, 1)
                e.wait_ge(conv_hi, b + 1)
                TT(cl[:, b % 2], conv[:, b % 2], ch[:, b % 2].bitcast(fp32), ALU.subtract).then_inc(conv_lo, 1)

            def decays(b):
                e.wait_ge(a2_ready, b + 1)
                e.wait_ge(tanh_ready, b + 1)
                STT(out=r_gate[:, b], in0=squared[:, :], scalar=1.0, in1=r_gate[:, b],
                    op0=ALU.add, op1=ALU.mult).then_inc(mult2_ready, 1)

            def scan(b):
                e.wait_ge(mult_ready, b + 1)
                e.wait_ge(gated_x, b + 1)
                TT(i_gate[:, b], i_gate[:, b], r_gate[:, b], ALU.mult).then_inc(scan_step, 1)
                e.wait_ge(scan_step, 3 * b + 1)
                for m in range(NC):
                    V.tensor_tensor_scan(r_gate[:, b, m, :], decay[:, b, m, :], i_gate[:, b, m, :], 0.0,
                                         ALU.mult, ALU.add).then_inc(scan_step, 1)
                e.wait_ge(scan_step, 3 * b + 3)
                TT(left[:, b], left[:, b], r_gate[:, b], ALU.mult).then_inc(lr_ready, 1)

            def lr_split(b):
                e.wait_ge(lr_hi, b + 1)
                TT(cl[:, b % 2], left[:, b], ch[:, b % 2].bitcast(fp32), ALU.subtract).then_inc(lr_lo, 1)

            def out(b):
                wait_filled(e, "out", b)
                e.wait_ge(xo_ready, b + 1)
                drains(TT(x1[:, b], bank("out", b)[:, :].rearrange("p (t d) -> p t d", t=NT), x0o[:, b], ALU.add),
                       "out", b)

            def hidden_lo(b, j, n):
                e.wait_ge(hid_hi, n + 1)
                TT(hl[:, b % 2, 2 * j:2 * j + 2, :], hid[:, n % 2], hh[:, b % 2, 2 * j:2 * j + 2, :].bitcast(fp32),
                   ALU.subtract).then_inc(hid_lo, 1)

            def mlp(b):
                for j in range(F // 256):
                    n = 3 * b + j
                    wait_filled(e, "up2", b, j)
                    wait_drained(e, "up1", b, j)
                    if n >= 2:
                        e.wait_ge(hid_lo, n - 1)
                    for m in range(2):
                        last = STT(out=hid[:, n % 2, m, :], in0=bank("up2", b, j)[:, m * S:(m + 1) * S],
                                   scalar=v("up2_b", 2 * j + m), in1=act[:, n % 3, m, :], op0=ALU.add, op1=ALU.mult)
                    drains(last, "up2", b, j)
                    if j >= 1:
                        hidden_lo(b, j - 1, n - 1)
                hidden_lo(b, j, n)

            def ffn(b):
                for j in range(E // 256):
                    n = 3 * B + 4 * b + j
                    wait_filled(e, "fgate", b, j)
                    wait_drained(e, "fup", b, j)
                    e.wait_ge(hid_lo, n - 1)
                    drains(TT(hid[:, n % 2], bank("fgate", b, j)[:, :].rearrange("p (c s) -> p c s", c=2), act[:, n % 3],
                              ALU.mult), "fgate", b, j)
                    if j >= 1:
                        hidden_lo(b, j - 1, n - 1)
                hidden_lo(b, j, n)

            def close(stage, dst, resid, ready, scaled):
                def work(b):
                    wait_filled(e, stage, b)
                    if ready is not None:
                        e.wait_ge(ready, b + 1)
                    z = bank(stage, b)[:, :].rearrange("p (t d) -> p t d", t=NT)
                    if scaled:
                        last = STT(out=dst[:, b], in0=z, scalar=qc[:, 1:2], in1=resid[:, b], op0=ALU.mult, op1=ALU.add)
                    else:
                        last = TT(dst[:, b], z, resid[:, b], ALU.add)
                    drains(last, stage, b)
                    wait_drained(e, stage, b)
                    n = ln_count[stage, b]
                    for t in range(NT):
                        V.bn_stats(stats[:, b, t, :], dst[:, b, t, :]).then_inc(stats_ready, 1)
                    e.wait_ge(stats_ready, NT * n)
                    for t in range(NT):
                        last = V.bn_aggr(mv[:, b, t, :], stats[:, b, t, :])
                    last.then_inc(var_ready, 1)
                return work

            def qkv(b):
                for t in range(NT):
                    i = NT * b + t
                    wait_filled(e, "qk", b, t)
                    if i == 0:
                        e.wait_ge(tables_loaded, 16)
                    if b >= 2 and t == 0:
                        wait_filled(e, "kv", b - 2)
                    if i >= 2:
                        e.wait_ge(qk_ready, i - 1)
                    TT(qk[:, i % 4, :], bank("qk", b, t)[:, :], rope[:, 0, t, :], ALU.mult).then_inc(cos_done, 1)
                    pairs = lambda ap: ap.rearrange("p (n two) -> p n two", two=2)
                    drains(TT(pairs(qk_sin[:, i % 2, :]), pairs(bank("qk", b, t)[:, :])[:, :, ::-1],
                              pairs(rope[:, 1, t, :]), ALU.mult), "qk", b, t)

            def kv(b):
                wait_filled(e, "kv", b)
                if b == 0:
                    e.wait_ge(masks_loaded, 16)
                if b >= 2:
                    wait_filled(e, "y", b - 2, 1)
                drains(TT(state[:, b % 2], bank("kv", b)[:, :].rearrange("p (c n) -> p c n", c=NC),
                          own_head[:, None, :].to_broadcast([P, NC, 256]), ALU.mult), "kv", b)

            def spread(b):
                for t in range(NT):
                    i = NT * b + t
                    wait_drained(e, "qk_T", b, t)
                    if b >= 1:
                        wait_filled(e, "sc", b - 1, t, QUADS - 1)
                    for c in range(NC):
                        last = TT(qz[i % 2][:, 8 * c:8 * c + 8, :],
                                  qkT[:, i % 4, c, :][:, None, :].to_broadcast([P, 8, P]),
                                  head_rows[:, :, None].to_broadcast([P, 8, P]), ALU.mult)
                    last.then_inc(qz_ready, 1)

            def scores(b):
                for t in range(NT):
                    for q in range(QUADS):
                        wait_filled(e, "sc", b, t, q)
                        if t > 0:
                            wait_filled(e, "y", b, 0)
                        elif b > 0:
                            wait_filled(e, "y", b - 1, NT - 1)
                        drains(TT(probs[:, q, :].rearrange("p (j s) -> p j s", j=4),
                                  bank("sc", b, t, q)[:, :].rearrange("p (j s) -> p j s", j=4),
                                  causal[:, None, :].to_broadcast([P, 4, P]), ALU.mult), "sc", b, t, q)

            def y_T(b):
                for t in range(NT):
                    i = NT * b + t
                    e.wait_ge(ysq_ready, i + 1)
                    V.tensor_reduce(ysum[:, b, t, :], ysq[:, i % 2].rearrange("p (h s) -> p h s", s=DH), AX.X,
                                    ALU.add).then_inc(ysum_ready, 1)

            def yn_work(b):
                for t in range(NT):
                    i = NT * b + t
                    e.wait_ge(yrs_ready, i + 1)
                    wait_drained(e, "y_T", b, t)
                    y = yn[:, i % 4].rearrange("p (h s) -> p h s", s=DH)
                    TT(y, y, yrs[:, b, t, :][:, :, None].to_broadcast([P, H, DH]), ALU.mult).then_inc(yn_ready, 1)

            def yn_T(b):
                wait_drained(e, "yn_T", b)
                wait_drained(e, "gate", b)
                TT(y3[:, b % 2], y3[:, b % 2], gate[:, b], ALU.mult).then_inc(y3_gated, 1)
                e.wait_ge(y3_hi, b + 1)
                TT(y3l[:, b % 2], y3[:, b % 2], y3h[:, b % 2].bitcast(fp32), ALU.subtract).then_inc(y3_lo, 1)

            def prep_up(k):
                e.wait_ge(w_hi_p, k + 1)
                STT(out=w_ups[1][:, k, :], in0=staging[LOAD[f"up_k{k}"] % 2][:, 0:2 * F], scalar=v("norm2_w", k),
                    in1=w_ups[0][:, k, :].bitcast(fp32), op0=ALU.mult, op1=ALU.subtract).then_inc(w_lo, 1)

            def quant(n):
                wait_filled(e, "absum", n)
                drains(V.tensor_reduce(qs[:, n:n + 1], bank("absum", n)[:, 0:4], AX.X, ALU.add), "absum", n)
                wait_drained(e, "absum", n)
                TS(qs[:, n:n + 1], qs[:, n:n + 1], 1.0 / (D * E), EPS_Q, ALU.mult, ALU.add).then_inc(quant_step, 1)
                e.wait_ge(quant_step, n + 1)
                TS(qt[:, 1, n:n + 1], qs[:, n:n + 1], -0.5, None, ALU.mult)
                TS(qt[:, 0, n:n + 1], qs[:, n:n + 1], 0.5, None, ALU.mult).then_inc(scales_ready, 1)
                if n == 2:
                    TS(qc[:, 0:1], qs[:, 0:1], -1.0, None, ALU.mult)
                    TT(qc[:, 1:2], qs[:, 1:2], qs[:, 2:3], ALU.mult).then_inc(scales_ready, 1)

            def ternary(n):
                dst = (q_up, q_gate, q_down)[n]
                e.wait_ge(above_ready, n + 1)
                e.wait_ge(scales_ready, n + 1)
                name = ("ffn_up", "ffn_gate", "ffn_down")[n]
                STT(out=dst[:, :, :], in0=staging[LOAD[name] % 2][:, :].rearrange("p (k n) -> p k n", k=dst.shape[1]),
                    scalar=qt[:, 1, n:n + 1], in1=dst[:, :, :].bitcast(fp32), op0=ALU.is_lt, op1=ALU.subtract)\
                    .then_inc(ternary_ready, 1)

            def prep_qkvg(_):
                raw = raw_wait(e, "qkvg")
                for k in range(NC):
                    part = raw[:, k * 4 * D + 2 * D:k * 4 * D + 3 * D].rearrange("p (h s) -> p h s", s=DH)
                    V.tensor_reduce(vmean[:, k, :], part, AX.X, ALU.add).then_inc(vmean_ready, 1)
                for k in range(NC):
                    part = raw[:, k * 4 * D + 2 * D:k * 4 * D + 3 * D].rearrange("p (h s) -> p h s", s=DH)
                    e.wait_ge(vmean_ready, k + 1)
                    STT(out=part, in0=vmean[:, k, :][:, :, None].to_broadcast([P, H, DH]), scalar=-1.0 / DH, in1=part,
                        op0=ALU.mult, op1=ALU.add).then_inc(centred, 1)

            V.memset(right[:, :, :, 0:3], 0.0).then_inc(pads_ready, 1)
            e.wait_ge(softplus_a, 1)
            chain = [0]

            def link(instruction):
                chain[0] += 1
                instruction.then_inc(softplus_step, 1)
                e.wait_ge(softplus_step, chain[0])

            link(TS(sp[:, 3, :], sp[:, 1, :], 1.0, -1.0, ALU.add, ALU.add))
            link(TS(sp[:, 4, :], sp[:, 3, :], 0.0, None, ALU.is_equal))
            link(TT(sp[:, 5, :], sp[:, 3, :], sp[:, 4, :], ALU.add))
            link(V.reciprocal(sp[:, 6, :], sp[:, 5, :]))
            link(TT(sp[:, 6, :], sp[:, 6, :], sp[:, 2, :], ALU.mult))
            link(TT(sp[:, 6, :], sp[:, 6, :], sp[:, 4, :], ALU.add))
            link(TT(sp[:, 6, :], sp[:, 6, :], sp[:, 1, :], ALU.mult))
            link(STT(out=sp[:, 7, :], in0=v("a_param", 0, 2), scalar=0.0, in1=sp[:, 6, :], op0=ALU.max, op1=ALU.add))
            link(TS(decay_c[:, 0, :], sp[:, 7, :], -C_RGLRU, None, ALU.mult))
            TS(decay_c[:, 1, :], sp[:, 7, :], C_RGLRU, None, ALU.mult).then_inc(softplus_d, 1)
            raw = staging[0]
            for j in range(4):
                e.wait_ge(w_hi, j + 1)
                for k in range(NC):
                    src = raw[:, (2 * j + k) * D:(2 * j + k + 1) * D]
                    hi = w_rg[0][:, j, k, :].bitcast(fp32)
                    last = STT(out=w_rg[1][:, j, k, :], in0=src, scalar=v("norm1_w", k), in1=hi,
                               op0=ALU.mult, op1=ALU.subtract) if j < 2 else \
                        TT(w_rg[1][:, j, k, :], src, hi, ALU.subtract)
                last.then_inc(w_lo, 1)
            e.wait_ge(w_hi, 5)
            TT(w_out[1][:, :, :], staging[1][:, 0:2 * D].rearrange("p (k n) -> p k n", k=NC),
               w_out[0][:, :, :].bitcast(fp32), ALU.subtract).then_inc(w_lo, 1)

            for work, b in walk({
                    "norm_x0": norm("norm_x0", "square_x0", x0, x1, False), "xn_T": turned("xn_T"), "conv": conv_work,
                    "decay": decays, "scan": scan, "lr_split": lr_split, "out": out,
                    "norm_x1": norm("norm_x1", "out", x1, x0o, False), "x1_T": turned("x1_T"), "mlp": mlp,
                    "down": close("down", x0o, x0, xs_ready, False),
                    "norm_x2": norm("norm_x2", "down", x0o, x0o, True), "x2_T": turned("x2_T"), "ffn": ffn,
                    "ffn_down": close("ffn_down", x0, x0o, None, True),
                    "norm_x3": norm("norm_x3", "ffn_down", x0, x0, True), "x3_T": turned("x3_T"), "qkv": qkv,
                    "qk_T": kv, "qz": spread, "scores": scores, "y_T": y_T, "yn": yn_work, "yn_T": yn_T,
                    "o": close("o", x1, x0, None, False),
                    "norm_x4": norm("norm_x4", "o", x1, x1, True), "x4_T": turned("x4_T"),
                    "f": close("f", x0o, x0, x4b_ready, False),
                    "final": norm("final", "f", x0o, x0o, True),
                    "prep_up": prep_up, "quant": quant, "ternary": ternary, "prep_qkvg": prep_qkvg}):
                work(b)

        @block.gpsimd
        def _(pool):
            e, G = pool, nc.gpsimd

            def spread_row(n):
                return rows[:, n, :][:, None, :].to_broadcast([P, NT, D])

            def root(stage, src, scale, eps):
                def work(b):
                    if stage == "square_x0":
                        e.wait_ge(squares_ready, NT * (b + 1))
                    elif stage == "out":
                        e.wait_ge(squares_ready, NT * (B + b + 1))
                    else:
                        e.wait_ge(var_ready, ln_count[stage, b])
                    n = rs_count[stage, b]
                    G.tensor_scalar(rse[:, b, :], src(b), scale, eps, ALU.mult, ALU.add).then_inc(rse_ready, 1)
                    e.wait_ge(rse_ready, n)
                    G.tensor_tensor(rs[:, b, :], rse[:, b, :], neg_half[:, 0:NT], ALU.pow).then_inc(rs_ready, 1)
                return work

            def ssq_of(b):
                return ssq[:, b, :]

            def var_of(b):
                return mv[:, b, :, 1]

            def add_out_b(b):
                if b == 0:
                    e.wait_ge(rows_loaded, 16)
                e.wait_ge(x_loaded[b], 16)
                G.tensor_tensor(x0o[:, b], x0[:, b], spread_row(0), ALU.add).then_inc(xo_ready, 1)

            def gate_x(b):
                wait_drained(e, "gx", b)
                e.wait_ge(conv_ready, b + 1)
                G.tensor_tensor(i_gate[:, b], i_gate[:, b], conv[:, b % 2], ALU.mult).then_inc(gated_x, 1)

            def square_decay(b):
                e.wait_ge(decay_ready, b + 1)
                if b >= 1:
                    e.wait_ge(mult2_ready, b)
                G.tensor_tensor(squared[:, :], decay[:, b], decay[:, b], ALU.mult).then_inc(a2_ready, 1)

            def residual(b):
                e.wait_ge(normed, normed_count["norm_x0", b])
                e.wait_ge(xo_ready, b + 1)
                G.tensor_tensor(x0[:, b], x0[:, b], spread_row(1), ALU.add).then_inc(xs_part, 1)
                e.wait_ge(xs_part, b + 1)
                wait_drained(e, "out", b)
                G.tensor_tensor(x0[:, b], x0[:, b], x1[:, b], ALU.add).then_inc(xs_ready, 1)

            def add_ffn_bias(b):
                e.wait_ge(normed, normed_count["norm_x4", b])
                G.tensor_tensor(x0[:, b], x1[:, b], spread_row(2), ALU.add).then_inc(x4b_ready, 1)

            def qkv(b):
                for t in range(NT):
                    i = NT * b + t
                    wait_drained(e, "qk", b, t)
                    G.tensor_tensor(qk[:, i % 4, :], qk[:, i % 4, :], qk_sin[:, i % 2, :], ALU.add).then_inc(qk_ready, 1)

            def clear_values(b):
                if b == 0:
                    wait_filled(e, "down", B - 1)
                    G.memset(vpad[:, :, :, :], 0.0).then_inc(vzero, 1)

            def y_T(b):
                for t in range(NT):
                    i = NT * b + t
                    e.wait_ge(ysum_ready, i + 1)
                    if i >= 2:
                        e.wait_ge(yrs_ready, i - 1)
                    G.tensor_scalar(yse[:, i % 2, :], ysum[:, b, t, :], 1.0 / DH, EPS_LN, ALU.mult, ALU.add).then_inc(yse_ready, 1)
                    e.wait_ge(yse_ready, i + 1)
                    G.tensor_tensor(yrs[:, b, t, :], yse[:, i % 2, :], neg_half[:, :], ALU.pow).then_inc(yrs_ready, 1)

            def prep_up(k):
                raw = raw_wait(e, f"up_k{k}")
                G.tensor_scalar(w_ups[0][:, k, :], raw[:, 0:2 * F], v("norm2_w", k), None, ALU.mult).then_inc(w_hi_p, 1)

            def split_weights(hi, lo, src):
                G.tensor_scalar(hi, src, 1.0, None, ALU.mult).then_inc(pool_hi, 1)
                pool_his[0] += 1
                e.wait_ge(pool_hi, pool_his[0])
                return G.tensor_tensor(lo, src, hi.bitcast(fp32), ALU.subtract)

            pool_his = [0]

            def prep_down(_):
                raw = raw_wait(e, "out_down")
                e.wait_ge(w_lo, 5)
                split_weights(w_dn[0][:, :, :], w_dn[1][:, :, :],
                              raw[:, 2 * D:8 * D].rearrange("p (k n) -> p k n", k=F // P)).then_inc(w_ready_p, 1)

            def ternary(n):
                name = ("ffn_up", "ffn_gate", "ffn_down")[n]
                dst = (q_up, q_gate, q_down)[n]
                raw = raw_wait(e, name)
                e.wait_ge(scales_ready, n + 1)
                G.tensor_scalar(dst[:, :, :], raw[:, :].rearrange("p (k n) -> p k n", k=dst.shape[1]),
                                qt[:, 0, n:n + 1], None, ALU.is_gt).then_inc(above_ready, 1)

            def prep_qkvg(_):
                raw = raw_wait(e, "qkvg")
                e.wait_ge(centred, NC)
                wait_filled(e, "out", B - 1)
                split_weights(w_qkvg[0][:, :, :], w_qkvg[1][:, :, :],
                              raw[:, :].rearrange("p (k n) -> p k n", k=NC)).then_inc(w_ready_p, 1)

            def prep_f(half):
                raw = raw_wait(e, f"factors{half}")
                for r in range(4):
                    n = 4 * half + r
                    if n == 0:
                        G.tensor_scalar(fsum[:, :], raw[:, 0:512], 1.0, None, ALU.mult).then_inc(fsum_step, 1)
                    else:
                        e.wait_ge(fsum_step, n)
                        G.tensor_tensor(fsum[:, :], fsum[:, :], raw[:, r * 512:(r + 1) * 512], ALU.add).then_inc(fsum_step, 1)
                if half == 1:
                    e.wait_ge(fsum_step, RANK)
                    G.tensor_scalar(fsum[:, :], fsum[:, :], float(RANK) ** -0.5, None, ALU.mult).then_inc(fsum_step, 1)
                    e.wait_ge(fsum_step, RANK + 1)
                    split_weights(w_f[0][:, :, :], w_f[1][:, :, :],
                                  fsum[:, :].rearrange("p (k n) -> p k n", k=NC)).then_inc(w_ready_p, 1)

            def prep_o(_):
                raw = raw_wait(e, "o")
                split_weights(w_o[0][:, :, :], w_o[1][:, :, :],
                              raw[:, 0:2 * D].rearrange("p (k n) -> p k n", k=NC)).then_inc(w_ready_p, 1)

            G.memset(neg_half[:, :], -0.5).then_inc(half_ready, 1)
            e.wait_ge(half_ready, 1)
            for work, b in walk({
                    "square_x0": root("square_x0", ssq_of, 1.0 / D, EPS_RMS), "xn_T": add_out_b, "gates": gate_x,
                    "decay": square_decay, "out": root("out", ssq_of, 1.0 / D, EPS_RMS), "norm_x1": residual,
                    "down": root("down", var_of, 1.0, EPS_LN), "ffn_down": root("ffn_down", var_of, 1.0, EPS_LN),
                    "ffn": clear_values, "qkv": qkv, "y_T": y_T, "o": root("o", var_of, 1.0, EPS_LN),
                    "norm_x4": add_ffn_bias, "f": root("f", var_of, 1.0, EPS_LN),
                    "prep_up": prep_up, "prep_down": prep_down, "ternary": ternary, "prep_qkvg": prep_qkvg,
                    "prep_f": prep_f, "prep_o": prep_o}):
                work(b)


def tables():
    n = np.arange(S, dtype=np.float64)[:, None]
    half = DH // 2
    xscale = (np.arange(0, DH, 2, dtype=np.float64) + 0.4 * DH) / (1.4 * DH)
    scale = xscale[None, :] ** (n / 64.0)
    angle = n * (1.0 / 10000.0 ** (np.arange(half, dtype=np.float64) / half))[None, :]
    gamma = 1.0 - np.exp(np.linspace(np.log(1.0 / 32), np.log(1.0 / 64), H))
    sign = np.tile([-1.0, 1.0], half)
    table = np.zeros((2, S, 2, H, DH))
    for part, (s, g) in enumerate(((scale, gamma[None, :] ** n), (1.0 / scale, gamma[None, :] ** -n))):
        for which, wave in enumerate((np.cos(angle), np.sin(angle))):
            row = np.repeat(wave * s, 2, axis=1) * (sign if which else 1.0)
            table[which, :, part] = g[:, :, None] * row[:, None, :]
    rope = table.reshape(2, NT, P, 2 * D).transpose(2, 0, 1, 3).reshape(P, -1)
    p = np.arange(P)
    causal = p[None, :] >= p[:, None]
    own_head = p[:, None] // DH == np.arange(8 * SLOT)[None, :] // SLOT
    head_rows = p[:, None] // DH == np.arange(8)[None, :]
    early = np.concatenate([np.eye(P), np.ones((P, P))], axis=1)
    return early.astype(np.float32), np.concatenate([rope, causal, own_head, head_rows], axis=1).astype(np.float32)


def kernel(**inputs):
    import concourse.bacc as bacc
    from concourse.bass_utils import run_bass_kernel_spmd as run

    a = {k: np.asarray(x) for k, x in inputs.items()}

    def by_chunk(w):
        return w.reshape(-1, P, w.shape[1]).transpose(1, 0, 2).reshape(P, -1)

    def columns(x):
        return x.reshape(-1, P).T

    def heads(w):
        return w.transpose(1, 0, 2).reshape(D, D)

    vec = np.concatenate([columns(x) for x in (
        a["L0_attn_norm1_w"], a["L0_attn_left_b"], a["L0_attn_right_b"], a["L0_attn_conv_w"].reshape(-1),
        a["L0_attn_conv_b"], a["L0_attn_ga_b"], a["L0_attn_gx_b"], a["L0_attn_a_param"], a["L0_attn_norm2_w"],
        a["L0_attn_up1_b"], a["L0_attn_up2_b"], a["L1_attn_gn_weight"], a["L1_attn_gn_bias"])], axis=1)
    row = np.broadcast_to(np.stack([a["L0_attn_out_b"], a["L0_attn_down_b"], a["L1_ffn_bias"]]), (P, 3, D))
    ups = np.concatenate([a["L0_attn_up1_W"], a["L0_attn_up2_W"]], axis=1)
    qkvg = np.concatenate([heads(a["L1_attn_W_Q"]), heads(a["L1_attn_W_K"]), heads(a["L1_attn_W_V"]),
                           a["L1_attn_W_G"]], axis=1)
    factors = [by_chunk(f) for f in a["L1_ffn_factors"]]
    weights = np.concatenate(
        [by_chunk(a[f"L0_attn_{n}_W"]) for n in ("left", "right", "ga", "gx", "out", "down")]
        + [ups[0:P], ups[P:2 * P], by_chunk(a["L0_ffn_W_up"].T), by_chunk(a["L0_ffn_W_gate"].T),
           by_chunk(a["L0_ffn_W_down"].T), by_chunk(qkvg)] + factors + [by_chunk(a["L1_attn_W_O"])], axis=1)
    early, table = tables()
    arrays = {
        "x": a["L0_attn_x"].reshape(B, NT, P, D).transpose(2, 0, 1, 3),
        "vectors": vec, "rows": row, "early": early, "tables": table, "weights": weights,
    }
    arrays = {k: np.ascontiguousarray(x) for k, x in arrays.items()}
    assert arrays["weights"].shape[1] == N_WEIGHTS and vec.shape[1] == N_VECTORS
    nc = bacc.Bacc("TRN2", target_bir_lowering=False, num_devices=1)
    args = [nc.dram_tensor(k, x.shape, mybir.dt.float32, kind="ExternalInput").ap() for k, x in arrays.items()]
    out = nc.dram_tensor("out", (P, B, NT, D), mybir.dt.float32, kind="ExternalOutput").ap()
    build(nc, *args, out)
    got = run(nc, [arrays], core_ids=[0]).results[0]["out"]
    return np.ascontiguousarray(got.transpose(1, 2, 0, 3).reshape(B, S, D))
```

```python
import numpy as np
import concourse.bass as bass
from concourse import mybir
from contextlib import ExitStack

B, S, D = 4, 256, 256
P = 128
NT, NC = S // P, D // P
F, E = 768, 1024
H, DH = 16, 16
CH = 64
SLOT = 2 * DH
QUADS = H // 4
RANK = 8
BANKS = 8
EPS_RMS, EPS_Q, EPS_LN = 1e-8, 1e-8, 1e-5
C_RGLRU = 8.0

VECTORS, _at = {}, 0
for _name, _n in (("norm1_w", 2), ("left_b", 2), ("right_b", 2), ("conv_w", 8), ("conv_b", 2),
                  ("ga_b", 2), ("gx_b", 2), ("a_param", 2), ("norm2_w", 2), ("up1_b", 6),
                  ("up2_b", 6), ("gn_w", 2), ("gn_b", 2)):
    VECTORS[_name] = _at
    _at += _n
N_VECTORS = _at

LOADS, _at = [], 0
for _name, _n in (("rg", 4 * 512), ("out_down", 512 + 6 * 256), ("up_k0", 2 * F), ("up_k1", 2 * F),
                  ("ffn_up", 2 * E), ("ffn_gate", 2 * E), ("qkvg", 4 * 512),
                  ("factors0", 2048), ("factors1", 2048), ("o", 512), ("ffn_down", 2 * E)):
    LOADS.append((_name, _at, _n))
    _at += _n
N_WEIGHTS = _at
LOAD = {name: n for n, (name, _, _) in enumerate(LOADS)}
TERNARY = ("ffn_down", "ffn_up", "ffn_gate")

STAGES = [
    ("x4_T", 42), ("final", 46), ("norm_x4", 41), ("f", 43), ("o", 40), ("yn_T", 39), ("yn", 38),
    ("y_T", 37), ("scores", 36), ("ternary", 10), ("ffn", 29), ("qk_T", 35), ("qz", 35), ("qkv", 34),
    ("x2_T", 28), ("norm_x2", 27), ("x3_T", 33), ("norm_x3", 31), ("mlp", 25), ("ffn_down", 30),
    ("down", 26), ("decay", 15), ("x1_T", 23), ("out", 20), ("norm_x1", 21), ("gates", 8), ("lr_split", 18),
    ("conv", 5), ("scan", 17), ("xn_T", 2), ("left_right", 4), ("norm_x0", 0), ("square_x0", 0),
    ("conv_split", 6), ("prep_out", 2), ("add_out_b", 18), ("residual", 22), ("quant", 9), ("prep_rg", 0),
    ("prep_down", 3), ("prep_up", 7), ("absum", 7), ("prep_f", 29), ("prep_o", 30), ("centre", 17),
    ("prep_qkvg", 24), ("lo_qkvg", 24), ("clear", 32),
]
COUNT = {"prep_up": 2, "prep_rg": 4, "prep_out": 1, "prep_down": 1, "absum": 3, "quant": 3, "ternary": 3, "centre": 1, "prep_qkvg": 1, "lo_qkvg": 1, "prep_f": 2, "prep_o": 1}
STRIDE = {"absum": 3, "quant": 2, "ternary": 2}
STEPS = max(s for _, s in STAGES) + B


def walk(work):
    for step in range(STEPS):
        for stage, start in STAGES:
            n, rest = divmod(step - start, STRIDE.get(stage, 1))
            if stage in work and rest == 0 and 0 <= n < COUNT.get(stage, B):
                yield work[stage], n


GROUPS = {
    "xn_T": [("xn_T",)], "left_right": [("left",), ("right",)], "gates": [("ga",), ("gx",)],
    "out": [("out",)], "x1_T": [("x1_T",)],
    "mlp": [(k, j) for j in range(F // 256) for k in ("up1", "up2")],
    "down": [("down",)], "x2_T": [("x2_T",)],
    "ffn": [(k, j) for j in range(E // 256) for k in ("fup", "fgate")],
    "ffn_down": [("ffn_down",)], "x3_T": [("x3_T",)],
    "qkv": [("qk", 0), ("qk", 1), ("v",), ("gate",)],
    "qk_T": [("qk_T", 0), ("qk_T", 1), ("kv", 0), ("kv", 1)],
    "scores": [("sc", t, c) for t in range(NT) for c in range(NC)] + [("y", 0), ("y", 1)],
    "y_T": [("y_T",)], "yn_T": [("yn_T",)], "o": [("o",)], "x4_T": [("x4_T",)],
    "f": [("f",)], "quant": [("absum",)],
}


def number_groups():
    order = []
    for (stage, b) in walk({s: s for s in GROUPS}):
        order += [(key[0], b, *key[1:]) for key in GROUPS[stage]]
    return {key: n for n, key in enumerate(order)}


def build(nc, x_dram, vec_dram, row_dram, early_dram, table_dram, w_dram, out_dram):
    fp32, fp32r = mybir.dt.float32, mybir.dt.float32r
    ALU, ACT, AX = mybir.AluOpType, mybir.ActivationFunctionType, mybir.AxisListType
    number = number_groups()

    ctx = ExitStack()
    with ctx:
        def sb(name, shape, dt=fp32, scope=None):
            return (scope or ctx).enter_context(nc.sbuf_tensor(name, shape, dt))

        def sem(name):
            return ctx.enter_context(nc.semaphore(name))

        x0 = sb("x0", [P, B, NT, D])
        x0o = sb("x0o", [P, B, NT, D])
        x1 = sb("x1", [P, B, NT, D])
        xh = sb("xh", [P, B, NC, S], fp32r)
        xl = sb("xl", [P, B, NC, S], fp32r)
        staging = [sb(f"staging{i}", [P, 2048]) for i in range(2)]
        q_up = sb("q_up", [P, NC, E], fp32r)
        q_gate = sb("q_gate", [P, NC, E], fp32r)
        q_down = sb("q_down", [P, E // P, D], fp32r)
        rope = sb("rope", [P, 2, NT, 2 * D])
        raw_ffn_down = rope[:, :, :, :].rearrange("p w t n -> p (w t n)")
        early = sb("consts", [P, 2 * P])
        ident, ones = early[:, 0:P], early[:, P:2 * P]
        masks = sb("masks", [P, 3 * CH + 8])
        causal, head_rows = masks[:, 0:CH], masks[:, 3 * CH:3 * CH + 8]
        pick = [masks[:, (1 + a) * CH:(2 + a) * CH] for a in range(2)]
        rows = sb("row_vectors", [P, 3, D])
        vec = sb("vec", [P, N_VECTORS])
        stats = sb("stats", [P, B, NT, 6])
        mv = sb("mv", [P, B, NT, 2])
        ssq = sb("ssq", [P, B, NT])
        rs = sb("rs", [P, B, NT])
        rse = sb("rse", [P, B, NT])
        neg_half = sb("neg_half", [P, NT * H])
        sp = sb("sp", [P, 9, 2])
        decay_c = sb("decay_c", [P, 2, 2])
        absums = sb("absums", [P, 12])
        qs = sb("qs", [P, 3])
        qt = sb("qt", [P, 2, 3])
        qc = sb("qc", [P, 2])
        vmean = sb("vmean", [P, NC, H])
        ysum = sb("ysum", [P, B, NT, H])
        yrs = sb("yrs", [P, B, NT, H])
        square_out = sb("square_out", [P, 2, 256], mybir.dt.bfloat16)
        abs_out = sb("abs_out", [P, 512], mybir.dt.bfloat16)
        yse = sb("yse", [P, NT * H])

        with ExitStack() as r1:
            w_ups = [sb(f"w_ups_{k}", [P, NC, 2 * F], fp32r, r1) for k in ("hi", "lo")]
            w_dn = [sb(f"w_down_{k}", [P, F // P, D], fp32r, r1) for k in ("hi", "lo")]
        r1 = ctx.enter_context(ExitStack())
        qz = [sb(f"qz{i}", [P, H, P], fp32, r1) for i in range(2)]
        vpad = sb("vpad", [P, 2, NT, H * SLOT], fp32, r1)
        probs = sb("probs", [P, 4, 8 * CH], fp32, r1)
        state_b = sb("state_b", [P, 2, NC, 8 * SLOT], fp32, r1)

        with ExitStack() as r2:
            lru = sb("lru", [P, B, 4, NC, S], fp32, r2)
            right = sb("right", [P, 2, NC, S + 3], fp32, r2)
            squared = sb("squared", [P, NC, S], fp32, r2)
            sb("spare", [P, 2 * NC * S], fp32, r2)
            ch = sb("ch", [P, 2, NC, S], fp32r, r2)
            cl = sb("cl", [P, 2, NC, S], fp32r, r2)
        left, r_gate, i_gate, decay = (lru[:, :, n, :, :] for n in range(4))
        conv = decay
        with ExitStack() as r2:
            hidden = [[sb(f"hidden{i}_{k}", [P, E // P, S], fp32r, r2) for k in ("hi", "lo")] for i in range(2)]
            hid = sb("hid", [P, 2, 2, S], fp32, r2)
            sb("pad_mlp", [P, 12], fp32, r2)
            act = sb("act", [P, 3, 2, S], fp32, r2)
            fsum = sb("fsum", [P, NC * D], fp32, r2)
        hh, hl = ([hidden[i][k] for i in range(2)] for k in range(2))
        r2 = ctx.enter_context(ExitStack())
        qk = sb("qk", [P, 4, 2 * D], fp32, r2)
        qk_sin = sb("qk_sin", [P, 2, 2 * D], fp32, r2)
        qkT = sb("qkT", [P, 4, 4, P], fp32, r2)
        ys = sb("ys", [P, 2, QUADS, CH], fp32, r2)
        state_a = sb("state_a", [P, NC, 8 * SLOT], fp32, r2)
        ysq = sb("ysq", [P, NT, D], fp32, r2)
        yn = sb("yn", [P, 4, D], fp32, r2)
        gate = sb("gate", [P, B, NC, S], fp32, r2)
        y3 = sb("y3", [P, 2, NC, S], fp32, r2)
        y3h = sb("y3h", [P, 2, NC, S], fp32r, r2)
        y3l = sb("y3l", [P, 2, NC, S], fp32r, r2)
        sb("pad", [P, 12], fp32, r2)

        with ExitStack() as r3:
            w_rg = [sb(f"w_rg_{k}", [P, 4, NC, D], fp32r, r3) for k in ("hi", "lo")]
            w_out = [sb(f"w_out_{k}", [P, NC, D], fp32r, r3) for k in ("hi", "lo")]
        r3 = ctx.enter_context(ExitStack())
        w_qkvg = [sb(f"w_qkvg_{k}", [P, NC, 4 * D], fp32r, r3) for k in ("hi", "lo")]
        w_o = [sb(f"w_o_{k}", [P, NC, D], fp32r, r3) for k in ("hi", "lo")]
        w_f = [sb(f"w_f_{k}", [P, NC, D], fp32r, r3) for k in ("hi", "lo")]

        banks = [ctx.enter_context(nc.psum_tensor(f"bank{i}", [P, 512], fp32)) for i in range(BANKS)]

        x_loaded = [sem(f"x_loaded{b}") for b in range(B)]
        vec_loaded, rows_loaded = sem("vec_loaded"), sem("rows_loaded")
        early_loaded, tables_loaded, masks_loaded = sem("early_loaded"), sem("tables_loaded"), sem("masks_loaded")
        ffn_down_loaded = sem("ffn_down_loaded")
        raw_loaded = [sem(f"raw_loaded{i}") for i in range(2)]
        filled = sem("filled")
        drained = [sem(f"drained{k}") for k in range(BANKS)]
        half_ready = sem("half_ready")
        pads_ready = sem("pads_ready")
        squares_ready = sem("squares_ready")
        var_ready, rs_ready = sem("var_ready"), sem("rs_ready")
        act_chain = sem("act_chain")
        for_names = ("stats_ready", "quant_step", "vmean_ready", "centred", "softplus_step", "rse_ready",
                     "yse_ready", "pool_hi", "fsum_step")
        (stats_ready, quant_step, vmean_ready, centred, softplus_step, rse_ready, yse_ready, pool_hi,
         fsum_step) = (sem(x) for x in for_names)
        normed = sem("normed")
        hi_ready = sem("hi_ready")
        w_hi, w_lo = sem("w_hi"), sem("w_lo")
        w_ready_p = sem("w_ready_p")
        softplus_a, softplus_d = sem("softplus_a"), sem("softplus_d")
        absums_ready = sem("absums_ready")
        scales_ready, above_ready, ternary_ready = sem("scales_ready"), sem("above_ready"), sem("ternary_ready")
        xo_ready, xs_part, xs_ready, x4b_ready = sem("xo_ready"), sem("xs_part"), sem("xs_ready"), sem("x4b_ready")
        conv_step, conv_ready, conv_hi, conv_lo = (
            sem(x) for x in ("conv_step", "conv_ready", "conv_hi", "conv_lo"))
        gated_x, decay_ready, tanh_ready, a2_ready, mult2_ready = (
            sem("gated_x"), sem("decay_ready"), sem("tanh_ready"), sem("a2_ready"), sem("mult2_ready"))
        mult_ready, scan_step, lr_ready, lr_hi, lr_lo = (
            sem("mult_ready"), sem("scan_step"), sem("lr_ready"), sem("lr_hi"), sem("lr_lo"))
        hid_hi, hid_lo = sem("hid_hi"), sem("hid_lo")
        cos_done, sin_done, qk_ready = sem("cos_done"), sem("sin_done"), sem("qk_ready")
        state_part, state_ready, vzero, qz_ready, probs_ready = sem("state_part"), sem("state_ready"), sem("vzero"), sem("qz_ready"), sem("probs_ready")
        qz_ready_a, qz_ready_p = sem("qz_ready_a"), sem("qz_ready_p")
        ysq_ready, ysum_ready, yrs_ready, yn_ready = sem("ysq_ready"), sem("ysum_ready"), sem("yrs_ready"), sem("yn_ready")
        y3_ready, y3_gated, y3_hi, y3_lo = sem("y3_ready"), sem("y3_gated"), sem("y3_hi"), sem("y3_lo")
        out_ready = sem("out_ready")
        out_stored = [sem(f"out_stored{b}") for b in range(B)]

        def bank(*key):
            return banks[number[key] % BANKS]

        def wait_filled(eng, *key):
            eng.wait_ge(filled, number[key] + 1)

        def wait_drained(eng, *key):
            eng.wait_ge(drained[number[key] % BANKS], number[key] // BANKS + 1)

        def drains(instruction, *key):
            instruction.then_inc(drained[number[key] % BANKS], 1)

        def v(name, c=0, n=1):
            return vec[:, VECTORS[name] + c:VECTORS[name] + c + n]

        def raw_wait(eng, name):
            n = LOAD[name]
            if name == "ffn_down":
                eng.wait_ge(ffn_down_loaded, 16)
                return raw_ffn_down
            eng.wait_ge(raw_loaded[n % 2], 16 * (n // 2 + 1))
            return staging[n % 2]

        hi_count = {}
        for stage, b in walk({s: s for s in ("xn_T", "x1_T", "x2_T", "x3_T", "x4_T")}):
            hi_count[stage, b] = len(hi_count) + 1
        def hidden_key(n):
            return ("up2", n // 3, n % 3) if n < 3 * B else ("fgate", (n - 3 * B) // 4, (n - 3 * B) % 4)

        weight_count = {}
        for stage, n in walk({s: s for s in ("prep_rg", "prep_out", "prep_up", "prep_down", "prep_qkvg")}):
            weight_count[stage, n] = len(weight_count) + 1

        pool_count = {}
        for stage, n in walk({s: s for s in ("prep_f", "prep_o")}):
            if (stage, n) != ("prep_f", 0):
                pool_count[stage, n] = len(pool_count) + 1

        rs_count = {}
        for stage, b in walk({s: s for s in ("square_x0", "out", "down", "ffn_down", "o", "f")}):
            rs_count[stage, b] = len(rs_count) + 1
        ln_count = {}
        for stage, b in walk({s: s for s in ("down", "ffn_down", "o", "f")}):
            ln_count[stage, b] = len(ln_count) + 1
        normed_count = {}
        for stage, b in walk({s: s for s in ("norm_x0", "norm_x1", "norm_x2", "norm_x3", "norm_x4")}):
            normed_count[stage, b] = len(normed_count) + 1

        def slots(ap):
            if len(ap.shape) == 2:
                return ap[:, :].rearrange("p (c h a s) -> p c h a s", c=NC, a=2, s=DH)
            return ap[:, :, :].rearrange("p c (h a s) -> p c h a s", a=2, s=DH)

        own_head = head_rows[:, None, :, None].to_broadcast([P, NC, 8, DH])

        block = ctx.enter_context(nc.Block())

        @block.sync
        def _(sp_eng):
            e = sp_eng
            last_use = [(w_lo, weight_count["prep_rg", 3]),
                        (w_lo, max(weight_count["prep_out", 0], weight_count["prep_down", 0])),
                        (w_lo, weight_count["prep_up", 0]), (w_lo, weight_count["prep_up", 1])]
            last_use += [(ternary_ready, 2), (ternary_ready, 3)]
            last_use += [(w_lo, weight_count["prep_qkvg", 0]), (fsum_step, 4)]
            e.dma_start(early[:, :], early_dram).then_inc(early_loaded, 16)
            e.dma_start(vec[:, :], vec_dram).then_inc(vec_loaded, 16)
            for b in range(B):
                e.dma_start(x0[:, b], x_dram[:, b]).then_inc(x_loaded[b], 16)
                if b in (0, B - 1):
                    n = min(b, 1)
                    _, at, cols = LOADS[n]
                    e.dma_start(staging[n][:, 0:cols], w_dram[:, at:at + cols]).then_inc(raw_loaded[n], 16)
            e.dma_start(rows[:, :, :], row_dram).then_inc(rows_loaded, 16)
            _, at, cols = LOADS[-1]
            e.dma_start(raw_ffn_down, w_dram[:, at:at + cols]).then_inc(ffn_down_loaded, 16)
            for n in range(2, len(LOADS) - 1):
                _, at, cols = LOADS[n]
                e.wait_ge(*last_use[n - 2])
                e.dma_start(staging[n % 2][:, 0:cols], w_dram[:, at:at + cols]).then_inc(raw_loaded[n % 2], 16)
                if n == LOAD["factors0"]:
                    e.wait_ge(ternary_ready, 1)
                    e.dma_start(rope[:, :, :, :], table_dram[:, 0:4 * 2 * D]).then_inc(tables_loaded, 16)
                    e.dma_start(masks[:, :], table_dram[:, 4 * 2 * D:]).then_inc(masks_loaded, 16)
            for b in range(B):
                e.wait_ge(out_ready, b + 1)
                e.dma_start(out_dram[:, b], x0o[:, b]).then_inc(out_stored[b], 16)
            for b in range(B):
                e.wait_ge(out_stored[b], 16)

        @block.tensor
        def _(pe):
            def open_bank(*key):
                n = number[key]
                if n >= BANKS:
                    pe.wait_ge(drained[n % BANKS], n // BANKS)
                return banks[n % BANKS]

            def split_product(out, stationary, moving, first=True):
                terms = []
                for (sh, sl), (mh, ml) in zip(stationary, moving):
                    if sl is not None:
                        terms.append((sl, mh))
                    if ml is not None:
                        terms.append((sh, ml))
                terms += [(sh, mh) for (sh, _), (mh, _) in zip(stationary, moving)]
                for n, (a, m) in enumerate(terms):
                    last = nc.tensor.matmul(out, a, m, start=(first and n == 0), stop=(n == len(terms) - 1),
                                            skip_group_check=True)
                return last

            def fm_product(key, weights, k_chunks, acts, m_at=0):
                out = open_bank(*key)
                for m in range(2):
                    last = split_product(
                        out[:, m * S:(m + 1) * S],
                        [weights(k, m_at + m) for k in range(k_chunks)],
                        [acts(k) for k in range(k_chunks)], first=(m == 0))
                last.then_inc(filled, 1)

            def tm_product(key, acts, k_chunks, weights):
                out = open_bank(*key)
                for t in range(NT):
                    last = split_product(
                        out[:, t * D:(t + 1) * D],
                        [tuple(None if a is None else a[:, t * P:(t + 1) * P] for a in acts(k))
                         for k in range(k_chunks)],
                        [weights(k) for k in range(k_chunks)], first=(t == 0))
                last.then_inc(filled, 1)

            def x_acts(b):
                return lambda k: (xh[:, b, k, :], xl[:, b, k, :])

            def turn(stage, source):
                def work(b):
                    pe.wait_ge(normed, normed_count[source[0], b])
                    out = open_bank(stage, b)
                    for c in range(NC):
                        for t in range(NT):
                            last = nc.tensor.transpose(out[:, c * S + t * P:c * S + (t + 1) * P],
                                                       source[1][:, b, t, c * P:(c + 1) * P], ident)
                    last.then_inc(filled, 1)
                return work

            def left_right(b):
                wait_drained(pe, "xn_T", b)
                for j, name in enumerate(("left", "right")):
                    if b == 0:
                        pe.wait_ge(w_lo, weight_count["prep_rg", j])
                    fm_product((name, b), lambda k, m: tuple(w[:, j, k, m * P:(m + 1) * P] for w in w_rg), NC, x_acts(b))

            def quant(n):
                pe.wait_ge(absums_ready, 4 * (n + 1))
                nc.tensor.matmul(open_bank("absum", n)[:, 0:4], ones, absums[:, 4 * n:4 * n + 4],
                                 start=True, stop=True).then_inc(filled, 1)

            def gates(b):
                pe.wait_ge(conv_lo, b + 1)
                for j, name in enumerate(("ga", "gx")):
                    if b == 0:
                        pe.wait_ge(w_lo, weight_count["prep_rg", j + 2])
                    fm_product((name, b), lambda k, m: tuple(w[:, 2 + j, k, m * P:(m + 1) * P] for w in w_rg), NC,
                               lambda k: (ch[:, b % 2, k, :], cl[:, b % 2, k, :]))

            def out(b):
                pe.wait_ge(lr_lo, b + 1)
                if b == 0:
                    pe.wait_ge(w_lo, weight_count["prep_out", 0])
                tm_product(("out", b), lambda k: (ch[:, b % 2, k, :], cl[:, b % 2, k, :]), NC,
                           lambda k: tuple(w[:, k, :] for w in w_out))

            def mlp(b):
                wait_drained(pe, "x1_T", b)
                if b == 0:
                    pe.wait_ge(w_lo, weight_count["prep_up", 1])
                for j in range(F // 256):
                    for n, name in enumerate(("up1", "up2")):
                        fm_product((name, b, j), lambda k, m: tuple(w[:, k, n * F + m * P:n * F + (m + 1) * P] for w in w_ups),
                                   NC, x_acts(b), m_at=2 * j)

            def down(b):
                if b == 0:
                    pe.wait_ge(w_lo, weight_count["prep_down", 0])
                pe.wait_ge(hid_lo, 3 * (b + 1))
                tm_product(("down", b), lambda k: (hh[b % 2][:, k, :], hl[b % 2][:, k, :]), F // P,
                           lambda k: tuple(w[:, k, :] for w in w_dn))

            def ffn(b):
                wait_drained(pe, "x2_T", b)
                if b == 0:
                    pe.wait_ge(ternary_ready, 3)
                for j in range(E // 256):
                    for name, w in (("fup", q_up), ("fgate", q_gate)):
                        fm_product((name, b, j), lambda k, m: (w[:, k, m * P:(m + 1) * P], None), NC, x_acts(b), m_at=2 * j)

            def ffn_down(b):
                pe.wait_ge(hid_lo, 3 * B + 4 * (b + 1))
                tm_product(("ffn_down", b), lambda k: (hh[b % 2][:, k, :], hl[b % 2][:, k, :]), E // P,
                           lambda k: (q_down[:, k, :], None))

            def qkv(b):
                wait_drained(pe, "x3_T", b)
                if b == 0:
                    pe.wait_ge(w_lo, weight_count["prep_qkvg", 0])
                    pe.wait_ge(w_ready_p, pool_count["prep_f", 1])
                def tile(k, t):
                    return xh[:, b, k, t * P:(t + 1) * P], xl[:, b, k, t * P:(t + 1) * P]
                for t in range(NT):
                    dst = open_bank("qk", b, t)
                    split_product(dst[:, :], [tile(k, t) for k in range(NC)],
                                  [tuple(w[:, k, 0:2 * D] for w in w_qkvg) for k in range(NC)]).then_inc(filled, 1)
                tm_product(("v", b), x_acts(b), NC, lambda k: tuple(w[:, k, 2 * D:3 * D] for w in w_qkvg))
                fm_product(("gate", b), lambda k, m: tuple(w[:, k, 3 * D + m * P:3 * D + (m + 1) * P] for w in w_qkvg),
                           NC, x_acts(b))

            def qk_T(b):
                for t in range(NT):
                    i = NT * b + t
                    pe.wait_ge(qk_ready, i + 1)
                    dst = open_bank("qk_T", b, t)
                    for c in range(4):
                        last = nc.tensor.transpose(dst[:, c * P:(c + 1) * P], qk[:, i % 4, c * P:(c + 1) * P], ident)
                    last.then_inc(filled, 1)
                wait_drained(pe, "v", b)
                for t in range(NT):
                    dst = open_bank("kv", b, t)
                    for c in range(NC):
                        last = nc.tensor.matmul(dst[:, c * 256:(c + 1) * 256],
                                                qk[:, (NT * b + t) % 4, D + c * P:D + (c + 1) * P],
                                                vpad[:, b % 2, t, c * 256:(c + 1) * 256], start=(c == 0), stop=True,
                                                skip_group_check=True)
                    last.then_inc(filled, 1)

            def scores(b):
                for t in range(NT):
                    i = NT * b + t
                    pe.wait_ge(qz_ready, i + 1)
                    pe.wait_ge(qz_ready_a, i + 1)
                    pe.wait_ge(qz_ready_p, i + 1)
                    for c in range(NC):
                        dst = open_bank("sc", b, t, c)
                        for a in range(2):
                            part = slice(a * CH, (a + 1) * CH)
                            last = nc.tensor.matmul(dst[part, :], qkT[:, i % 4, 2 + c, part], qz[i % 2][:, 8 * c:8 * c + 8, part],
                                                    start=True, stop=True, skip_group_check=True)
                        last.then_inc(filled, 1)
                for t in range(NT):
                    i = NT * b + t
                    dst = open_bank("y", b, t)
                    pe.wait_ge(state_ready, 2 * b + t + 1)
                    for q in range(QUADS):
                        half = slice((q % 2) * P, (q % 2 + 1) * P)
                        for a, state in ((0, state_a), (1, state_b[:, t])):
                            if t == 0 and a == 0:
                                continue
                            nc.tensor.matmul(dst[:, q * CH:(q + 1) * CH], state[:, q // 2, half],
                                             qkT[:, i % 4, q // 2, a * CH:(a + 1) * CH],
                                             start=(q == 0 and a == 1 - t), stop=False, skip_group_check=True)
                    for q in range(QUADS):
                        wait_drained(pe, "sc", b, t, q // 2)
                        for j in range(4):
                            h = 4 * q + j
                            last = nc.tensor.matmul(dst[SLOT * j:SLOT * (j + 1), q * CH:(q + 1) * CH],
                                                    vpad[:, b % 2, t, h * SLOT:(h + 1) * SLOT],
                                                    probs[:, 2 * t + h // 8, (h % 8) * CH:(h % 8 + 1) * CH],
                                                    start=False, stop=True, skip_group_check=True)
                    last.then_inc(filled, 1)

            def y_T(b):
                dst = open_bank("y_T", b)
                for t in range(NT):
                    wait_drained(pe, "y", b, t)
                    for q in range(QUADS):
                        at = t * D + q * 4 * DH
                        for a in range(2):
                            last = nc.tensor.matmul(dst[a * CH:(a + 1) * CH, at:at + 4 * DH], ys[:, (NT * b + t) % 2, q, :],
                                                    pick[a], start=(t == 0 and q == 0), stop=True, skip_group_check=True)
                last.then_inc(filled, 1)

            def yn_T(b):
                pe.wait_ge(yn_ready, b + 1)
                dst = open_bank("yn_T", b)
                for c in range(NC):
                    for t in range(NT):
                        last = nc.tensor.transpose(dst[:, c * S + t * P:c * S + (t + 1) * P],
                                                   yn[:, (NT * b + t) % 4, c * P:(c + 1) * P], ident)
                last.then_inc(filled, 1)

            def o(b):
                pe.wait_ge(y3_lo, b + 1)
                if b == 0:
                    pe.wait_ge(w_ready_p, pool_count["prep_o", 0])
                tm_product(("o", b), lambda k: (y3h[:, b % 2, k, :], y3l[:, b % 2, k, :]), NC,
                           lambda k: tuple(w[:, k, :] for w in w_o))

            def f(b):
                wait_drained(pe, "x4_T", b)
                if b == 0:
                    pe.wait_ge(w_ready_p, pool_count["prep_f", 1])
                tm_product(("f", b), x_acts(b), NC, lambda k: tuple(w[:, k, :] for w in w_f))

            pe.wait_ge(early_loaded, 16)
            for work, b in walk({
                    "xn_T": turn("xn_T", ("norm_x0", x1)), "left_right": left_right, "gates": gates, "out": out, "quant": quant,
                    "x1_T": turn("x1_T", ("norm_x1", x0o)), "mlp": mlp, "down": down,
                    "x2_T": turn("x2_T", ("norm_x2", x0o)), "ffn": ffn, "ffn_down": ffn_down,
                    "x3_T": turn("x3_T", ("norm_x3", x0)), "qkv": qkv, "qk_T": qk_T, "scores": scores,
                    "y_T": y_T, "yn_T": yn_T, "o": o, "x4_T": turn("x4_T", ("norm_x4", x1)), "f": f}):
                work(b)

        @block.scalar
        def _(act_eng):
            e = act_eng
            A = nc.scalar.activation

            def square_x0(b):
                e.wait_ge(x_loaded[b], 16)
                for t in range(NT):
                    if NT * b + t >= 2:
                        e.wait_ge(squares_ready, NT * b + t - 1)
                    A(square_out[:, t, :], x0[:, b, t, :], ACT.Square, accum_out=ssq[:, b, t:t + 1]).then_inc(squares_ready, 1)

            def turned(stage):
                def work(b):
                    wait_filled(e, stage, b)
                    A(xh[:, b], bank(stage, b)[:, :], ACT.Copy).then_inc(hi_ready, 1)
                return work

            def left_right(b):
                e.wait_ge(vec_loaded, 16)
                wait_filled(e, "left", b)
                for m in range(NC):
                    last = A(left[:, b, m, :], bank("left", b)[:, m * S:(m + 1) * S], ACT.Gelu, bias=v("left_b", m))
                drains(last, "left", b)
                wait_filled(e, "right", b)
                if b >= 2:
                    e.wait_ge(conv_ready, NC * (b - 1))
                for m in range(NC):
                    last = A(right[:, b % 2, m, 3:], bank("right", b)[:, m * S:(m + 1) * S], ACT.Identity, bias=v("right_b", m))
                drains(last, "right", b)

            def conv_split(b):
                e.wait_ge(conv_ready, NC * (b + 1))
                if b >= 2:
                    wait_filled(e, "gx", b - 2)
                A(ch[:, b % 2], conv[:, b], ACT.Copy).then_inc(conv_hi, 1)

            def gates(b):
                for name, dst in (("ga", r_gate), ("gx", i_gate)):
                    wait_filled(e, name, b)
                    for m in range(NC):
                        last = A(dst[:, b, m, :], bank(name, b)[:, m * S:(m + 1) * S], ACT.Sigmoid, bias=v(f"{name}_b", m))
                    drains(last, name, b)

            def decays(b):
                if b == 0:
                    e.wait_ge(softplus_d, 1)
                wait_drained(e, "ga", b)
                e.wait_ge(conv_lo, b + 1)
                e.wait_ge(gated_x, b + 1)
                for m in range(NC):
                    last = A(decay[:, b, m, :], r_gate[:, b, m, :], ACT.Exp, scale=decay_c[:, 0, m:m + 1])
                last.then_inc(decay_ready, 1)
                e.wait_ge(decay_ready, b + 1)
                for m in range(NC):
                    last = A(r_gate[:, b, m, :], r_gate[:, b, m, :], ACT.Tanh, scale=decay_c[:, 1, m:m + 1])
                last.then_inc(tanh_ready, 1)

            def scan(b):
                e.wait_ge(mult2_ready, b + 1)
                A(r_gate[:, b], r_gate[:, b], ACT.Sqrt).then_inc(mult_ready, 1)

            def out_split(b):
                e.wait_ge(lr_ready, b + 1)
                if b < 2:
                    wait_filled(e, "gx", b + 2)
                else:
                    wait_filled(e, "out", b - 2)
                A(ch[:, b % 2], left[:, b], ACT.Copy).then_inc(lr_hi, 1)

            def square_x1(b):
                wait_drained(e, "out", b)
                for t in range(NT):
                    e.wait_ge(squares_ready, NT * (B + b) + t - 1)
                    A(square_out[:, t, :], x1[:, b, t, :], ACT.Square, accum_out=ssq[:, b, t:t + 1]).then_inc(squares_ready, 1)

            def gated(b, j, name, n, func, biased, count):
                wait_filled(e, name, b, j)
                if n >= 3:
                    wait_drained(e, *hidden_key(n - 3))
                if biased:
                    for m in range(2):
                        last = A(act[:, n % 3, m, :], bank(name, b, j)[:, m * S:(m + 1) * S], func, bias=v("up1_b", 2 * j + m))
                else:
                    last = A(act[:, n % 3], bank(name, b, j)[:, :], func, scale=qc[:, 0:1])
                drains(last, name, b, j)
                wait_drained(e, *hidden_key(n))
                A(hh[b % 2][:, 2 * j:2 * j + 2, :], hid[:, n % 2], ACT.Copy).then_inc(hid_hi, 1)

            def mlp(b):
                if b >= 2:
                    wait_filled(e, "down", b - 2)
                if b < 2:
                    e.wait_ge(lr_lo, 2 * (b + 1))
                if b == 0:
                    e.wait_ge(mult2_ready, B)
                for j in range(F // 256):
                    gated(b, j, "up1", 3 * b + j, ACT.Gelu, True, None)

            def ffn(b):
                if b == 0:
                    e.wait_ge(scales_ready, 4)
                if b >= 2:
                    wait_filled(e, "ffn_down", b - 2)
                else:
                    wait_filled(e, "down", b + 2)
                for j in range(E // 256):
                    gated(b, j, "fup", 3 * B + 4 * b + j, ACT.Silu, False, None)

            def qkv(b):
                wait_filled(e, "v", b)
                e.wait_ge(vzero, 1)
                if b >= 2:
                    wait_filled(e, "y", b - 2, 1)
                for a in range(2):
                    part = slice(a * CH, (a + 1) * CH)
                    for t in range(NT):
                        last = A(vpad[part, b % 2, t].rearrange("p (h s) -> p h s", s=SLOT)[:, :, a * DH:(a + 1) * DH],
                                 bank("v", b)[part, t * D:(t + 1) * D].rearrange("p (h s) -> p h s", s=DH), ACT.Copy)
                drains(last, "v", b)
                wait_filled(e, "gate", b)
                drains(A(gate[:, b], bank("gate", b)[:, :], ACT.Silu), "gate", b)

            def qk_T(b):
                for t in range(NT):
                    wait_filled(e, "qk_T", b, t)
                    if b >= 2:
                        wait_filled(e, "y", b - 2, t)
                    drains(A(qkT[:, (NT * b + t) % 4], bank("qk_T", b, t)[:, :], ACT.Copy), "qk_T", b, t)

            def spread(b):
                if b == 0:
                    e.wait_ge(masks_loaded, 16)
                for t in range(NT):
                    i = NT * b + t
                    wait_drained(e, "qk_T", b, t)
                    if b >= 1:
                        wait_filled(e, "sc", b - 1, t, NC - 1)
                    for h in range(8, 12):
                        last = A(qz[i % 2][:, h, :], qkT[:, i % 4, 1, :], ACT.Copy, scale=head_rows[:, h - 8:h - 7])
                    last.then_inc(qz_ready_a, 1)

            def scores(b):
                for t in range(NT):
                    wait_filled(e, "y", b, t)
                    if b >= 1:
                        wait_filled(e, "y_T", b - 1)
                    drains(A(ys[:, (NT * b + t) % 2], bank("y", b, t)[:, 0:D], ACT.Copy), "y", b, t)

            def y_T(b):
                wait_filled(e, "y_T", b)
                if b >= 1:
                    e.wait_ge(ysum_ready, b)
                A(ysq[:, :, :], bank("y_T", b)[:, :], ACT.Square).then_inc(ysq_ready, 1)
                if b >= 2:
                    wait_filled(e, "yn_T", b - 2)
                drains(A(yn[:, NT * (b % 2):NT * (b % 2 + 1)], bank("y_T", b)[:, :], ACT.Copy), "y_T", b)

            def yn_T(b):
                wait_filled(e, "yn_T", b)
                if b >= 2:
                    e.wait_ge(y3_lo, b - 1)
                for c in range(NC):
                    last = A(y3[:, b % 2, c, :], bank("yn_T", b)[:, c * S:(c + 1) * S], ACT.Identity,
                             scale=v("gn_w", c), bias=v("gn_b", c))
                drains(last, "yn_T", b)
                e.wait_ge(y3_gated, b + 1)
                if b >= 2:
                    wait_filled(e, "o", b - 2)
                A(y3h[:, b % 2], y3[:, b % 2], ACT.Copy).then_inc(y3_hi, 1)

            e.wait_ge(vec_loaded, 16)
            A(sp[:, 0, :], v("a_param", 0, 2), ACT.Abs).then_inc(act_chain, 1)
            e.wait_ge(act_chain, 1)
            A(sp[:, 1, :], sp[:, 0, :], ACT.Exp, scale=-1.0).then_inc(act_chain, 1)
            e.wait_ge(act_chain, 2)
            A(sp[:, 2, :], sp[:, 1, :], ACT.Ln, bias=1.0).then_inc(softplus_a, 1)
            def prep_rg(j):
                raw = raw_wait(e, "rg")
                for k in range(NC):
                    src = raw[:, (2 * j + k) * D:(2 * j + k + 1) * D]
                    last = A(w_rg[0][:, j, k, :], src, ACT.Copy, scale=v("norm1_w", k)) if j < 2 else \
                        A(w_rg[0][:, j, k, :], src, ACT.Copy)
                last.then_inc(w_hi, 1)

            def prep_out(_):
                A(w_out[0][:, :, :], raw_wait(e, "out_down")[:, 0:2 * D], ACT.Copy).then_inc(w_hi, 1)

            def prep_down(_):
                A(w_dn[0][:, :, :], raw_wait(e, "out_down")[:, 2 * D:8 * D], ACT.Copy).then_inc(w_hi, 1)

            def prep_up(k):
                A(w_ups[0][:, k, :], raw_wait(e, f"up_k{k}")[:, 0:2 * F], ACT.Copy,
                  scale=v("norm2_w", k)).then_inc(w_hi, 1)

            def prep_qkvg(_):
                raw = raw_wait(e, "qkvg")
                e.wait_ge(centred, NC)
                wait_filled(e, "out", B - 1)
                A(w_qkvg[0][:, :, :], raw[:, :], ACT.Copy).then_inc(w_hi, 1)

            def absum(n):
                raw = raw_wait(e, TERNARY[n])
                for part in range(4 * n, 4 * n + 4):
                    if part >= 1:
                        e.wait_ge(absums_ready, part)
                    at = (part - 4 * n) * 512
                    A(abs_out[:, :], raw[:, at:at + 512], ACT.Abs,
                      accum_out=absums[:, part:part + 1]).then_inc(absums_ready, 1)

            for work, b in walk({
                    "square_x0": square_x0, "xn_T": turned("xn_T"), "left_right": left_right, "conv_split": conv_split,
                    "gates": gates, "decay": decays, "scan": scan, "lr_split": out_split,
                    "out": square_x1, "absum": absum, "prep_rg": prep_rg, "prep_out": prep_out, "prep_down": prep_down,
                    "prep_up": prep_up, "prep_qkvg": prep_qkvg,
                    "x1_T": turned("x1_T"), "mlp": mlp, "x2_T": turned("x2_T"), "ffn": ffn,
                    "x3_T": turned("x3_T"), "qkv": qkv, "qk_T": qk_T, "qz": spread, "scores": scores, "y_T": y_T,
                    "yn_T": yn_T, "x4_T": turned("x4_T")}):
                work(b)

        @block.vector
        def _(dve):
            e, V = dve, nc.vector
            TT, TS, STT = V.tensor_tensor, V.tensor_scalar, V.scalar_tensor_tensor

            def norm(stage, stat_stage, src, dst, mean):
                def work(b):
                    e.wait_ge(rs_ready, rs_count[stat_stage, b])
                    for t in range(NT):
                        if mean:
                            last = TS(dst[:, b, t, :], src[:, b, t, :], mv[:, b, t, 0:1], rs[:, b, t:t + 1],
                                      ALU.subtract, ALU.mult)
                        else:
                            last = TS(dst[:, b, t, :], src[:, b, t, :], rs[:, b, t:t + 1], None, ALU.mult)
                    last.then_inc(out_ready if stage == "final" else normed, 1)
                return work

            def turned(stage):
                def work(b):
                    e.wait_ge(hi_ready, hi_count[stage, b])
                    drains(TT(xl[:, b], bank(stage, b)[:, :].rearrange("p (c s) -> p c s", c=NC),
                              xh[:, b].bitcast(fp32), ALU.subtract), stage, b)
                return work

            def conv_work(b):
                wait_drained(e, "right", b)
                if b == 0:
                    e.wait_ge(pads_ready, 1)
                for k in range(4):
                    for m in range(NC):
                        dst, tap, w = conv[:, b, m, :], right[:, b % 2, m, k:k + S], v("conv_w", NC * k + m)
                        if k == 0:
                            TS(dst, tap, w, v("conv_b", m), ALU.mult, ALU.add).then_inc(conv_step, 1)
                        else:
                            e.wait_ge(conv_step, 3 * NC * b + NC * (k - 1) + m + 1)
                            STT(out=dst, in0=tap, scalar=w, in1=dst, op0=ALU.mult, op1=ALU.add)\
                                .then_inc(conv_step if k < 3 else conv_ready, 1)

            def conv_split(b):
                e.wait_ge(conv_hi, b + 1)
                TT(cl[:, b % 2], conv[:, b], ch[:, b % 2].bitcast(fp32), ALU.subtract).then_inc(conv_lo, 1)

            def decays(b):
                e.wait_ge(a2_ready, b + 1)
                e.wait_ge(tanh_ready, b + 1)
                STT(out=r_gate[:, b], in0=squared[:, :], scalar=1.0, in1=r_gate[:, b],
                    op0=ALU.add, op1=ALU.mult).then_inc(mult2_ready, 1)

            def scan(b):
                e.wait_ge(mult_ready, b + 1)
                e.wait_ge(gated_x, b + 1)
                TT(i_gate[:, b], i_gate[:, b], r_gate[:, b], ALU.mult).then_inc(scan_step, 1)
                e.wait_ge(scan_step, 3 * b + 1)
                for m in range(NC):
                    V.tensor_tensor_scan(r_gate[:, b, m, :], decay[:, b, m, :], i_gate[:, b, m, :], 0.0,
                                         ALU.mult, ALU.add).then_inc(scan_step, 1)
                e.wait_ge(scan_step, 3 * b + 3)
                TT(left[:, b], left[:, b], r_gate[:, b], ALU.mult).then_inc(lr_ready, 1)

            def lr_split(b):
                e.wait_ge(lr_hi, b + 1)
                TT(cl[:, b % 2], left[:, b], ch[:, b % 2].bitcast(fp32), ALU.subtract).then_inc(lr_lo, 1)

            def out(b):
                wait_filled(e, "out", b)
                e.wait_ge(xo_ready, b + 1)
                drains(TT(x1[:, b], bank("out", b)[:, :].rearrange("p (t d) -> p t d", t=NT), x0o[:, b], ALU.add),
                       "out", b)

            def hidden_lo(b, j, n):
                e.wait_ge(hid_hi, n + 1)
                TT(hl[b % 2][:, 2 * j:2 * j + 2, :], hid[:, n % 2], hh[b % 2][:, 2 * j:2 * j + 2, :].bitcast(fp32),
                   ALU.subtract).then_inc(hid_lo, 1)

            def mlp(b):
                for j in range(F // 256):
                    n = 3 * b + j
                    wait_filled(e, "up2", b, j)
                    wait_drained(e, "up1", b, j)
                    if n >= 2:
                        e.wait_ge(hid_lo, n - 1)
                    for m in range(2):
                        last = STT(out=hid[:, n % 2, m, :], in0=bank("up2", b, j)[:, m * S:(m + 1) * S],
                                   scalar=v("up2_b", 2 * j + m), in1=act[:, n % 3, m, :], op0=ALU.add, op1=ALU.mult)
                    drains(last, "up2", b, j)
                    if j >= 1:
                        hidden_lo(b, j - 1, n - 1)
                hidden_lo(b, j, n)

            def ffn(b):
                for j in range(E // 256):
                    n = 3 * B + 4 * b + j
                    wait_filled(e, "fgate", b, j)
                    wait_drained(e, "fup", b, j)
                    e.wait_ge(hid_lo, n - 1)
                    drains(TT(hid[:, n % 2], bank("fgate", b, j)[:, :].rearrange("p (c s) -> p c s", c=2), act[:, n % 3],
                              ALU.mult), "fgate", b, j)
                    if j >= 1:
                        hidden_lo(b, j - 1, n - 1)
                hidden_lo(b, j, n)

            def close(stage, dst, resid, ready, scaled):
                def work(b):
                    wait_filled(e, stage, b)
                    if ready is not None:
                        e.wait_ge(ready, b + 1)
                    z = bank(stage, b)[:, :].rearrange("p (t d) -> p t d", t=NT)
                    if scaled:
                        last = STT(out=dst[:, b], in0=z, scalar=qc[:, 1:2], in1=resid[:, b], op0=ALU.mult, op1=ALU.add)
                    else:
                        last = TT(dst[:, b], z, resid[:, b], ALU.add)
                    drains(last, stage, b)
                    wait_drained(e, stage, b)
                    n = ln_count[stage, b]
                    for t in range(NT):
                        V.bn_stats(stats[:, b, t, :], dst[:, b, t, :]).then_inc(stats_ready, 1)
                    e.wait_ge(stats_ready, NT * n)
                    for t in range(NT):
                        last = V.bn_aggr(mv[:, b, t, :], stats[:, b, t, :])
                    last.then_inc(var_ready, 1)
                return work

            def qkv(b):
                for t in range(NT):
                    i = NT * b + t
                    wait_filled(e, "qk", b, t)
                    if i == 0:
                        e.wait_ge(tables_loaded, 16)
                    if b >= 2 and t == 0:
                        wait_filled(e, "kv", b - 2, 1)
                    if i >= 2:
                        e.wait_ge(qk_ready, i - 1)
                    TT(qk[:, i % 4, :], bank("qk", b, t)[:, :], rope[:, 0, t, :], ALU.mult).then_inc(cos_done, 1)
                    pairs = lambda ap: ap.rearrange("p (n two) -> p n two", two=2)
                    drains(TT(pairs(qk_sin[:, i % 2, :]), pairs(bank("qk", b, t)[:, :])[:, :, ::-1],
                              pairs(rope[:, 1, t, :]), ALU.mult), "qk", b, t)

            def kv(b):
                if b == 0:
                    e.wait_ge(vzero, 1)
                for t in range(NT):
                    wait_filled(e, "kv", b, t)
                    if b >= 1:
                        wait_filled(e, "y", b - 1, 1)
                    kv_t = slots(bank("kv", b, t))
                    last = TT(slots(state_b[:, t])[:, :, :, 1, :], kv_t[:, :, :, 0, :], own_head, ALU.mult)
                    if t == 0:
                        last.then_inc(state_part, 1)
                        last = TT(slots(state_a)[:, :, :, 0, :], kv_t[:, :, :, 1, :], own_head, ALU.mult)
                    drains(last, "kv", b, t)

            def spread(b):
                for t in range(NT):
                    i = NT * b + t
                    wait_drained(e, "qk_T", b, t)
                    if b >= 1:
                        wait_filled(e, "sc", b - 1, t, NC - 1)
                    TT(qz[i % 2][:, 0:8, :], qkT[:, i % 4, 0, :][:, None, :].to_broadcast([P, 8, P]),
                       head_rows[:, :, None].to_broadcast([P, 8, P]), ALU.mult).then_inc(qz_ready, 1)

            def scores(b):
                for t in range(NT):
                    for c in range(NC):
                        wait_filled(e, "sc", b, t, c)
                        if b > 0:
                            wait_filled(e, "y", b - 1, t)
                        drains(TT(probs[:, 2 * t + c, :].rearrange("p (j s) -> p j s", s=CH),
                                  bank("sc", b, t, c)[:, :].rearrange("p (j s) -> p j s", s=CH),
                                  causal[:, None, :].to_broadcast([P, 8, CH]), ALU.mult), "sc", b, t, c)

            def y_T(b):
                e.wait_ge(ysq_ready, b + 1)
                V.tensor_reduce(ysum[:, b], ysq[:, :, :].rearrange("p t (h s) -> p t h s", s=DH), AX.X,
                                ALU.add).then_inc(ysum_ready, 1)

            def yn_work(b):
                e.wait_ge(yrs_ready, b + 1)
                wait_drained(e, "y_T", b)
                y = yn[:, NT * (b % 2):NT * (b % 2 + 1)].rearrange("p t (h s) -> p (t h) s", s=DH)
                TT(y, y, yrs[:, b].rearrange("p t h -> p (t h)")[:, :, None].to_broadcast([P, NT * H, DH]),
                   ALU.mult).then_inc(yn_ready, 1)

            def yn_T(b):
                wait_drained(e, "yn_T", b)
                wait_drained(e, "gate", b)
                TT(y3[:, b % 2], y3[:, b % 2], gate[:, b], ALU.mult).then_inc(y3_gated, 1)
                e.wait_ge(y3_hi, b + 1)
                TT(y3l[:, b % 2], y3[:, b % 2], y3h[:, b % 2].bitcast(fp32), ALU.subtract).then_inc(y3_lo, 1)

            def prep_rg(j):
                e.wait_ge(w_hi, weight_count["prep_rg", j])
                for k in range(NC):
                    src = staging[LOAD["rg"] % 2][:, (2 * j + k) * D:(2 * j + k + 1) * D]
                    hi = w_rg[0][:, j, k, :].bitcast(fp32)
                    last = STT(out=w_rg[1][:, j, k, :], in0=src, scalar=v("norm1_w", k), in1=hi,
                               op0=ALU.mult, op1=ALU.subtract) if j < 2 else \
                        TT(w_rg[1][:, j, k, :], src, hi, ALU.subtract)
                last.then_inc(w_lo, 1)

            def lo_half(stage, w, load, lo, hi):
                e.wait_ge(w_hi, weight_count[stage, 0])
                TT(w[1][:, :, :], staging[LOAD[load] % 2][:, lo:hi].rearrange("p (k n) -> p k n", k=w[0].shape[1]),
                   w[0][:, :, :].bitcast(fp32), ALU.subtract).then_inc(w_lo, 1)

            def prep_out(_):
                lo_half("prep_out", w_out, "out_down", 0, 2 * D)

            def prep_down(_):
                lo_half("prep_down", w_dn, "out_down", 2 * D, 8 * D)

            def prep_up(k):
                e.wait_ge(w_hi, weight_count["prep_up", k])
                STT(out=w_ups[1][:, k, :], in0=staging[LOAD[f"up_k{k}"] % 2][:, 0:2 * F], scalar=v("norm2_w", k),
                    in1=w_ups[0][:, k, :].bitcast(fp32), op0=ALU.mult, op1=ALU.subtract).then_inc(w_lo, 1)

            def quant(n):
                wait_filled(e, "absum", n)
                drains(V.tensor_reduce(qs[:, n:n + 1], bank("absum", n)[:, 0:4], AX.X, ALU.add), "absum", n)
                wait_drained(e, "absum", n)
                TS(qs[:, n:n + 1], qs[:, n:n + 1], 1.0 / (D * E), EPS_Q, ALU.mult, ALU.add).then_inc(quant_step, 1)
                e.wait_ge(quant_step, n + 1)
                TS(qt[:, 1, n:n + 1], qs[:, n:n + 1], -0.5, None, ALU.mult)
                TS(qt[:, 0, n:n + 1], qs[:, n:n + 1], 0.5, None, ALU.mult).then_inc(scales_ready, 1)
                if n == 2:
                    TS(qc[:, 0:1], qs[:, 1:2], -1.0, None, ALU.mult)
                    TT(qc[:, 1:2], qs[:, 0:1], qs[:, 2:3], ALU.mult).then_inc(scales_ready, 1)

            def ternary(n):
                dst = (q_down, q_up, q_gate)[n]
                e.wait_ge(scales_ready, n + 1)
                raw = (raw_ffn_down if n == 0 else staging[LOAD[TERNARY[n]] % 2])[:, :].rearrange(
                    "p (k n) -> p k n", k=dst.shape[1])
                TS(dst[:, :, :], raw, qt[:, 0, n:n + 1], None, ALU.is_gt).then_inc(above_ready, 1)
                e.wait_ge(above_ready, n + 1)
                STT(out=dst[:, :, :], in0=raw, scalar=qt[:, 1, n:n + 1], in1=dst[:, :, :].bitcast(fp32),
                    op0=ALU.is_lt, op1=ALU.subtract).then_inc(ternary_ready, 1)

            def centre(_):
                raw = raw_wait(e, "qkvg")
                for k in range(NC):
                    part = raw[:, k * 4 * D + 2 * D:k * 4 * D + 3 * D].rearrange("p (h s) -> p h s", s=DH)
                    V.tensor_reduce(vmean[:, k, :], part, AX.X, ALU.add).then_inc(vmean_ready, 1)
                for k in range(NC):
                    part = raw[:, k * 4 * D + 2 * D:k * 4 * D + 3 * D].rearrange("p (h s) -> p h s", s=DH)
                    e.wait_ge(vmean_ready, k + 1)
                    STT(out=part, in0=vmean[:, k, :][:, :, None].to_broadcast([P, H, DH]), scalar=-1.0 / DH, in1=part,
                        op0=ALU.mult, op1=ALU.add).then_inc(centred, 1)

            def lo_qkvg(_):
                lo_half("prep_qkvg", w_qkvg, "qkvg", 0, 4 * 2 * D)

            V.memset(right[:, :, :, 0:3], 0.0).then_inc(pads_ready, 1)
            e.wait_ge(softplus_a, 1)
            chain = [0]

            def link(instruction):
                chain[0] += 1
                instruction.then_inc(softplus_step, 1)
                e.wait_ge(softplus_step, chain[0])

            link(TS(sp[:, 3, :], sp[:, 1, :], 1.0, -1.0, ALU.add, ALU.add))
            link(TS(sp[:, 4, :], sp[:, 3, :], 0.0, None, ALU.is_equal))
            link(TT(sp[:, 5, :], sp[:, 3, :], sp[:, 4, :], ALU.add))
            link(V.reciprocal(sp[:, 6, :], sp[:, 5, :]))
            link(TT(sp[:, 6, :], sp[:, 6, :], sp[:, 2, :], ALU.mult))
            link(TT(sp[:, 6, :], sp[:, 6, :], sp[:, 4, :], ALU.add))
            link(TT(sp[:, 6, :], sp[:, 6, :], sp[:, 1, :], ALU.mult))
            link(STT(out=sp[:, 7, :], in0=v("a_param", 0, 2), scalar=0.0, in1=sp[:, 6, :], op0=ALU.max, op1=ALU.add))
            link(TS(decay_c[:, 0, :], sp[:, 7, :], -C_RGLRU, None, ALU.mult))
            TS(decay_c[:, 1, :], sp[:, 7, :], C_RGLRU, None, ALU.mult).then_inc(softplus_d, 1)

            for work, b in walk({
                    "norm_x0": norm("norm_x0", "square_x0", x0, x1, False), "xn_T": turned("xn_T"), "conv": conv_work, "conv_split": conv_split,
                    "decay": decays, "scan": scan, "lr_split": lr_split, "out": out,
                    "norm_x1": norm("norm_x1", "out", x1, x0o, False), "x1_T": turned("x1_T"), "mlp": mlp,
                    "down": close("down", x0o, x0, xs_ready, False),
                    "norm_x2": norm("norm_x2", "down", x0o, x0o, True), "x2_T": turned("x2_T"), "ffn": ffn,
                    "ffn_down": close("ffn_down", x0, x0o, None, True),
                    "norm_x3": norm("norm_x3", "ffn_down", x0, x0, True), "x3_T": turned("x3_T"), "qkv": qkv,
                    "qk_T": kv, "qz": spread, "scores": scores, "y_T": y_T, "yn": yn_work, "yn_T": yn_T,
                    "o": close("o", x1, x0, None, False),
                    "norm_x4": norm("norm_x4", "o", x1, x1, True), "x4_T": turned("x4_T"),
                    "f": close("f", x0o, x0, x4b_ready, False),
                    "final": norm("final", "f", x0o, x0o, True),
                    "prep_rg": prep_rg, "prep_out": prep_out, "prep_down": prep_down, "prep_up": prep_up, "quant": quant,
                    "ternary": ternary, "centre": centre, "lo_qkvg": lo_qkvg}):
                work(b)

        @block.gpsimd
        def _(pool):
            e, G = pool, nc.gpsimd

            def spread_row(n):
                return rows[:, n, :][:, None, :].to_broadcast([P, NT, D])

            def root(stage, src, scale, eps):
                def work(b):
                    if stage == "square_x0":
                        e.wait_ge(squares_ready, NT * (b + 1))
                    elif stage == "out":
                        e.wait_ge(squares_ready, NT * (B + b + 1))
                    else:
                        e.wait_ge(var_ready, ln_count[stage, b])
                    n = rs_count[stage, b]
                    G.tensor_scalar(rse[:, b, :], src(b), scale, eps, ALU.mult, ALU.add).then_inc(rse_ready, 1)
                    e.wait_ge(rse_ready, n)
                    G.tensor_tensor(rs[:, b, :], rse[:, b, :], neg_half[:, 0:NT], ALU.pow).then_inc(rs_ready, 1)
                return work

            def ssq_of(b):
                return ssq[:, b, :]

            def var_of(b):
                return mv[:, b, :, 1]

            def add_out_b(b):
                if b == 0:
                    e.wait_ge(rows_loaded, 16)
                e.wait_ge(x_loaded[b], 16)
                G.tensor_tensor(x0o[:, b], x0[:, b], spread_row(0), ALU.add).then_inc(xo_ready, 1)

            def gate_x(b):
                wait_drained(e, "gx", b)
                e.wait_ge(conv_ready, NC * (b + 1))
                G.tensor_tensor(i_gate[:, b], i_gate[:, b], conv[:, b], ALU.mult).then_inc(gated_x, 1)

            def square_decay(b):
                e.wait_ge(decay_ready, b + 1)
                if b >= 1:
                    e.wait_ge(mult2_ready, b)
                G.tensor_tensor(squared[:, :], decay[:, b], decay[:, b], ALU.mult).then_inc(a2_ready, 1)

            def residual(b):
                e.wait_ge(normed, normed_count["norm_x0", b])
                e.wait_ge(xo_ready, b + 1)
                G.tensor_tensor(x0[:, b], x0[:, b], spread_row(1), ALU.add).then_inc(xs_part, 1)
                e.wait_ge(xs_part, b + 1)
                wait_drained(e, "out", b)
                G.tensor_tensor(x0[:, b], x0[:, b], x1[:, b], ALU.add).then_inc(xs_ready, 1)

            def add_ffn_bias(b):
                e.wait_ge(normed, normed_count["norm_x4", b])
                G.tensor_tensor(x0[:, b], x1[:, b], spread_row(2), ALU.add).then_inc(x4b_ready, 1)

            def qkv(b):
                for t in range(NT):
                    i = NT * b + t
                    wait_drained(e, "qk", b, t)
                    G.tensor_tensor(qk[:, i % 4, :], qk[:, i % 4, :], qk_sin[:, i % 2, :], ALU.add).then_inc(qk_ready, 1)

            def clear_values(b):
                if b == 0:
                    wait_filled(e, "down", B - 1)
                    wait_filled(e, "ffn_down", B - 1)
                    G.memset(vpad[:, :, :, :], 0.0)
                    G.memset(state_b[:, :, :, :], 0.0)
                    G.memset(state_a[:, :, :], 0.0).then_inc(vzero, 1)

            def kv(b):
                wait_drained(e, "kv", b, 0)
                e.wait_ge(state_part, b + 1)
                a, b0, b1 = (slots(x)[:, :, :, n, :] for x, n in ((state_a, 0), (state_b[:, 0], 1), (state_b[:, 1], 1)))
                G.tensor_tensor(a, a, b0, ALU.add).then_inc(state_ready, 1)
                wait_drained(e, "kv", b, 1)
                e.wait_ge(state_ready, 2 * b + 1)
                G.tensor_tensor(b1, b1, a, ALU.add).then_inc(state_ready, 1)

            def spread(b):
                if b == 0:
                    e.wait_ge(masks_loaded, 16)
                for t in range(NT):
                    i = NT * b + t
                    wait_drained(e, "qk_T", b, t)
                    if b >= 1:
                        wait_filled(e, "sc", b - 1, t, NC - 1)
                    G.tensor_tensor(qz[i % 2][:, 12:H, :], qkT[:, i % 4, 1, :][:, None, :].to_broadcast([P, 4, P]),
                                    head_rows[:, 4:8, None].to_broadcast([P, 4, P]), ALU.mult).then_inc(qz_ready_p, 1)

            def y_T(b):
                e.wait_ge(ysum_ready, b + 1)
                if b >= 1:
                    e.wait_ge(yrs_ready, b)
                G.tensor_scalar(yse[:, :], ysum[:, b], 1.0 / DH, EPS_LN, ALU.mult, ALU.add).then_inc(yse_ready, 1)
                e.wait_ge(yse_ready, b + 1)
                G.tensor_tensor(yrs[:, b], yse[:, :], neg_half[:, :], ALU.pow).then_inc(yrs_ready, 1)

            def split_weights(hi, lo, src):
                G.tensor_scalar(hi, src, 1.0, None, ALU.mult).then_inc(pool_hi, 1)
                pool_his[0] += 1
                e.wait_ge(pool_hi, pool_his[0])
                return G.tensor_tensor(lo, src, hi.bitcast(fp32), ALU.subtract)

            pool_his = [0]

            def prep_f(half):
                raw = raw_wait(e, f"factors{half}")
                if half == 0:
                    wait_filled(e, "out", B - 1)
                for r in range(4):
                    n = 4 * half + r
                    if n == 0:
                        G.tensor_scalar(fsum[:, :], raw[:, 0:512], 1.0, None, ALU.mult).then_inc(fsum_step, 1)
                    else:
                        e.wait_ge(fsum_step, n)
                        G.tensor_tensor(fsum[:, :], fsum[:, :], raw[:, r * 512:(r + 1) * 512], ALU.add).then_inc(fsum_step, 1)
                if half == 1:
                    e.wait_ge(fsum_step, RANK)
                    G.tensor_scalar(fsum[:, :], fsum[:, :], float(RANK) ** -0.5, None, ALU.mult).then_inc(fsum_step, 1)
                    e.wait_ge(fsum_step, RANK + 1)
                    split_weights(w_f[0][:, :, :], w_f[1][:, :, :],
                                  fsum[:, :].rearrange("p (k n) -> p k n", k=NC)).then_inc(w_ready_p, 1)

            def prep_o(_):
                raw = raw_wait(e, "o")
                wait_filled(e, "out", B - 1)
                split_weights(w_o[0][:, :, :], w_o[1][:, :, :],
                              raw[:, 0:2 * D].rearrange("p (k n) -> p k n", k=NC)).then_inc(w_ready_p, 1)

            G.memset(neg_half[:, :], -0.5).then_inc(half_ready, 1)
            e.wait_ge(half_ready, 1)
            for work, b in walk({
                    "square_x0": root("square_x0", ssq_of, 1.0 / D, EPS_RMS), "add_out_b": add_out_b, "gates": gate_x,
                    "decay": square_decay, "out": root("out", ssq_of, 1.0 / D, EPS_RMS), "residual": residual,
                    "down": root("down", var_of, 1.0, EPS_LN), "ffn_down": root("ffn_down", var_of, 1.0, EPS_LN),
                    "clear": clear_values, "qkv": qkv, "qk_T": kv, "qz": spread, "y_T": y_T, "o": root("o", var_of, 1.0, EPS_LN),
                    "norm_x4": add_ffn_bias, "f": root("f", var_of, 1.0, EPS_LN),
                    "prep_f": prep_f, "prep_o": prep_o}):
                work(b)


def tables():
    n = np.arange(S, dtype=np.float64)[:, None]
    half = DH // 2
    xscale = (np.arange(0, DH, 2, dtype=np.float64) + 0.4 * DH) / (1.4 * DH)
    scale = xscale[None, :] ** (n / 64.0)
    angle = n * (1.0 / 10000.0 ** (np.arange(half, dtype=np.float64) / half))[None, :]
    gamma = 1.0 - np.exp(np.linspace(np.log(1.0 / 32), np.log(1.0 / 64), H))
    sign = np.tile([-1.0, 1.0], half)
    table = np.zeros((2, S, 2, H, DH))
    for part, (s, g) in enumerate(((scale, gamma[None, :] ** n), (1.0 / scale, gamma[None, :] ** -n))):
        for which, wave in enumerate((np.cos(angle), np.sin(angle))):
            row = np.repeat(wave * s, 2, axis=1) * (sign if which else 1.0)
            table[which, :, part] = g[:, :, None] * row[:, None, :]
    rope = table.reshape(2, NT, P, 2 * D).transpose(2, 0, 1, 3).reshape(P, -1)
    p = np.arange(P)
    q = np.arange(CH)
    causal = q[None, :] >= p[:, None] % CH
    pick = [(p[:, None] // SLOT == q[None, :] // DH) & (p[:, None] % SLOT == a * DH + q[None, :] % DH) for a in range(2)]
    head_rows = p[:, None] // DH == np.arange(8)[None, :]
    early = np.concatenate([np.eye(P), np.ones((P, P))], axis=1)
    return early.astype(np.float32), np.concatenate([rope, causal, *pick, head_rows], axis=1).astype(np.float32)


def kernel(**inputs):
    import concourse.bacc as bacc
    from concourse.bass_utils import run_bass_kernel_spmd as run

    a = {k: np.asarray(x) for k, x in inputs.items()}

    def by_chunk(w):
        return w.reshape(-1, P, w.shape[1]).transpose(1, 0, 2).reshape(P, -1)

    def columns(x):
        return x.reshape(-1, P).T

    def heads(w):
        return w.transpose(1, 0, 2).reshape(D, D)

    vec = np.concatenate([columns(x) for x in (
        a["L0_attn_norm1_w"], a["L0_attn_left_b"], a["L0_attn_right_b"], a["L0_attn_conv_w"].reshape(-1),
        a["L0_attn_conv_b"], a["L0_attn_ga_b"], a["L0_attn_gx_b"], a["L0_attn_a_param"], a["L0_attn_norm2_w"],
        a["L0_attn_up1_b"], a["L0_attn_up2_b"], a["L1_attn_gn_weight"], a["L1_attn_gn_bias"])], axis=1)
    row = np.broadcast_to(np.stack([a["L0_attn_out_b"], a["L0_attn_down_b"], a["L1_ffn_bias"]]), (P, 3, D))
    ups = np.concatenate([a["L0_attn_up1_W"], a["L0_attn_up2_W"]], axis=1)
    qkvg = np.concatenate([heads(a["L1_attn_W_Q"]), heads(a["L1_attn_W_K"]), heads(a["L1_attn_W_V"]),
                           a["L1_attn_W_G"]], axis=1)
    factors = [by_chunk(f) for f in a["L1_ffn_factors"]]
    weights = np.concatenate(
        [by_chunk(a[f"L0_attn_{n}_W"]) for n in ("left", "right", "ga", "gx", "out", "down")]
        + [ups[0:P], ups[P:2 * P], by_chunk(a["L0_ffn_W_up"].T), by_chunk(a["L0_ffn_W_gate"].T),
           by_chunk(qkvg)] + factors + [by_chunk(a["L1_attn_W_O"]), by_chunk(a["L0_ffn_W_down"].T)], axis=1)
    early, table = tables()
    arrays = {
        "x": a["L0_attn_x"].reshape(B, NT, P, D).transpose(2, 0, 1, 3),
        "vectors": vec, "rows": row, "early": early, "tables": table, "weights": weights,
    }
    arrays = {k: np.ascontiguousarray(x) for k, x in arrays.items()}
    assert arrays["weights"].shape[1] == N_WEIGHTS and vec.shape[1] == N_VECTORS
    nc = bacc.Bacc("TRN2", target_bir_lowering=False, num_devices=1)
    args = [nc.dram_tensor(k, x.shape, mybir.dt.float32, kind="ExternalInput").ap() for k, x in arrays.items()]
    out = nc.dram_tensor("out", (P, B, NT, D), mybir.dt.float32, kind="ExternalOutput").ap()
    build(nc, *args, out)
    got = run(nc, [arrays], core_ids=[0]).results[0]["out"]
    return np.ascontiguousarray(got.transpose(1, 2, 0, 3).reshape(B, S, D))
```

```python
import numpy as np
import concourse.bass as bass
from concourse import mybir
from contextlib import ExitStack

B, S, D = 4, 256, 256
P = 128
NT, NC = S // P, D // P
F, E = 768, 1024
H, DH = 16, 16
CH = 64
SLOT = 2 * DH
QUADS = H // 4
RANK = 8
BANKS = 8
EPS_RMS, EPS_Q, EPS_LN = 1e-8, 1e-8, 1e-5
C_RGLRU = 8.0

VECTORS, _at = {}, 0
for _name, _n in (("norm1_w", 2), ("left_b", 2), ("right_b", 2), ("conv_w", 8), ("conv_b", 2),
                  ("ga_b", 2), ("gx_b", 2), ("a_param", 2), ("norm2_w", 2), ("up1_b", 6),
                  ("up2_b", 6), ("gn_w", 2), ("gn_b", 2)):
    VECTORS[_name] = _at
    _at += _n
N_VECTORS = _at

PLACED, STAGED, _at = {}, [], 0
for _name, _n in (("left_right", 4 * D), ("gates", 4 * D), ("out", 2 * D), ("o", 2 * D), ("ffn_down", 2 * E)):
    PLACED[_name] = (_at, _n)
    _at += _n
for _name, _n in (("down", 6 * D), ("up_k0", 2 * F), ("up_k1", 2 * F), ("ffn_up", 2 * E), ("ffn_gate", 2 * E),
                  ("qkvg", 2 * 4 * D), ("factors0", 8 * D), ("factors1", 8 * D)):
    STAGED.append((_name, _at, _n))
    _at += _n
N_WEIGHTS = _at
LOAD = {name: n for n, (name, _, _) in enumerate(STAGED)}
TERNARY = ("ffn_down", "ffn_up", "ffn_gate")

ORDER = """
    square_x0/0 square_x0/1 xn_T/0 norm_x0/0 prep_lr/0 norm_x0/1 norm_x0/2 softplus/0 square_x0/2 xn_T/1
    square_x0/3 prep_down/0 norm_x0/3 left_right/0 add_out_b/0 conv/0 xn_T/2 left_right/1 xn_T/3 prep_up/0
    absum/0 left_right/2 conv/1 add_out_b/1 conv/2 left_right/3 prep_up/1 conv/3 gates/0 absum/1 gates/1
    quant/0 gates/2 ternary/0 gates/3 quant/1 ternary/1 decay/0 add_out_b/2 decay/1 decay/2 scan/0 scan/1
    decay/3 residual/0 scan/2 out/0 add_out_b/3 scan/3 norm_x1/0 absum/2 out/1 out/2 centre/0 norm_x1/1
    x1_T/0 norm_x1/2 out/3 quant/2 x1_T/1 prep_qkvg/0 lo_qkvg/0 mlp/0 residual/1 norm_x1/3 x1_T/2 mlp/1
    residual/2 down/0 x1_T/3 ternary/2 norm_x2/0 mlp/2 down/1 residual/3 x2_T/0 norm_x2/1 mlp/3 down/2
    x2_T/1 ffn/0 down/3 norm_x2/2 ffn/1 norm_x2/3 prep_f/0 x2_T/2 ffn_down/0 x2_T/3 ffn/2 norm_x3/0
    ffn_down/1 ffn/3 x3_T/0 ffn_down/2 norm_x3/1 norm_x3/2 clear/0 ffn_down/3 x3_T/1 qkv/0 x3_T/2 norm_x3/3
    qk_T/0 qz/0 qkv/1 scores/0 y_T/0 qk_T/1 qz/1 qkv/2 scores/1 prep_f/1 x3_T/3 qk_T/2 qz/2 yn/0 qkv/3
    y_T/1 yn_T/0 scores/2 qk_T/3 yn/1 qz/3 y_T/2 o/0 yn_T/1 yn/2 scores/3 norm_x4/0 yn_T/2 y_T/3 o/1 yn/3
    norm_x4/1 o/2 x4_T/0 yn_T/3 x4_T/1 f/0 norm_x4/2 o/3 f/1 norm_x4/3 final/0 final/1 x4_T/2 f/2 x4_T/3
    f/3 final/2 final/3
"""
MLP_SLOTS, FFN_SLOTS = (0, 1, 0, 1), (0, 1, 0, 1)


def walk(work):
    for item in ORDER.split():
        stage, n = item.split("/")
        if stage in work:
            yield work[stage], int(n)


GROUPS = {
    "xn_T": [("xn_T",)], "left_right": [("left",), ("right",)], "gates": [("ga",), ("gx",)],
    "out": [("out",)], "x1_T": [("x1_T",)],
    "mlp": [(k, j) for j in range(F // 256) for k in ("up1", "up2")],
    "down": [("down",)], "x2_T": [("x2_T",)],
    "ffn": [(k, j) for j in range(E // 256) for k in ("fup", "fgate")],
    "ffn_down": [("ffn_down",)], "x3_T": [("x3_T",)],
    "qkv": [("qk", 0), ("qk", 1), ("v",), ("gate",)],
    "qk_T": [("qk_T", 0), ("qk_T", 1), ("kv", 0), ("kv", 1)],
    "scores": [("sc", t, c) for t in range(NT) for c in range(NC)] + [("y", 0), ("y", 1)],
    "y_T": [("y_T",)], "yn_T": [("yn_T",)], "o": [("o",)], "x4_T": [("x4_T",)],
    "f": [("f",)], "quant": [("absum",)],
}


def number_groups():
    order = []
    for (stage, b) in walk({s: s for s in GROUPS}):
        order += [(key[0], b, *key[1:]) for key in GROUPS[stage]]
    return {key: n for n, key in enumerate(order)}


def build(nc, x_dram, vec_dram, row_dram, early_dram, table_dram, w_dram, out_dram):
    fp32, fp32r = mybir.dt.float32, mybir.dt.float32r
    ALU, ACT, AX = mybir.AluOpType, mybir.ActivationFunctionType, mybir.AxisListType
    number = number_groups()

    ctx = ExitStack()
    with ctx:
        def sb(name, shape, dt=fp32, scope=None):
            return (scope or ctx).enter_context(nc.sbuf_tensor(name, shape, dt))

        def sem(name):
            return ctx.enter_context(nc.semaphore(name))

        x0 = sb("x0", [P, B, NT, D])
        x0o = sb("x0o", [P, B, NT, D])
        x1 = sb("x1", [P, B, NT, D])
        xh = sb("xh", [P, B, NC, S], fp32r)
        xl = sb("xl", [P, B, NC, S], fp32r)
        staging = [sb(f"staging{i}", [P, 2048]) for i in range(2)]
        q_up = sb("q_up", [P, NC, E], fp32r)
        q_gate = sb("q_gate", [P, NC, E], fp32r)
        q_down = sb("q_down", [P, E // P, D], fp32r)
        with ExitStack() as r0:
            mlp_act = sb("mlp_act", [P, 3, 2, S], fp32, r0)
        rope = sb("rope", [P, 2, NT, 2 * D])
        early = sb("consts", [P, 2 * P])
        ident, ones = early[:, 0:P], early[:, P:2 * P]
        masks = sb("masks", [P, 3 * CH + 8])
        causal, head_rows = masks[:, 0:CH], masks[:, 3 * CH:3 * CH + 8]
        pick = [masks[:, (1 + a) * CH:(2 + a) * CH] for a in range(2)]
        rows = sb("row_vectors", [P, 3, D])
        vec = sb("vec", [P, N_VECTORS])
        stats = sb("stats", [P, B, NT, 6])
        mv = sb("mv", [P, B, NT, 2])
        ssq = sb("ssq", [P, B, NT])
        rs = sb("rs", [P, B, NT])
        rse = sb("rse", [P, B, NT])
        neg_half = sb("neg_half", [P, NT])
        sp = sb("sp", [P, 9, 2])
        decay_c = sb("decay_c", [P, 2, 2])
        absums = sb("absums", [P, 12])
        qs = sb("qs", [P, 3])
        qt = sb("qt", [P, 2, 3])
        qc = sb("qc", [P, 2])
        vmean = sb("vmean", [P, NC, H])
        ysum = sb("ysum", [P, B, NT, H])
        yrs = sb("yrs", [P, B, NT, H])
        square_out = sb("square_out", [P, 2, 256], mybir.dt.bfloat16)
        abs_out = sb("abs_out", [P, 512], mybir.dt.bfloat16)

        with ExitStack() as r1:
            w_ups = [sb(f"w_ups_{k}", [P, NC, 2 * F], fp32r, r1) for k in ("hi", "lo")]
            w_dn = [sb(f"w_down_{k}", [P, F // P, D], fp32r, r1) for k in ("hi", "lo")]
        r1 = ctx.enter_context(ExitStack())
        qz = [sb(f"qz{i}", [P, H, P], fp32, r1) for i in range(2)]
        vpad = sb("vpad", [P, 2, NT, H * SLOT], fp32, r1)
        probs = sb("probs", [P, 4, 8 * CH], fp32, r1)
        state_b = sb("state_b", [P, 2, NC, 8 * SLOT], fp32, r1)

        with ExitStack() as r2:
            lru = sb("lru", [P, B, 4, NC, S], fp32, r2)
            right = sb("right", [P, 2, NC, S + 3], fp32, r2)
            squared = sb("squared", [P, NC, S], fp32, r2)
            hid = sb("hid", [P, 2, 2, S], fp32, r2)
            x0T = sb("x0T", [P, B, NC, S], fp32, r2)
        left, r_gate, i_gate, decay = (lru[:, :, n, :, :] for n in range(4))
        conv = decay
        with ExitStack() as r2:
            hidden = [[sb(f"hidden{i}_{k}", [P, E // P, S], fp32r, r2) for k in ("hi", "lo")] for i in range(2)]
            ffn_act = sb("ffn_act", [P, 3, 2, S], fp32, r2)
            sb("pad_mlp", [P, 12 + 2 * 2 * S], fp32, r2)
        hh, hl = ([hidden[i][k] for i in range(2)] for k in range(2))
        r2 = ctx.enter_context(ExitStack())
        qk = sb("qk", [P, 4, 2 * D], fp32, r2)
        qk_sin = sb("qk_sin", [P, 2, 2 * D], fp32, r2)
        qkT = sb("qkT", [P, 4, 4, P], fp32, r2)
        ys = sb("ys", [P, 2, QUADS, CH], fp32, r2)
        state_a = sb("state_a", [P, NC, 8 * SLOT], fp32, r2)
        ysq = sb("ysq", [P, NT, D], fp32, r2)
        yn = sb("yn", [P, 4, D], fp32, r2)
        gate = sb("gate", [P, B, NC, S], fp32, r2)
        y3 = sb("y3", [P, 2, NC, S], fp32, r2)
        x4T = sb("x4T", [P, B, NC, S], fp32, r2)
        sb("pad", [P, 12], fp32, r2)

        with ExitStack() as r3:
            w_lr = sb("w_left_right", [P, 2, NC, D], fp32, r3)
            w_gates = sb("w_gates", [P, 2, NC, D], fp32, r3)
            w_out = sb("w_out", [P, NC, D], fp32, r3)
            raw_ffn_down = sb("raw_ffn_down", [P, 2 * E], fp32, r3)
        r3 = ctx.enter_context(ExitStack())
        w_qkvg = [sb(f"w_qkvg_{k}", [P, NC, 4 * D], fp32r, r3) for k in ("hi", "lo")]
        w_o = sb("w_o", [P, NC, D])
        w_f = sb("w_f", [P, NC, D])

        banks = [ctx.enter_context(nc.psum_tensor(f"bank{i}", [P, 512], fp32)) for i in range(BANKS)]

        x_loaded = [sem(f"x_loaded{b}") for b in range(B)]
        vec_loaded, rows_loaded = sem("vec_loaded"), sem("rows_loaded")
        early_loaded, tables_loaded, masks_loaded = sem("early_loaded"), sem("tables_loaded"), sem("masks_loaded")
        placed = {name: sem(f"{name}_loaded") for name in ("left_right", "gates", "out", "o")}
        lr_scaled = sem("lr_scaled")
        ffn_down_loaded = sem("ffn_down_loaded")
        raw_loaded = [sem(f"raw_loaded{i}") for i in range(2)]
        filled = sem("filled")
        drained = [sem(f"drained{k}") for k in range(BANKS)]
        neg_half_ready = sem("neg_half_ready")
        pads_ready = sem("pads_ready")
        squares_ready = sem("squares_ready")
        var_ready, rs_ready = sem("var_ready"), sem("rs_ready")
        act_chain = sem("act_chain")
        stats_ready, quant_step, vmean_ready, centred = (
            sem("stats_ready"), sem("quant_step"), sem("vmean_ready"), sem("centred"))
        softplus_step, rse_ready, fsum_step = sem("softplus_step"), sem("rse_ready"), sem("fsum_step")
        normed = sem("normed")
        hi_ready = sem("hi_ready")
        w_hi, w_lo = sem("w_hi"), sem("w_lo")
        softplus_a, softplus_d = sem("softplus_a"), sem("softplus_d")
        absums_ready = sem("absums_ready")
        scales_ready, above_ready, ternary_ready = sem("scales_ready"), sem("above_ready"), sem("ternary_ready")
        xo_ready, xs_part, xs_ready, x4b_ready = sem("xo_ready"), sem("xs_part"), sem("xs_ready"), sem("x4b_ready")
        conv_step, conv_ready = sem("conv_step"), sem("conv_ready")
        gated_x, decay_ready, tanh_ready, a2_ready, mult2_ready = (
            sem("gated_x"), sem("decay_ready"), sem("tanh_ready"), sem("a2_ready"), sem("mult2_ready"))
        mult_ready, scan_step, lr_ready = sem("mult_ready"), sem("scan_step"), sem("lr_ready")
        hid_hi, hid_lo = sem("hid_hi"), sem("hid_lo")
        qk_ready, vzero = sem("qk_ready"), sem("vzero")
        state_part, state_ready = sem("state_part"), sem("state_ready")
        qz_ready, qz_ready_a, qz_ready_p = sem("qz_ready"), sem("qz_ready_a"), sem("qz_ready_p")
        ysq_ready, ysum_ready = sem("ysq_ready"), sem("ysum_ready")
        yrs_ready, yn_ready = sem("yrs_ready"), sem("yn_ready")
        head_var_ready, head_root_ready = sem("head_var_ready"), sem("head_root_ready")
        y3_gated = sem("y3_gated")
        out_ready = sem("out_ready")
        out_stored = [sem(f"out_stored{b}") for b in range(B)]

        def bank(*key):
            return banks[number[key] % BANKS]

        def wait_filled(eng, *key):
            eng.wait_ge(filled, number[key] + 1)

        def wait_drained(eng, *key):
            eng.wait_ge(drained[number[key] % BANKS], number[key] // BANKS + 1)

        def drains(instruction, *key):
            instruction.then_inc(drained[number[key] % BANKS], 1)

        def v(name, c=0, n=1):
            return vec[:, VECTORS[name] + c:VECTORS[name] + c + n]

        def raw_wait(eng, name):
            if name == "ffn_down":
                eng.wait_ge(ffn_down_loaded, 16)
                return raw_ffn_down
            n = LOAD[name]
            eng.wait_ge(raw_loaded[n % 2], 16 * (n // 2 + 1))
            return staging[n % 2]

        hi_count = {}
        for stage, b in walk({s: s for s in ("x1_T", "x2_T", "x3_T")}):
            hi_count[stage, b] = len(hi_count) + 1

        def hidden_key(n):
            return ("up2", n // 3, n % 3) if n < 3 * B else ("fgate", (n - 3 * B) // 4, (n - 3 * B) % 4)

        weight_count = {}
        for stage, n in walk({s: s for s in ("prep_up", "prep_down", "prep_qkvg")}):
            weight_count[stage, n] = len(weight_count) + 1

        rs_count = {}
        for stage, b in walk({s: s for s in ("square_x0", "out", "down", "ffn_down", "o", "f")}):
            rs_count[stage, b] = len(rs_count) + 1
        ln_count = {}
        for stage, b in walk({s: s for s in ("down", "ffn_down", "o", "f")}):
            ln_count[stage, b] = len(ln_count) + 1
        normed_count = {}
        for stage, b in walk({s: s for s in ("norm_x0", "norm_x1", "norm_x2", "norm_x3", "norm_x4")}):
            normed_count[stage, b] = len(normed_count) + 1

        slot = {}
        hidden_after, last_down = {}, {}
        for stage, b in walk({s: s for s in ("mlp", "ffn")}):
            n = slot[stage, b] = (MLP_SLOTS if stage == "mlp" else FFN_SLOTS)[b]
            hidden_after[stage, b] = last_down.get(n)
            last_down[n] = ("down" if stage == "mlp" else "ffn_down", b)

        def slots(ap):
            if len(ap.shape) == 2:
                return ap[:, :].rearrange("p (c h a s) -> p c h a s", c=NC, a=2, s=DH)
            return ap[:, :, :].rearrange("p c (h a s) -> p c h a s", a=2, s=DH)

        own_head = head_rows[:, None, :, None].to_broadcast([P, NC, 8, DH])

        block = ctx.enter_context(nc.Block())

        @block.sync
        def _(sp_eng):
            e = sp_eng
            last_use = [(w_lo, weight_count[n]) for n in (("prep_down", 0), ("prep_up", 0), ("prep_up", 1))]
            last_use += [(ternary_ready, 2), (ternary_ready, 3), (w_lo, weight_count["prep_qkvg", 0])]

            def load(dst, name):
                at, cols = PLACED[name]
                e.dma_start(dst, w_dram[:, at:at + cols]).then_inc(placed[name], 16)

            def stage_load(n):
                _, at, cols = STAGED[n]
                e.dma_start(staging[n % 2][:, 0:cols], w_dram[:, at:at + cols]).then_inc(raw_loaded[n % 2], 16)

            e.dma_start(x0[:, 0], x_dram[:, 0]).then_inc(x_loaded[0], 16)
            e.dma_start(vec[:, :], vec_dram).then_inc(vec_loaded, 16)
            e.dma_start(early[:, :], early_dram).then_inc(early_loaded, 16)
            load(w_lr[:, :, :, :], "left_right")
            e.dma_start(x0[:, 1], x_dram[:, 1]).then_inc(x_loaded[1], 16)
            load(w_gates[:, :, :, :], "gates")
            for b in range(2, B):
                e.dma_start(x0[:, b], x_dram[:, b]).then_inc(x_loaded[b], 16)
            for n in range(2):
                stage_load(n)
            at, cols = PLACED["ffn_down"]
            e.dma_start(raw_ffn_down[:, :], w_dram[:, at:at + cols]).then_inc(ffn_down_loaded, 16)
            load(w_out[:, :, :], "out")
            e.dma_start(rows[:, :, :], row_dram).then_inc(rows_loaded, 16)
            for n in range(2, len(STAGED)):
                e.wait_ge(*last_use[n - 2])
                stage_load(n)
            e.dma_start(masks[:, :], table_dram[:, 4 * 2 * D:]).then_inc(masks_loaded, 16)
            e.wait_ge(ternary_ready, 1)
            load(w_o[:, :, :], "o")
            wait_drained(e, "up2", B - 1, F // 256 - 1)
            e.dma_start(rope[:, :, :, :], table_dram[:, 0:4 * 2 * D]).then_inc(tables_loaded, 16)
            for b in range(B):
                e.wait_ge(out_ready, b + 1)
                e.dma_start(out_dram[:, b], x0o[:, b]).then_inc(out_stored[b], 16)
            for b in range(B):
                e.wait_ge(out_stored[b], 16)

        @block.tensor
        def _(pe):
            def open_bank(*key):
                n = number[key]
                if n >= BANKS:
                    pe.wait_ge(drained[n % BANKS], n // BANKS)
                return banks[n % BANKS]

            def split_product(out, stationary, moving, first=True):
                terms = []
                for (sh, sl), (mh, ml) in zip(stationary, moving):
                    if sl is not None:
                        terms.append((sl, mh))
                    if ml is not None:
                        terms.append((sh, ml))
                terms += [(sh, mh) for (sh, _), (mh, _) in zip(stationary, moving)]
                for n, (a, m) in enumerate(terms):
                    last = nc.tensor.matmul(out, a, m, start=(first and n == 0), stop=(n == len(terms) - 1),
                                            skip_group_check=True)
                return last

            def fm_product(key, weights, k_chunks, acts, m_at=0):
                out = open_bank(*key)
                for m in range(2):
                    last = split_product(
                        out[:, m * S:(m + 1) * S],
                        [weights(k, m_at + m) for k in range(k_chunks)],
                        [acts(k) for k in range(k_chunks)], first=(m == 0))
                last.then_inc(filled, 1)

            def tm_product(key, acts, k_chunks, weights):
                out = open_bank(*key)
                for t in range(NT):
                    last = split_product(
                        out[:, t * D:(t + 1) * D],
                        [tuple(None if a is None else a[:, t * P:(t + 1) * P] for a in acts(k))
                         for k in range(k_chunks)],
                        [weights(k) for k in range(k_chunks)], first=(t == 0))
                last.then_inc(filled, 1)

            def x_acts(b):
                return lambda k: (xh[:, b, k, :], xl[:, b, k, :])

            def turn(stage, source):
                def work(b):
                    pe.wait_ge(normed, normed_count[source[0], b])
                    out = open_bank(stage, b)
                    for c in range(NC):
                        for t in range(NT):
                            last = nc.tensor.transpose(out[:, c * S + t * P:c * S + (t + 1) * P],
                                                       source[1][:, b, t, c * P:(c + 1) * P], ident)
                    last.then_inc(filled, 1)
                return work

            def left_right(b):
                wait_drained(pe, "xn_T", b)
                for j, name in enumerate(("left", "right")):
                    if b == 0:
                        pe.wait_ge(lr_scaled, NC)
                    fm_product((name, b), lambda k, m: (w_lr[:, j, k, m * P:(m + 1) * P], None), NC,
                               lambda k: (x0T[:, b, k, :], None))

            def quant(n):
                pe.wait_ge(absums_ready, 4 * (n + 1))
                nc.tensor.matmul(open_bank("absum", n)[:, 0:4], ones, absums[:, 4 * n:4 * n + 4],
                                 start=True, stop=True).then_inc(filled, 1)

            def gates(b):
                pe.wait_ge(conv_ready, NC * (b + 1))
                if b == 0:
                    pe.wait_ge(placed["gates"], 16)
                for j, name in enumerate(("ga", "gx")):
                    fm_product((name, b), lambda k, m: (w_gates[:, j, k, m * P:(m + 1) * P], None), NC,
                               lambda k: (conv[:, b, k, :], None))

            def out(b):
                pe.wait_ge(lr_ready, b + 1)
                if b == 0:
                    pe.wait_ge(placed["out"], 16)
                tm_product(("out", b), lambda k: (left[:, b, k, :], None), NC, lambda k: (w_out[:, k, :], None))

            def mlp(b):
                wait_drained(pe, "x1_T", b)
                if b == 0:
                    pe.wait_ge(w_lo, weight_count["prep_up", 1])
                for j in range(F // 256):
                    for n, name in enumerate(("up1", "up2")):
                        fm_product((name, b, j),
                                   lambda k, m: tuple(w[:, k, n * F + m * P:n * F + (m + 1) * P] for w in w_ups),
                                   NC, x_acts(b), m_at=2 * j)

            def down(b):
                if b == 0:
                    pe.wait_ge(w_lo, weight_count["prep_down", 0])
                pe.wait_ge(hid_lo, 3 * (b + 1))
                tm_product(("down", b), lambda k: (hh[slot["mlp", b]][:, k, :], hl[slot["mlp", b]][:, k, :]), F // P,
                           lambda k: tuple(w[:, k, :] for w in w_dn))

            def ffn(b):
                wait_drained(pe, "x2_T", b)
                if b == 0:
                    pe.wait_ge(ternary_ready, 3)
                for j in range(E // 256):
                    for name, w in (("fup", q_up), ("fgate", q_gate)):
                        fm_product((name, b, j), lambda k, m: (w[:, k, m * P:(m + 1) * P], None), NC, x_acts(b),
                                   m_at=2 * j)

            def ffn_down(b):
                pe.wait_ge(hid_lo, 3 * B + 4 * (b + 1))
                side = slot["ffn", b]
                tm_product(("ffn_down", b), lambda k: (hh[side][:, k, :], hl[side][:, k, :]), E // P,
                           lambda k: (q_down[:, k, :], None))

            def qkv(b):
                wait_drained(pe, "x3_T", b)
                if b == 0:
                    pe.wait_ge(w_lo, weight_count["prep_qkvg", 0])
                def tile(k, t):
                    return xh[:, b, k, t * P:(t + 1) * P], xl[:, b, k, t * P:(t + 1) * P]
                for t in range(NT):
                    dst = open_bank("qk", b, t)
                    split_product(dst[:, :], [tile(k, t) for k in range(NC)],
                                  [tuple(w[:, k, 0:2 * D] for w in w_qkvg) for k in range(NC)]).then_inc(filled, 1)
                tm_product(("v", b), x_acts(b), NC, lambda k: tuple(w[:, k, 2 * D:3 * D] for w in w_qkvg))
                fm_product(("gate", b), lambda k, m: tuple(w[:, k, 3 * D + m * P:3 * D + (m + 1) * P] for w in w_qkvg),
                           NC, x_acts(b))

            def qk_T(b):
                for t in range(NT):
                    i = NT * b + t
                    pe.wait_ge(qk_ready, i + 1)
                    dst = open_bank("qk_T", b, t)
                    for c in range(4):
                        last = nc.tensor.transpose(dst[:, c * P:(c + 1) * P], qk[:, i % 4, c * P:(c + 1) * P], ident)
                    last.then_inc(filled, 1)
                wait_drained(pe, "v", b)
                for t in range(NT):
                    dst = open_bank("kv", b, t)
                    for c in range(NC):
                        last = nc.tensor.matmul(dst[:, c * 256:(c + 1) * 256],
                                                qk[:, (NT * b + t) % 4, D + c * P:D + (c + 1) * P],
                                                vpad[:, b % 2, t, c * 256:(c + 1) * 256], start=(c == 0), stop=True,
                                                skip_group_check=True)
                    last.then_inc(filled, 1)

            def scores(b):
                for t in range(NT):
                    i = NT * b + t
                    pe.wait_ge(qz_ready, i + 1)
                    pe.wait_ge(qz_ready_a, i + 1)
                    pe.wait_ge(qz_ready_p, i + 1)
                    for c in range(NC):
                        dst = open_bank("sc", b, t, c)
                        for a in range(2):
                            part = slice(a * CH, (a + 1) * CH)
                            last = nc.tensor.matmul(dst[part, :], qkT[:, i % 4, 2 + c, part],
                                                    qz[i % 2][:, 8 * c:8 * c + 8, part], start=True, stop=True,
                                                    skip_group_check=True)
                        last.then_inc(filled, 1)
                for t in range(NT):
                    i = NT * b + t
                    dst = open_bank("y", b, t)
                    pe.wait_ge(state_ready, 2 * b + t + 1)
                    for q in range(QUADS):
                        half = slice((q % 2) * P, (q % 2 + 1) * P)
                        for a, state in ((0, state_a), (1, state_b[:, t])):
                            if t == 0 and a == 0:
                                continue
                            nc.tensor.matmul(dst[:, q * CH:(q + 1) * CH], state[:, q // 2, half],
                                             qkT[:, i % 4, q // 2, a * CH:(a + 1) * CH],
                                             start=(q == 0 and a == 1 - t), stop=False, skip_group_check=True)
                    for q in range(QUADS):
                        wait_drained(pe, "sc", b, t, q // 2)
                        for j in range(4):
                            h = 4 * q + j
                            last = nc.tensor.matmul(dst[SLOT * j:SLOT * (j + 1), q * CH:(q + 1) * CH],
                                                    vpad[:, b % 2, t, h * SLOT:(h + 1) * SLOT],
                                                    probs[:, 2 * t + h // 8, (h % 8) * CH:(h % 8 + 1) * CH],
                                                    start=False, stop=True, skip_group_check=True)
                    last.then_inc(filled, 1)

            def y_T(b):
                dst = open_bank("y_T", b)
                for t in range(NT):
                    wait_drained(pe, "y", b, t)
                    for q in range(QUADS):
                        at = t * D + q * 4 * DH
                        for a in range(2):
                            last = nc.tensor.matmul(dst[a * CH:(a + 1) * CH, at:at + 4 * DH],
                                                    ys[:, (NT * b + t) % 2, q, :], pick[a], start=(t == 0 and q == 0),
                                                    stop=True, skip_group_check=True)
                last.then_inc(filled, 1)

            def yn_T(b):
                pe.wait_ge(yn_ready, b + 1)
                dst = open_bank("yn_T", b)
                for c in range(NC):
                    for t in range(NT):
                        last = nc.tensor.transpose(dst[:, c * S + t * P:c * S + (t + 1) * P],
                                                   yn[:, (NT * b + t) % 4, c * P:(c + 1) * P], ident)
                last.then_inc(filled, 1)

            def o(b):
                pe.wait_ge(y3_gated, b + 1)
                if b == 0:
                    pe.wait_ge(placed["o"], 16)
                tm_product(("o", b), lambda k: (y3[:, b % 2, k, :], None), NC, lambda k: (w_o[:, k, :], None))

            def f(b):
                wait_drained(pe, "x4_T", b)
                if b == 0:
                    pe.wait_ge(fsum_step, RANK + 1)
                tm_product(("f", b), lambda k: (x4T[:, b, k, :], None), NC, lambda k: (w_f[:, k, :], None))

            def warm_up(n):
                for _ in range(n):
                    nc.tensor.matmul(banks[BANKS - 1][:, 0:P], ident, ones, start=True, stop=True)

            def xn_T(b):
                turn("xn_T", ("norm_x0", x1))(b)
                if b == 0:
                    warm_up(4)

            pe.wait_ge(early_loaded, 16)
            warm_up(5)
            for work, b in walk({
                    "xn_T": xn_T, "left_right": left_right, "gates": gates, "out": out, "quant": quant,
                    "x1_T": turn("x1_T", ("norm_x1", x0o)), "mlp": mlp, "down": down,
                    "x2_T": turn("x2_T", ("norm_x2", x0o)), "ffn": ffn, "ffn_down": ffn_down,
                    "x3_T": turn("x3_T", ("norm_x3", x0)), "qkv": qkv, "qk_T": qk_T, "scores": scores,
                    "y_T": y_T, "yn_T": yn_T, "o": o, "x4_T": turn("x4_T", ("norm_x4", x1)), "f": f}):
                work(b)

        @block.scalar
        def _(act_eng):
            e = act_eng
            A = nc.scalar.activation

            def square_x0(b):
                e.wait_ge(x_loaded[b], 16)
                for t in range(NT):
                    if NT * b + t >= 2:
                        e.wait_ge(squares_ready, NT * b + t - 1)
                    A(square_out[:, t, :], x0[:, b, t, :], ACT.Square,
                      accum_out=ssq[:, b, t:t + 1]).then_inc(squares_ready, 1)

            def turned(stage):
                def work(b):
                    wait_filled(e, stage, b)
                    A(xh[:, b], bank(stage, b)[:, :], ACT.Copy).then_inc(hi_ready, 1)
                return work

            def copied(stage, dst):
                def work(b):
                    wait_filled(e, stage, b)
                    drains(A(dst[:, b], bank(stage, b)[:, :], ACT.Copy), stage, b)
                return work

            def left_right(b):
                e.wait_ge(vec_loaded, 16)
                wait_filled(e, "left", b)
                for m in range(NC):
                    last = A(left[:, b, m, :], bank("left", b)[:, m * S:(m + 1) * S], ACT.Gelu, bias=v("left_b", m))
                drains(last, "left", b)
                wait_filled(e, "right", b)
                if b >= 2:
                    e.wait_ge(conv_ready, NC * (b - 1))
                for m in range(NC):
                    last = A(right[:, b % 2, m, 3:], bank("right", b)[:, m * S:(m + 1) * S], ACT.Identity,
                             bias=v("right_b", m))
                drains(last, "right", b)

            def gates(b):
                for name, dst in (("ga", r_gate), ("gx", i_gate)):
                    wait_filled(e, name, b)
                    for m in range(NC):
                        last = A(dst[:, b, m, :], bank(name, b)[:, m * S:(m + 1) * S], ACT.Sigmoid, bias=v(f"{name}_b", m))
                    drains(last, name, b)

            def decays(b):
                if b == 0:
                    e.wait_ge(softplus_d, 1)
                wait_drained(e, "ga", b)
                e.wait_ge(gated_x, b + 1)
                for m in range(NC):
                    last = A(decay[:, b, m, :], r_gate[:, b, m, :], ACT.Exp, scale=decay_c[:, 0, m:m + 1])
                last.then_inc(decay_ready, 1)
                e.wait_ge(decay_ready, b + 1)
                for m in range(NC):
                    last = A(r_gate[:, b, m, :], r_gate[:, b, m, :], ACT.Tanh, scale=decay_c[:, 1, m:m + 1])
                last.then_inc(tanh_ready, 1)

            def scan(b):
                e.wait_ge(mult2_ready, b + 1)
                A(r_gate[:, b], r_gate[:, b], ACT.Sqrt).then_inc(mult_ready, 1)

            def square_x1(b):
                wait_drained(e, "out", b)
                for t in range(NT):
                    e.wait_ge(squares_ready, NT * (B + b) + t - 1)
                    A(square_out[:, t, :], x1[:, b, t, :], ACT.Square,
                      accum_out=ssq[:, b, t:t + 1]).then_inc(squares_ready, 1)

            def gated(b, j, name, n, act, hi, activate):
                wait_filled(e, name, b, j)
                if n >= 3:
                    wait_drained(e, *hidden_key(n - 3))
                drains(activate(act[:, n % 3]), name, b, j)
                wait_drained(e, *hidden_key(n))
                A(hi[:, 2 * j:2 * j + 2, :], hid[:, n % 2], ACT.Copy).then_inc(hid_hi, 1)

            def mlp(b):
                if hidden_after["mlp", b]:
                    wait_filled(e, *hidden_after["mlp", b])
                else:
                    wait_filled(e, "out", 2 * slot["mlp", b] + 1)
                for j in range(F // 256):
                    def activate(dst):
                        for m in range(2):
                            last = A(dst[:, m, :], bank("up1", b, j)[:, m * S:(m + 1) * S], ACT.Gelu,
                                     bias=v("up1_b", 2 * j + m))
                        return last
                    gated(b, j, "up1", 3 * b + j, mlp_act, hh[slot["mlp", b]], activate)

            def ffn(b):
                if b == 0:
                    e.wait_ge(scales_ready, 4)
                    e.wait_ge(mult2_ready, B)
                wait_filled(e, *hidden_after["ffn", b])
                for j in range(E // 256):
                    gated(b, j, "fup", 3 * B + 4 * b + j, ffn_act, hh[slot["ffn", b]],
                          lambda dst: A(dst, bank("fup", b, j)[:, :], ACT.Silu, scale=qc[:, 0:1]))

            def qkv(b):
                wait_filled(e, "v", b)
                e.wait_ge(vzero, 1)
                if b >= 2:
                    wait_filled(e, "y", b - 2, 1)
                for a in range(2):
                    part = slice(a * CH, (a + 1) * CH)
                    for t in range(NT):
                        last = A(vpad[part, b % 2, t].rearrange("p (h s) -> p h s", s=SLOT)[:, :, a * DH:(a + 1) * DH],
                                 bank("v", b)[part, t * D:(t + 1) * D].rearrange("p (h s) -> p h s", s=DH), ACT.Copy)
                drains(last, "v", b)
                wait_filled(e, "gate", b)
                drains(A(gate[:, b], bank("gate", b)[:, :], ACT.Silu), "gate", b)

            def qk_T(b):
                for t in range(NT):
                    wait_filled(e, "qk_T", b, t)
                    if b >= 2:
                        wait_filled(e, "y", b - 2, t)
                    drains(A(qkT[:, (NT * b + t) % 4], bank("qk_T", b, t)[:, :], ACT.Copy), "qk_T", b, t)

            def spread(b):
                if b == 0:
                    e.wait_ge(masks_loaded, 16)
                for t in range(NT):
                    i = NT * b + t
                    wait_drained(e, "qk_T", b, t)
                    if b >= 1:
                        wait_filled(e, "sc", b - 1, t, NC - 1)
                    for h in range(8, 12):
                        last = A(qz[i % 2][:, h, :], qkT[:, i % 4, 1, :], ACT.Copy, scale=head_rows[:, h - 8:h - 7])
                    last.then_inc(qz_ready_a, 1)

            def scores(b):
                for t in range(NT):
                    wait_filled(e, "y", b, t)
                    if b >= 1:
                        wait_filled(e, "y_T", b - 1)
                    drains(A(ys[:, (NT * b + t) % 2], bank("y", b, t)[:, 0:D], ACT.Copy), "y", b, t)

            def y_T(b):
                wait_filled(e, "y_T", b)
                if b >= 1:
                    e.wait_ge(ysum_ready, b)
                A(ysq[:, :, :], bank("y_T", b)[:, :], ACT.Square).then_inc(ysq_ready, 1)
                if b >= 2:
                    wait_filled(e, "yn_T", b - 2)
                drains(A(yn[:, NT * (b % 2):NT * (b % 2 + 1)], bank("y_T", b)[:, :], ACT.Copy), "y_T", b)

            def head_root(b):
                e.wait_ge(head_var_ready, b + 1)
                A(ysum[:, b], ysum[:, b], ACT.Sqrt).then_inc(head_root_ready, 1)

            def yn_T(b):
                wait_filled(e, "yn_T", b)
                if b >= 2:
                    wait_filled(e, "o", b - 2)
                for c in range(NC):
                    last = A(y3[:, b % 2, c, :], bank("yn_T", b)[:, c * S:(c + 1) * S], ACT.Identity,
                             scale=v("gn_w", c), bias=v("gn_b", c))
                drains(last, "yn_T", b)

            def softplus(_):
                e.wait_ge(vec_loaded, 16)
                A(sp[:, 0, :], v("a_param", 0, 2), ACT.Abs).then_inc(act_chain, 1)
                e.wait_ge(act_chain, 1)
                A(sp[:, 1, :], sp[:, 0, :], ACT.Exp, scale=-1.0).then_inc(act_chain, 1)
                e.wait_ge(act_chain, 2)
                A(sp[:, 2, :], sp[:, 1, :], ACT.Ln, bias=1.0).then_inc(softplus_a, 1)

            def prep_down(_):
                A(w_dn[0][:, :, :], raw_wait(e, "down")[:, 0:6 * D], ACT.Copy).then_inc(w_hi, 1)

            def prep_up(k):
                A(w_ups[0][:, k, :], raw_wait(e, f"up_k{k}")[:, 0:2 * F], ACT.Copy,
                  scale=v("norm2_w", k)).then_inc(w_hi, 1)

            def prep_qkvg(_):
                raw = raw_wait(e, "qkvg")
                e.wait_ge(centred, NC)
                wait_filled(e, "out", B - 1)
                A(w_qkvg[0][:, :, :], raw[:, :], ACT.Copy).then_inc(w_hi, 1)

            def absum(n):
                raw = raw_wait(e, TERNARY[n])
                for part in range(4 * n, 4 * n + 4):
                    if part >= 1:
                        e.wait_ge(absums_ready, part)
                    at = (part - 4 * n) * 512
                    A(abs_out[:, :], raw[:, at:at + 512], ACT.Abs,
                      accum_out=absums[:, part:part + 1]).then_inc(absums_ready, 1)

            for work, b in walk({
                    "square_x0": square_x0, "xn_T": copied("xn_T", x0T), "left_right": left_right,
                    "gates": gates, "decay": decays, "scan": scan,
                    "out": square_x1, "softplus": softplus, "absum": absum, "prep_down": prep_down,
                    "prep_up": prep_up, "prep_qkvg": prep_qkvg,
                    "x1_T": turned("x1_T"), "mlp": mlp, "x2_T": turned("x2_T"), "ffn": ffn,
                    "x3_T": turned("x3_T"), "qkv": qkv, "qk_T": qk_T, "qz": spread, "scores": scores, "y_T": y_T,
                    "yn": head_root, "yn_T": yn_T, "x4_T": copied("x4_T", x4T)}):
                work(b)

        @block.vector
        def _(dve):
            e, V = dve, nc.vector
            TT, TS, STT = V.tensor_tensor, V.tensor_scalar, V.scalar_tensor_tensor

            def norm(stage, stat_stage, src, dst, mean):
                def work(b):
                    e.wait_ge(rs_ready, rs_count[stat_stage, b])
                    for t in range(NT):
                        if mean:
                            last = TS(dst[:, b, t, :], src[:, b, t, :], mv[:, b, t, 0:1], rs[:, b, t:t + 1],
                                      ALU.subtract, ALU.mult)
                        else:
                            last = TS(dst[:, b, t, :], src[:, b, t, :], rs[:, b, t:t + 1], None, ALU.mult)
                    last.then_inc(out_ready if stage == "final" else normed, 1)
                return work

            def turned(stage):
                def work(b):
                    e.wait_ge(hi_ready, hi_count[stage, b])
                    drains(TT(xl[:, b], bank(stage, b)[:, :].rearrange("p (c s) -> p c s", c=NC),
                              xh[:, b].bitcast(fp32), ALU.subtract), stage, b)
                return work

            def conv_work(b):
                wait_drained(e, "right", b)
                if b == 0:
                    e.wait_ge(pads_ready, 1)
                for k in range(4):
                    for m in range(NC):
                        dst, tap, w = conv[:, b, m, :], right[:, b % 2, m, k:k + S], v("conv_w", NC * k + m)
                        if k == 0:
                            TS(dst, tap, w, v("conv_b", m), ALU.mult, ALU.add).then_inc(conv_step, 1)
                        else:
                            e.wait_ge(conv_step, 3 * NC * b + NC * (k - 1) + m + 1)
                            STT(out=dst, in0=tap, scalar=w, in1=dst, op0=ALU.mult, op1=ALU.add)\
                                .then_inc(conv_step if k < 3 else conv_ready, 1)

            def decays(b):
                e.wait_ge(a2_ready, b + 1)
                e.wait_ge(tanh_ready, b + 1)
                STT(out=r_gate[:, b], in0=squared[:, :], scalar=1.0, in1=r_gate[:, b],
                    op0=ALU.add, op1=ALU.mult).then_inc(mult2_ready, 1)

            def scan(b):
                e.wait_ge(mult_ready, b + 1)
                e.wait_ge(gated_x, b + 1)
                TT(i_gate[:, b], i_gate[:, b], r_gate[:, b], ALU.mult).then_inc(scan_step, 1)
                e.wait_ge(scan_step, 3 * b + 1)
                for m in range(NC):
                    V.tensor_tensor_scan(r_gate[:, b, m, :], decay[:, b, m, :], i_gate[:, b, m, :], 0.0,
                                         ALU.mult, ALU.add).then_inc(scan_step, 1)
                e.wait_ge(scan_step, 3 * b + 3)
                TT(left[:, b], left[:, b], r_gate[:, b], ALU.mult).then_inc(lr_ready, 1)

            def out(b):
                wait_filled(e, "out", b)
                e.wait_ge(xo_ready, b + 1)
                drains(TT(x1[:, b], bank("out", b)[:, :].rearrange("p (t d) -> p t d", t=NT), x0o[:, b], ALU.add),
                       "out", b)

            def hidden_lo(side, j, n):
                e.wait_ge(hid_hi, n + 1)
                TT(hl[side][:, 2 * j:2 * j + 2, :], hid[:, n % 2], hh[side][:, 2 * j:2 * j + 2, :].bitcast(fp32),
                   ALU.subtract).then_inc(hid_lo, 1)

            def mlp(b):
                for j in range(F // 256):
                    n = 3 * b + j
                    wait_filled(e, "up2", b, j)
                    wait_drained(e, "up1", b, j)
                    if n >= 2:
                        e.wait_ge(hid_lo, n - 1)
                    for m in range(2):
                        last = STT(out=hid[:, n % 2, m, :], in0=bank("up2", b, j)[:, m * S:(m + 1) * S],
                                   scalar=v("up2_b", 2 * j + m), in1=mlp_act[:, n % 3, m, :], op0=ALU.add, op1=ALU.mult)
                    drains(last, "up2", b, j)
                    if j >= 1:
                        hidden_lo(slot["mlp", b], j - 1, n - 1)
                hidden_lo(slot["mlp", b], j, n)

            def ffn(b):
                for j in range(E // 256):
                    n = 3 * B + 4 * b + j
                    wait_filled(e, "fgate", b, j)
                    wait_drained(e, "fup", b, j)
                    e.wait_ge(hid_lo, n - 1)
                    drains(TT(hid[:, n % 2], bank("fgate", b, j)[:, :].rearrange("p (c s) -> p c s", c=2), ffn_act[:, n % 3],
                              ALU.mult), "fgate", b, j)
                    if j >= 1:
                        hidden_lo(slot["ffn", b], j - 1, n - 1)
                hidden_lo(slot["ffn", b], j, n)

            def close(stage, dst, resid, ready, scaled):
                def work(b):
                    wait_filled(e, stage, b)
                    if ready is not None:
                        e.wait_ge(ready, b + 1)
                    z = bank(stage, b)[:, :].rearrange("p (t d) -> p t d", t=NT)
                    if scaled:
                        last = STT(out=dst[:, b], in0=z, scalar=qc[:, 1:2], in1=resid[:, b], op0=ALU.mult, op1=ALU.add)
                    else:
                        last = TT(dst[:, b], z, resid[:, b], ALU.add)
                    drains(last, stage, b)
                    wait_drained(e, stage, b)
                    n = ln_count[stage, b]
                    for t in range(NT):
                        V.bn_stats(stats[:, b, t, :], dst[:, b, t, :]).then_inc(stats_ready, 1)
                    e.wait_ge(stats_ready, NT * n)
                    for t in range(NT):
                        last = V.bn_aggr(mv[:, b, t, :], stats[:, b, t, :])
                    last.then_inc(var_ready, 1)
                return work

            def qkv(b):
                for t in range(NT):
                    i = NT * b + t
                    wait_filled(e, "qk", b, t)
                    if i == 0:
                        e.wait_ge(tables_loaded, 16)
                    if b >= 2 and t == 0:
                        wait_filled(e, "kv", b - 2, 1)
                    if i >= 2:
                        e.wait_ge(qk_ready, i - 1)
                    TT(qk[:, i % 4, :], bank("qk", b, t)[:, :], rope[:, 0, t, :], ALU.mult)
                    pairs = lambda ap: ap.rearrange("p (n two) -> p n two", two=2)
                    drains(TT(pairs(qk_sin[:, i % 2, :]), pairs(bank("qk", b, t)[:, :])[:, :, ::-1],
                              pairs(rope[:, 1, t, :]), ALU.mult), "qk", b, t)

            def kv(b):
                if b == 0:
                    e.wait_ge(vzero, 1)
                for t in range(NT):
                    wait_filled(e, "kv", b, t)
                    if b >= 1:
                        wait_filled(e, "y", b - 1, 1)
                    kv_t = slots(bank("kv", b, t))
                    last = TT(slots(state_b[:, t])[:, :, :, 1, :], kv_t[:, :, :, 0, :], own_head, ALU.mult)
                    if t == 0:
                        last.then_inc(state_part, 1)
                        last = TT(slots(state_a)[:, :, :, 0, :], kv_t[:, :, :, 1, :], own_head, ALU.mult)
                    drains(last, "kv", b, t)

            def spread(b):
                for t in range(NT):
                    i = NT * b + t
                    wait_drained(e, "qk_T", b, t)
                    if b >= 1:
                        wait_filled(e, "sc", b - 1, t, NC - 1)
                    TT(qz[i % 2][:, 0:8, :], qkT[:, i % 4, 0, :][:, None, :].to_broadcast([P, 8, P]),
                       head_rows[:, :, None].to_broadcast([P, 8, P]), ALU.mult).then_inc(qz_ready, 1)

            def scores(b):
                for t in range(NT):
                    for c in range(NC):
                        wait_filled(e, "sc", b, t, c)
                        if b > 0:
                            wait_filled(e, "y", b - 1, t)
                        drains(TT(probs[:, 2 * t + c, :].rearrange("p (j s) -> p j s", s=CH),
                                  bank("sc", b, t, c)[:, :].rearrange("p (j s) -> p j s", s=CH),
                                  causal[:, None, :].to_broadcast([P, 8, CH]), ALU.mult), "sc", b, t, c)

            def y_T(b):
                e.wait_ge(ysq_ready, b + 1)
                V.tensor_reduce(ysum[:, b], ysq[:, :, :].rearrange("p t (h s) -> p t h s", s=DH), AX.X,
                                ALU.add).then_inc(ysum_ready, 1)
                e.wait_ge(ysum_ready, b + 1)
                TS(ysum[:, b], ysum[:, b], 1.0 / DH, EPS_LN, ALU.mult, ALU.add).then_inc(head_var_ready, 1)

            def yn_work(b):
                e.wait_ge(head_root_ready, b + 1)
                V.reciprocal(yrs[:, b], ysum[:, b]).then_inc(yrs_ready, 1)
                e.wait_ge(yrs_ready, b + 1)
                wait_drained(e, "y_T", b)
                y = yn[:, NT * (b % 2):NT * (b % 2 + 1)].rearrange("p t (h s) -> p (t h) s", s=DH)
                TT(y, y, yrs[:, b].rearrange("p t h -> p (t h)")[:, :, None].to_broadcast([P, NT * H, DH]),
                   ALU.mult).then_inc(yn_ready, 1)

            def yn_T(b):
                wait_drained(e, "yn_T", b)
                wait_drained(e, "gate", b)
                TT(y3[:, b % 2], y3[:, b % 2], gate[:, b], ALU.mult).then_inc(y3_gated, 1)

            def prep_lr(_):
                e.wait_ge(vec_loaded, 16)
                e.wait_ge(placed["left_right"], 16)
                for k in range(NC):
                    TS(w_lr[:, :, k, :], w_lr[:, :, k, :], v("norm1_w", k), None, ALU.mult).then_inc(lr_scaled, 1)

            def lo_half(stage, w, load, lo, hi):
                e.wait_ge(w_hi, weight_count[stage, 0])
                TT(w[1][:, :, :], staging[LOAD[load] % 2][:, lo:hi].rearrange("p (k n) -> p k n", k=w[0].shape[1]),
                   w[0][:, :, :].bitcast(fp32), ALU.subtract).then_inc(w_lo, 1)

            def prep_down(_):
                lo_half("prep_down", w_dn, "down", 0, 6 * D)

            def prep_up(k):
                e.wait_ge(w_hi, weight_count["prep_up", k])
                STT(out=w_ups[1][:, k, :], in0=staging[LOAD[f"up_k{k}"] % 2][:, 0:2 * F], scalar=v("norm2_w", k),
                    in1=w_ups[0][:, k, :].bitcast(fp32), op0=ALU.mult, op1=ALU.subtract).then_inc(w_lo, 1)

            def quant(n):
                wait_filled(e, "absum", n)
                drains(V.tensor_reduce(qs[:, n:n + 1], bank("absum", n)[:, 0:4], AX.X, ALU.add), "absum", n)
                wait_drained(e, "absum", n)
                TS(qs[:, n:n + 1], qs[:, n:n + 1], 1.0 / (D * E), EPS_Q, ALU.mult, ALU.add).then_inc(quant_step, 1)
                e.wait_ge(quant_step, n + 1)
                TS(qt[:, 1, n:n + 1], qs[:, n:n + 1], -0.5, None, ALU.mult)
                TS(qt[:, 0, n:n + 1], qs[:, n:n + 1], 0.5, None, ALU.mult).then_inc(scales_ready, 1)
                if n == 2:
                    TS(qc[:, 0:1], qs[:, 1:2], -1.0, None, ALU.mult)
                    TT(qc[:, 1:2], qs[:, 0:1], qs[:, 2:3], ALU.mult).then_inc(scales_ready, 1)

            def ternary(n):
                dst = (q_down, q_up, q_gate)[n]
                e.wait_ge(scales_ready, n + 1)
                raw = (raw_ffn_down if n == 0 else staging[LOAD[TERNARY[n]] % 2])[:, :].rearrange(
                    "p (k n) -> p k n", k=dst.shape[1])
                TS(dst[:, :, :], raw, qt[:, 0, n:n + 1], None, ALU.is_gt).then_inc(above_ready, 1)
                e.wait_ge(above_ready, n + 1)
                STT(out=dst[:, :, :], in0=raw, scalar=qt[:, 1, n:n + 1], in1=dst[:, :, :].bitcast(fp32),
                    op0=ALU.is_lt, op1=ALU.subtract).then_inc(ternary_ready, 1)

            def centre(_):
                raw = raw_wait(e, "qkvg")
                for k in range(NC):
                    part = raw[:, k * 4 * D + 2 * D:k * 4 * D + 3 * D].rearrange("p (h s) -> p h s", s=DH)
                    V.tensor_reduce(vmean[:, k, :], part, AX.X, ALU.add).then_inc(vmean_ready, 1)
                for k in range(NC):
                    part = raw[:, k * 4 * D + 2 * D:k * 4 * D + 3 * D].rearrange("p (h s) -> p h s", s=DH)
                    e.wait_ge(vmean_ready, k + 1)
                    STT(out=part, in0=vmean[:, k, :][:, :, None].to_broadcast([P, H, DH]), scalar=-1.0 / DH, in1=part,
                        op0=ALU.mult, op1=ALU.add).then_inc(centred, 1)

            def lo_qkvg(_):
                e.wait_ge(ternary_ready, 1)
                lo_half("prep_qkvg", w_qkvg, "qkvg", 0, 4 * 2 * D)

            V.memset(right[:, :, :, 0:3], 0.0).then_inc(pads_ready, 1)
            def softplus(_):
                e.wait_ge(softplus_a, 1)
                chain = [0]

                def link(instruction):
                    chain[0] += 1
                    instruction.then_inc(softplus_step, 1)
                    e.wait_ge(softplus_step, chain[0])

                link(TS(sp[:, 3, :], sp[:, 1, :], 1.0, -1.0, ALU.add, ALU.add))
                link(TS(sp[:, 4, :], sp[:, 3, :], 0.0, None, ALU.is_equal))
                link(TT(sp[:, 5, :], sp[:, 3, :], sp[:, 4, :], ALU.add))
                link(V.reciprocal(sp[:, 6, :], sp[:, 5, :]))
                link(TT(sp[:, 6, :], sp[:, 6, :], sp[:, 2, :], ALU.mult))
                link(TT(sp[:, 6, :], sp[:, 6, :], sp[:, 4, :], ALU.add))
                link(TT(sp[:, 6, :], sp[:, 6, :], sp[:, 1, :], ALU.mult))
                link(STT(out=sp[:, 7, :], in0=v("a_param", 0, 2), scalar=0.0, in1=sp[:, 6, :], op0=ALU.max, op1=ALU.add))
                link(TS(decay_c[:, 0, :], sp[:, 7, :], -C_RGLRU, None, ALU.mult))
                TS(decay_c[:, 1, :], sp[:, 7, :], C_RGLRU, None, ALU.mult).then_inc(softplus_d, 1)

            for work, b in walk({
                    "norm_x0": norm("norm_x0", "square_x0", x0, x1, False), "conv": conv_work,
                    "decay": decays, "scan": scan, "out": out,
                    "norm_x1": norm("norm_x1", "out", x1, x0o, False), "x1_T": turned("x1_T"), "mlp": mlp,
                    "down": close("down", x0o, x0, xs_ready, False),
                    "norm_x2": norm("norm_x2", "down", x0o, x0o, True), "x2_T": turned("x2_T"), "ffn": ffn,
                    "ffn_down": close("ffn_down", x0, x0o, None, True),
                    "norm_x3": norm("norm_x3", "ffn_down", x0, x0, True), "x3_T": turned("x3_T"), "qkv": qkv,
                    "qk_T": kv, "qz": spread, "scores": scores, "y_T": y_T, "yn": yn_work, "yn_T": yn_T,
                    "o": close("o", x1, x0, None, False),
                    "norm_x4": norm("norm_x4", "o", x1, x1, True), 
                    "f": close("f", x0o, x0, x4b_ready, False),
                    "final": norm("final", "f", x0o, x0o, True),
                    "softplus": softplus, "prep_lr": prep_lr, "prep_down": prep_down, "prep_up": prep_up, "quant": quant,
                    "ternary": ternary, "centre": centre, "lo_qkvg": lo_qkvg}):
                work(b)

        @block.gpsimd
        def _(pool):
            e, G = pool, nc.gpsimd

            def spread_row(n):
                return rows[:, n, :][:, None, :].to_broadcast([P, NT, D])

            def root(stage, src, scale, eps):
                def work(b):
                    if stage == "square_x0":
                        e.wait_ge(squares_ready, NT * (b + 1))
                    elif stage == "out":
                        e.wait_ge(squares_ready, NT * (B + b + 1))
                    else:
                        e.wait_ge(var_ready, ln_count[stage, b])
                    n = rs_count[stage, b]
                    G.tensor_scalar(rse[:, b, :], src(b), scale, eps, ALU.mult, ALU.add).then_inc(rse_ready, 1)
                    e.wait_ge(rse_ready, n)
                    G.tensor_tensor(rs[:, b, :], rse[:, b, :], neg_half[:, :], ALU.pow).then_inc(rs_ready, 1)
                return work

            def ssq_of(b):
                return ssq[:, b, :]

            def var_of(b):
                return mv[:, b, :, 1]

            def add_out_b(b):
                if b == 0:
                    e.wait_ge(rows_loaded, 16)
                e.wait_ge(x_loaded[b], 16)
                G.tensor_tensor(x0o[:, b], x0[:, b], spread_row(0), ALU.add).then_inc(xo_ready, 1)

            def gate_x(b):
                wait_drained(e, "gx", b)
                e.wait_ge(conv_ready, NC * (b + 1))
                G.tensor_tensor(i_gate[:, b], i_gate[:, b], conv[:, b], ALU.mult).then_inc(gated_x, 1)

            def square_decay(b):
                e.wait_ge(decay_ready, b + 1)
                if b >= 1:
                    e.wait_ge(mult2_ready, b)
                G.tensor_tensor(squared[:, :], decay[:, b], decay[:, b], ALU.mult).then_inc(a2_ready, 1)

            def residual(b):
                e.wait_ge(normed, normed_count["norm_x0", b])
                e.wait_ge(xo_ready, b + 1)
                G.tensor_tensor(x0[:, b], x0[:, b], spread_row(1), ALU.add).then_inc(xs_part, 1)
                e.wait_ge(xs_part, b + 1)
                wait_drained(e, "out", b)
                G.tensor_tensor(x0[:, b], x0[:, b], x1[:, b], ALU.add).then_inc(xs_ready, 1)

            def add_ffn_bias(b):
                e.wait_ge(normed, normed_count["norm_x4", b])
                G.tensor_tensor(x0[:, b], x1[:, b], spread_row(2), ALU.add).then_inc(x4b_ready, 1)

            def qkv(b):
                for t in range(NT):
                    i = NT * b + t
                    wait_drained(e, "qk", b, t)
                    G.tensor_tensor(qk[:, i % 4, :], qk[:, i % 4, :], qk_sin[:, i % 2, :], ALU.add).then_inc(qk_ready, 1)

            def clear_values(_):
                wait_filled(e, "down", B - 1)
                wait_filled(e, "ffn_down", B - 1)
                G.memset(vpad[:, :, :, :], 0.0)
                G.memset(state_b[:, :, :, :], 0.0)
                G.memset(state_a[:, :, :], 0.0).then_inc(vzero, 1)

            def kv(b):
                wait_drained(e, "kv", b, 0)
                e.wait_ge(state_part, b + 1)
                a, b0, b1 = (slots(x)[:, :, :, n, :] for x, n in ((state_a, 0), (state_b[:, 0], 1), (state_b[:, 1], 1)))
                G.tensor_tensor(a, a, b0, ALU.add).then_inc(state_ready, 1)
                wait_drained(e, "kv", b, 1)
                e.wait_ge(state_ready, 2 * b + 1)
                G.tensor_tensor(b1, b1, a, ALU.add).then_inc(state_ready, 1)

            def spread(b):
                if b == 0:
                    e.wait_ge(masks_loaded, 16)
                for t in range(NT):
                    i = NT * b + t
                    wait_drained(e, "qk_T", b, t)
                    if b >= 1:
                        wait_filled(e, "sc", b - 1, t, NC - 1)
                    G.tensor_tensor(qz[i % 2][:, 12:H, :], qkT[:, i % 4, 1, :][:, None, :].to_broadcast([P, 4, P]),
                                    head_rows[:, 4:8, None].to_broadcast([P, 4, P]), ALU.mult).then_inc(qz_ready_p, 1)

            def prep_f(half):
                raw = raw_wait(e, f"factors{half}")
                total = w_f[:, :, :].rearrange("p k n -> p (k n)")
                for r in range(4):
                    n = 4 * half + r
                    if n == 0:
                        G.tensor_scalar(total, raw[:, 0:512], 1.0, None, ALU.mult).then_inc(fsum_step, 1)
                    else:
                        e.wait_ge(fsum_step, n)
                        G.tensor_tensor(total, total, raw[:, r * 512:(r + 1) * 512], ALU.add).then_inc(fsum_step, 1)
                if half == 1:
                    e.wait_ge(fsum_step, RANK)
                    G.tensor_scalar(total, total, float(RANK) ** -0.5, None, ALU.mult).then_inc(fsum_step, 1)

            G.memset(neg_half[:, :], -0.5).then_inc(neg_half_ready, 1)
            e.wait_ge(neg_half_ready, 1)
            for work, b in walk({
                    "square_x0": root("square_x0", ssq_of, 1.0 / D, EPS_RMS), "add_out_b": add_out_b, "gates": gate_x,
                    "decay": square_decay, "out": root("out", ssq_of, 1.0 / D, EPS_RMS), "residual": residual,
                    "down": root("down", var_of, 1.0, EPS_LN), "ffn_down": root("ffn_down", var_of, 1.0, EPS_LN),
                    "clear": clear_values, "qkv": qkv, "qk_T": kv, "qz": spread, "o": root("o", var_of, 1.0, EPS_LN),
                    "norm_x4": add_ffn_bias, "f": root("f", var_of, 1.0, EPS_LN),
                    "prep_f": prep_f}):
                work(b)


def tables():
    n = np.arange(S, dtype=np.float64)[:, None]
    half = DH // 2
    xscale = (np.arange(0, DH, 2, dtype=np.float64) + 0.4 * DH) / (1.4 * DH)
    scale = xscale[None, :] ** (n / 64.0)
    angle = n * (1.0 / 10000.0 ** (np.arange(half, dtype=np.float64) / half))[None, :]
    gamma = 1.0 - np.exp(np.linspace(np.log(1.0 / 32), np.log(1.0 / 64), H))
    sign = np.tile([-1.0, 1.0], half)
    table = np.zeros((2, S, 2, H, DH))
    for part, (s, g) in enumerate(((scale, gamma[None, :] ** n), (1.0 / scale, gamma[None, :] ** -n))):
        for which, wave in enumerate((np.cos(angle), np.sin(angle))):
            row = np.repeat(wave * s, 2, axis=1) * (sign if which else 1.0)
            table[which, :, part] = g[:, :, None] * row[:, None, :]
    rope = table.reshape(2, NT, P, 2 * D).transpose(2, 0, 1, 3).reshape(P, -1)
    p = np.arange(P)
    q = np.arange(CH)
    causal = q[None, :] >= p[:, None] % CH
    pick = [(p[:, None] // SLOT == q[None, :] // DH) & (p[:, None] % SLOT == a * DH + q[None, :] % DH) for a in range(2)]
    head_rows = p[:, None] // DH == np.arange(8)[None, :]
    early = np.concatenate([np.eye(P), np.ones((P, P))], axis=1)
    return early.astype(np.float32), np.concatenate([rope, causal, *pick, head_rows], axis=1).astype(np.float32)


def kernel(**inputs):
    import concourse.bacc as bacc
    from concourse.bass_utils import run_bass_kernel_spmd as run

    a = {k: np.asarray(x) for k, x in inputs.items()}

    def by_chunk(w):
        return w.reshape(-1, P, w.shape[1]).transpose(1, 0, 2).reshape(P, -1)

    def columns(x):
        return x.reshape(-1, P).T

    def heads(w):
        return w.transpose(1, 0, 2).reshape(D, D)

    vec = np.concatenate([columns(x) for x in (
        a["L0_attn_norm1_w"], a["L0_attn_left_b"], a["L0_attn_right_b"], a["L0_attn_conv_w"].reshape(-1),
        a["L0_attn_conv_b"], a["L0_attn_ga_b"], a["L0_attn_gx_b"], a["L0_attn_a_param"], a["L0_attn_norm2_w"],
        a["L0_attn_up1_b"], a["L0_attn_up2_b"], a["L1_attn_gn_weight"], a["L1_attn_gn_bias"])], axis=1)
    row = np.broadcast_to(np.stack([a["L0_attn_out_b"], a["L0_attn_down_b"], a["L1_ffn_bias"]]), (P, 3, D))
    ups = np.concatenate([a["L0_attn_up1_W"], a["L0_attn_up2_W"]], axis=1)
    qkvg = np.concatenate([heads(a["L1_attn_W_Q"]), heads(a["L1_attn_W_K"]), heads(a["L1_attn_W_V"]),
                           a["L1_attn_W_G"]], axis=1)
    factors = [by_chunk(f) for f in a["L1_ffn_factors"]]
    rg = [by_chunk(a[f"L0_attn_{n}_W"]) for n in ("left", "right", "ga", "gx", "out")]
    weights = np.concatenate(
        rg + [by_chunk(a["L1_attn_W_O"]), by_chunk(a["L0_ffn_W_down"].T), by_chunk(a["L0_attn_down_W"]), ups[0:P],
              ups[P:2 * P], by_chunk(a["L0_ffn_W_up"].T), by_chunk(a["L0_ffn_W_gate"].T), by_chunk(qkvg)] + factors, axis=1)
    early, table = tables()
    arrays = {
        "x": a["L0_attn_x"].reshape(B, NT, P, D).transpose(2, 0, 1, 3),
        "vectors": vec, "rows": row, "early": early, "tables": table, "weights": weights,
    }
    arrays = {k: np.ascontiguousarray(x) for k, x in arrays.items()}
    assert arrays["weights"].shape[1] == N_WEIGHTS and vec.shape[1] == N_VECTORS
    nc = bacc.Bacc("TRN2", target_bir_lowering=False, num_devices=1)
    args = [nc.dram_tensor(k, x.shape, mybir.dt.float32, kind="ExternalInput").ap() for k, x in arrays.items()]
    out = nc.dram_tensor("out", (P, B, NT, D), mybir.dt.float32, kind="ExternalOutput").ap()
    build(nc, *args, out)
    got = run(nc, [arrays], core_ids=[0]).results[0]["out"]
    return np.ascontiguousarray(got.transpose(1, 2, 0, 3).reshape(B, S, D))
```
